# Optimizing a Trainium2 kernel written in Bass

```python
import numpy as np
import jax
import jax.numpy as jnp

def _softmax(x, axis=-1):
    return jax.nn.softmax(x, axis=axis)

def _gelu(x):
    return jax.nn.gelu(x, approximate=True)

def _silu(x):
    return jax.nn.silu(x)

def _sigmoid(x):
    return jax.nn.sigmoid(x)

def _layernorm(x, axis=-1, eps=1e-05):
    m = jnp.mean(x, axis=axis, keepdims=True)
    v = jnp.var(x, axis=axis, keepdims=True)
    return (x - m) / jnp.sqrt(v + eps)

def _scatter_add(tgt, idx, src, axis=0):
    return tgt.at[idx].add(src)

def _segment_sum(src, seg, n):
    return jax.ops.segment_sum(src, seg, n)
kernel_name = 'mk_cond_resid_d4_seqx_r8_086851'

def setup_inputs(seed: int=0):
    np.random.seed(seed)
    _w = jnp.asarray

    def _rec_inputs():
        import jax
        import jax.numpy as jnp
        _rk = jax.random.key(seed)
        x = -0.0005207 + 1.001 * jax.random.normal(jax.random.fold_in(_rk, 1), (64, 32, 512), jnp.float32)
        _lenS = 32 - jax.random.randint(jax.random.fold_in(_rk, 7), (64,), 0, max(1, 32 // 4) + 1, jnp.int32)
        _lenS2 = 32 - jax.random.randint(jax.random.fold_in(_rk, 8), (64,), 0, max(1, 32 // 4) + 1, jnp.int32)
        itok_Bx16_0_63 = jax.random.randint(jax.random.fold_in(_rk, 11), (64, 16), 0, 64, jnp.int32)
        itok_B_207_1644 = jax.random.randint(jax.random.fold_in(_rk, 12), (64,), 207, 1645, jnp.int32)
        itok_B_0_7 = jax.random.randint(jax.random.fold_in(_rk, 13), (64,), 0, 8, jnp.int32)
        itok_B_0_23 = jax.random.randint(jax.random.fold_in(_rk, 14), (64,), 0, 24, jnp.int32)
        itok_B_4_50 = jax.random.randint(jax.random.fold_in(_rk, 15), (64,), 4, 51, jnp.int32)
        return (x, itok_Bx16_0_63, itok_B_207_1644, itok_B_0_7, itok_B_0_23, itok_B_4_50)
    x, itok_Bx16_0_63, itok_B_207_1644, itok_B_0_7, itok_B_0_23, itok_B_4_50 = _rec_inputs()

    def _L0_cond_setup():
        import jax, jax.numpy as jnp
        import numpy as np
        B, S, HID = (4, 128, 512)
        D, HQ, HK = (128, 32, 8)
        PAGES, PSIZE, NPP = (64, 32, 16)
        THETA = 10000.0
        EPS = 1e-06
        SCALE = 1.0 / float(np.sqrt(D))

        def _rmsnorm(t, w):
            var = jnp.mean(t * t, axis=-1, keepdims=True)
            return t * jax.lax.rsqrt(var + EPS) * w

        def _rope(t, pos):
            inv_freq = 1.0 / THETA ** (jnp.arange(0, D, 2, dtype=jnp.float32) / D)
            freqs = pos[..., None].astype(jnp.float32) * inv_freq
            cos = jnp.cos(freqs)[:, :, None, :]
            sin = jnp.sin(freqs)[:, :, None, :]
            t1, t2 = (t[..., :D // 2], t[..., D // 2:])
            return jnp.concatenate([t1 * cos - t2 * sin, t2 * cos + t1 * sin], axis=-1)
        key = jax.random.key(seed)
        ks = jax.random.split(key, 10)
        x = jax.random.normal(ks[0], (B, S, HID), jnp.float32)
        Wq = jax.random.normal(ks[1], (HQ * D, HID), jnp.float32) * 0.02
        Wk = jax.random.normal(ks[2], (HK * D, HID), jnp.float32) * 0.02
        Wv = jax.random.normal(ks[3], (HK * D, HID), jnp.float32) * 0.02
        Wo = jax.random.normal(ks[4], (HID, HQ * D), jnp.float32) * 0.02
        q_norm_w = jax.random.uniform(ks[5], (D,), jnp.float32)
        k_norm_w = jax.random.uniform(ks[6], (D,), jnp.float32)
        k_cache = jax.random.normal(ks[7], (PAGES, PSIZE, HK, D), jnp.float32)
        v_cache = jax.random.normal(ks[8], (PAGES, PSIZE, HK, D), jnp.float32)
        block_table = jnp.arange(B * NPP, dtype=jnp.int32).reshape(B, NPP)
        cache_seqlens = jax.random.randint(ks[9], (B,), 0, 475).astype(jnp.int32)
        return dict(x=x, Wq=Wq, Wk=Wk, Wv=Wv, Wo=Wo, q_norm_w=q_norm_w, k_norm_w=k_norm_w, k_cache=k_cache, v_cache=v_cache, block_table=block_table, cache_seqlens=cache_seqlens)
    _L0_cond_all = _L0_cond_setup()
    _L0_cond_in = {k: v for k, v in _L0_cond_all.items() if k in ('Wq', 'Wk', 'Wv', 'Wo', 'q_norm_w', 'k_norm_w', 'k_cache', 'v_cache')}
    del _L0_cond_all

    def _L1_cond_setup():
        import jax, jax.numpy as jnp
        import numpy as np
        TOP_K = 2
        LANG_BIAS = 5.0
        SCALING = 32.0 / 16.0
        LANGUAGE_PAD_ID = -1
        key = jax.random.key(seed)
        ks = jax.random.split(key, 6)
        B, T, D, O, E, R = (4, 256, 512, 512, 8, 16)
        x = jax.random.normal(ks[0], (B, T, D), dtype=jnp.float32)
        language_ids = jax.random.randint(ks[1], (B,), 0, E).astype(jnp.int64)
        W = jax.random.normal(ks[2], (O, D), dtype=jnp.float32) * (1.0 / np.sqrt(D))
        Wr = jax.random.normal(ks[3], (E, D), dtype=jnp.float32) * (1.0 / np.sqrt(D))
        A = jax.random.normal(ks[4], (E, R, D), dtype=jnp.float32) * (1.0 / np.sqrt(D))
        Bm = jax.random.normal(ks[5], (O, R), dtype=jnp.float32) * 0.0
        Bm = jnp.broadcast_to(Bm, (E, O, R)) + jax.random.normal(ks[5], (E, O, R), dtype=jnp.float32) * 0.02
        return {'x': x, 'language_ids': language_ids, 'W': W, 'Wr': Wr, 'A': A, 'B': Bm}
    _L1_cond_all = _L1_cond_setup()
    _L1_cond_in = {k: v for k, v in _L1_cond_all.items() if k in ('W', 'Wr', 'A', 'B')}
    del _L1_cond_all

    def _L2_cond_setup():
        import jax, jax.numpy as jnp
        import numpy as np
        R = 16
        ALPHA = 32
        SCALING = ALPHA / R
        SLOTS = 32
        IN_F = 512
        OUT_F = 512
        B, T = (8, 128)
        key = jax.random.key(seed)
        k1, k2, k3, k4, k5, k6 = jax.random.split(key, 6)
        x = jax.random.normal(k1, (B, T, IN_F), dtype=jnp.float32)
        adapter_mapping = jax.random.randint(k2, (B,), 0, SLOTS, dtype=jnp.int32)
        W = jax.random.normal(k3, (OUT_F, IN_F), dtype=jnp.float32) * 0.02
        b = jax.random.normal(k4, (OUT_F,), dtype=jnp.float32) * 0.02
        lora_As = jax.random.normal(k5, (SLOTS, IN_F, R), dtype=jnp.float32) * 0.02
        lora_Bs = jax.random.normal(k6, (SLOTS, R, OUT_F), dtype=jnp.float32) * 0.02
        return {'x': x, 'adapter_mapping': adapter_mapping, 'W': W, 'b': b, 'lora_As': lora_As, 'lora_Bs': lora_Bs}
    _L2_cond_all = _L2_cond_setup()
    _L2_cond_in = {k: v for k, v in _L2_cond_all.items() if k in ('W', 'b', 'lora_As', 'lora_Bs')}
    del _L2_cond_all

    def _L3_cond_setup():
        import jax, jax.numpy as jnp
        import numpy as np
        RANK = 16
        ALPHA = 16.0
        SCALING = ALPHA / RANK
        key = jax.random.key(seed)
        k1, k2, k3, k4 = jax.random.split(key, 4)
        batch, n_tok, d_in, d_out, n_adapters, rank = (8, 256, 512, 512, 64, RANK)
        x = jax.random.normal(k1, (batch, n_tok, d_in), dtype=jnp.float32)
        A = jax.random.normal(k2, (n_adapters, d_out, rank), dtype=jnp.float32) * 0.02
        B = jax.random.normal(k3, (n_adapters, rank, d_in), dtype=jnp.float32)
        adapter_ids = jax.random.randint(k4, (batch,), 0, n_adapters, dtype=jnp.int32)
        return {'x': x, 'A': A, 'B': B, 'adapter_ids': adapter_ids}
    _L3_cond_all = _L3_cond_setup()
    _L3_cond_in = {k: v for k, v in _L3_cond_all.items() if k in ('A', 'B')}
    del _L3_cond_all
    return {'x': x, 'itok_Bx16_0_63': itok_Bx16_0_63, 'itok_B_207_1644': itok_B_207_1644, 'itok_B_0_7': itok_B_0_7, 'itok_B_0_23': itok_B_0_23, 'itok_B_4_50': itok_B_4_50, 'L0_cond_Wq': _L0_cond_in['Wq'], 'L0_cond_Wk': _L0_cond_in['Wk'], 'L0_cond_Wv': _L0_cond_in['Wv'], 'L0_cond_Wo': _L0_cond_in['Wo'], 'L0_cond_q_norm_w': _L0_cond_in['q_norm_w'], 'L0_cond_k_norm_w': _L0_cond_in['k_norm_w'], 'L0_cond_k_cache': _L0_cond_in['k_cache'], 'L0_cond_v_cache': _L0_cond_in['v_cache'], 'L1_cond_W': _L1_cond_in['W'], 'L1_cond_Wr': _L1_cond_in['Wr'], 'L1_cond_A': _L1_cond_in['A'], 'L1_cond_B': _L1_cond_in['B'], 'L2_cond_W': _L2_cond_in['W'], 'L2_cond_b': _L2_cond_in['b'], 'L2_cond_lora_As': _L2_cond_in['lora_As'], 'L2_cond_lora_Bs': _L2_cond_in['lora_Bs'], 'L3_cond_A': _L3_cond_in['A'], 'L3_cond_B': _L3_cond_in['B']}

def reference(x, itok_Bx16_0_63, itok_B_207_1644, itok_B_0_7, itok_B_0_23, itok_B_4_50, L0_cond_Wq, L0_cond_Wk, L0_cond_Wv, L0_cond_Wo, L0_cond_q_norm_w, L0_cond_k_norm_w, L0_cond_k_cache, L0_cond_v_cache, L1_cond_W, L1_cond_Wr, L1_cond_A, L1_cond_B, L2_cond_W, L2_cond_b, L2_cond_lora_As, L2_cond_lora_Bs, L3_cond_A, L3_cond_B):
    import jax
    import jax.numpy as jnp

    def _L0_cond_ref(x, Wq, Wk, Wv, Wo, q_norm_w, k_norm_w, k_cache, v_cache, block_table, cache_seqlens):
        import jax, jax.numpy as jnp
        import numpy as np
        B, S, HID = (4, 128, 512)
        D, HQ, HK = (128, 32, 8)
        PAGES, PSIZE, NPP = (64, 32, 16)
        THETA = 10000.0
        EPS = 1e-06
        SCALE = 1.0 / float(np.sqrt(D))

        def _rmsnorm(t, w):
            var = jnp.mean(t * t, axis=-1, keepdims=True)
            return t * jax.lax.rsqrt(var + EPS) * w

        def _rope(t, pos):
            inv_freq = 1.0 / THETA ** (jnp.arange(0, D, 2, dtype=jnp.float32) / D)
            freqs = pos[..., None].astype(jnp.float32) * inv_freq
            cos = jnp.cos(freqs)[:, :, None, :]
            sin = jnp.sin(freqs)[:, :, None, :]
            t1, t2 = (t[..., :D // 2], t[..., D // 2:])
            return jnp.concatenate([t1 * cos - t2 * sin, t2 * cos + t1 * sin], axis=-1)
        bsz, seqlen, _ = x.shape
        q = jnp.einsum('bsd,ed->bse', x, Wq).reshape(bsz, seqlen, HQ, D)
        k = jnp.einsum('bsd,ed->bse', x, Wk).reshape(bsz, seqlen, HK, D)
        v = jnp.einsum('bsd,ed->bse', x, Wv).reshape(bsz, seqlen, HK, D)
        q = _rmsnorm(q, q_norm_w)
        k = _rmsnorm(k, k_norm_w)
        pos = cache_seqlens[:, None] + jnp.arange(seqlen)[None, :]
        q = _rope(q, pos)
        k = _rope(k, pos)
        L = NPP * PSIZE
        kc = k_cache[block_table].reshape(bsz, L, HK, D)
        vc = v_cache[block_table].reshape(bsz, L, HK, D)
        k_all = jnp.concatenate([kc, k], axis=1)
        v_all = jnp.concatenate([vc, v], axis=1)
        valid_c = jnp.arange(L)[None, :] < cache_seqlens[:, None]
        valid = jnp.concatenate([valid_c, jnp.ones((bsz, seqlen), dtype=bool)], axis=1)
        rep = HQ // HK
        k_all = jnp.repeat(k_all, rep, axis=2)
        v_all = jnp.repeat(v_all, rep, axis=2)
        scores = jnp.einsum('bqhd,bkhd->bhqk', q, k_all) * SCALE
        scores = jnp.where(valid[:, None, None, :], scores, -1e+30)
        probs = jax.nn.softmax(scores, axis=-1)
        o = jnp.einsum('bhqk,bkhd->bqhd', probs, v_all)
        o = o.reshape(bsz, seqlen, HQ * D)
        return jnp.einsum('bse,de->bsd', o, Wo)

    def _L1_cond_ref(x, language_ids, W, Wr, A, B):
        import jax, jax.numpy as jnp
        import numpy as np
        TOP_K = 2
        LANG_BIAS = 5.0
        SCALING = 32.0 / 16.0
        LANGUAGE_PAD_ID = -1
        base = jnp.einsum('btd,od->bto', x, W)
        E = Wr.shape[0]
        logits = jnp.einsum('btd,ed->bte', x.astype(jnp.float32), Wr.astype(jnp.float32))
        expert_targets = language_ids
        valid = expert_targets >= 0
        tgt = jnp.where(valid, expert_targets, 0)
        bias = jax.nn.one_hot(tgt, E, dtype=logits.dtype) * LANG_BIAS
        bias = jnp.where(valid[:, None], bias, 0.0)
        logits = logits + bias[:, None, :]
        topw, topi = jax.lax.top_k(logits, TOP_K)
        weights = jax.nn.softmax(topw, axis=-1)
        gates = jnp.sum(jax.nn.one_hot(topi, E, dtype=weights.dtype) * weights[..., None], axis=-2)
        gates = gates.astype(x.dtype)
        h = jnp.einsum('btd,erd->bter', x, A)
        lora_out = jnp.einsum('bter,bte,eor->bto', h, gates, B)
        return base + SCALING * lora_out

    def _L2_cond_ref(x, adapter_mapping, W, b, lora_As, lora_Bs):
        import jax, jax.numpy as jnp
        import numpy as np
        R = 16
        ALPHA = 32
        SCALING = ALPHA / R
        SLOTS = 32
        IN_F = 512
        OUT_F = 512
        B, T = (8, 128)
        base_out = jnp.einsum('bti,oi->bto', x, W) + b
        A = lora_As[adapter_mapping]
        Bm = lora_Bs[adapter_mapping]
        lora_h = jnp.einsum('bti,bir->btr', x, A)
        lora_out = jnp.einsum('btr,bro->bto', lora_h, Bm)
        return base_out + lora_out * SCALING

    def _L3_cond_ref(x, A, B, adapter_ids):
        import jax, jax.numpy as jnp
        import numpy as np
        RANK = 16
        ALPHA = 16.0
        SCALING = ALPHA / RANK
        B_req = B[adapter_ids]
        A_req = A[adapter_ids]
        Bx = jnp.einsum('bni,bri->bnr', x, B_req)
        out = jnp.einsum('bnr,bor->bno', Bx, A_req)
        return out * SCALING
    x = x + _L0_cond_ref(x, L0_cond_Wq, L0_cond_Wk, L0_cond_Wv, L0_cond_Wo, L0_cond_q_norm_w, L0_cond_k_norm_w, L0_cond_k_cache, L0_cond_v_cache, itok_Bx16_0_63, itok_B_207_1644)
    x = x + _L1_cond_ref(x, itok_B_0_7, L1_cond_W, L1_cond_Wr, L1_cond_A, L1_cond_B)
    x = x + _L2_cond_ref(x, itok_B_0_23, L2_cond_W, L2_cond_b, L2_cond_lora_As, L2_cond_lora_Bs)
    x = x + _L3_cond_ref(x, L3_cond_A, L3_cond_B, itok_B_4_50)
    return x

_drawn_inputs = setup_inputs


def setup_inputs(seed=0):
    import zlib

    import numpy as np

    out = dict(_drawn_inputs(seed))
    spreads = {}
    factors = {'L0_cond_Wk': 8.0,
     'L0_cond_Wv': 8.0,
     'L0_cond_k_norm_w': 8.0,
     'L1_cond_Wr': 6.335,
     'L2_cond_b': 5.453,
     'L0_cond_k_cache': 4.134,
     'L0_cond_v_cache': 3.028}
    for name, (base, spread) in spreads.items():
        noise = np.random.default_rng([zlib.crc32(name.encode()), seed]).standard_normal(out[name].shape)
        drawn = base * np.exp(spread * noise) if base else spread * noise
        out[name] = jnp.asarray(drawn.astype(out[name].dtype))
    for name, factor in factors.items():
        out[name] = (out[name] * factor).astype(out[name].dtype)
    return out
```

```python
from contextlib import ExitStack

import concourse.bass as bass
from concourse import mybir
from concourse.alu_op_type import AluOpType as ALU

ACT = mybir.ActivationFunctionType
AX = mybir.AxisListType
F32 = mybir.dt.float32
F32R = mybir.dt.float32r
I32 = mybir.dt.int32
U32 = mybir.dt.uint32

P = 128
B, S, D = 64, 32, 512
DC = D // P
TOK = B * S
TB = P // S
NT = TOK // P
HQ, HK, HD = 32, 8, 128
REP = HQ // HK
NPP, PSIZE, PAGES = 16, 32, 64
L = NPP * PSIZE
KEYS = L + S
KC = L // P
ROWS = REP * S
SLICE = 512
NQ, NK, NV = HQ * HD // SLICE, HK * HD // SLICE, HK * HD // SLICE
NSL = NQ + NK + NV
HS = SLICE // HD
HALF = HD // 2
SCALE = float(HD) ** -0.5
RMS_EPS = 1e-6
NEG = -1e30
OWN_KEY = -3.0e9
E, R1 = 8, 16
LANG_BIAS = 5.0
MOE_SCALING = 2.0
R2, LORA_SCALING = 16, 2.0
R3 = 16
TWO_PI_HI, TWO_PI_MID, TWO_PI_LO = 6.28125, 0.0019350051879882812, 3.0199157663446332e-07
ROUND = 12582912.0
PI_IN = 3.1415925


def at_least(engine, sem, value):
    if not (isinstance(value, int) and value <= 0):
        engine.wait_ge(sem, value)


def decoder(nc, x_t, x_rows, w_qkv, wo_t, q_norm_w, k_norm_w, inv_freq, k_pages, v_rows, block_table, seqlens,
            lang, slot2, slot3, w1_t, wr_a_t, b1_rows, w2_t, bias2, a2_rows, b2_rows, b3_rows, a3_rows, out):
    with ExitStack() as whole:
        def sem(name):
            return whole.enter_context(nc.semaphore(name))

        ident = whole.enter_context(nc.sbuf_tensor("ident", [P, P], F32))
        q_dram = nc.dram_tensor("q_spill", (B, HD, HQ * S), F32, kind="Internal").ap()
        k_dram = nc.dram_tensor("k_spill", (B, HD, HK * S), F32, kind="Internal").ap()
        v_dram = nc.dram_tensor("v_spill", (TOK, HK * HD), F32, kind="Internal").ap()
        o_dram = nc.dram_tensor("o_spill", (B, HD, HQ * S), F32, kind="Internal").ap()

        with ExitStack() as ctx:
            def sb(name, shape, dt=F32):
                return ctx.enter_context(nc.sbuf_tensor(name, shape, dt))

            seq_f = sb("seq_f", [P, B])
            pages = sb("pages", [P, B * NPP], I32)
            page_row = sb("page_row", [P, B * KC], I32)
            in_page_i = sb("in_page_i", [P, 1], I32)
            key_index = sb("key_index", [P, KEYS])
            tables = (seq_f, pages, page_row, in_page_i, key_index)

            project(nc, sem, ident, *tables, x_t, w_qkv, q_norm_w, k_norm_w, inv_freq, block_table, seqlens,
                    q_dram, k_dram, v_dram)
            attend(nc, sem, ident, *tables, k_pages, v_rows, q_dram, k_dram, v_dram, o_dram)
        finish(nc, sem, ident, o_dram, x_rows, wo_t, lang, slot2, slot3, w1_t, wr_a_t, b1_rows, w2_t, bias2,
               a2_rows, b2_rows, b3_rows, a3_rows, out)


def project(nc, sem, ident, seq_f, pages, page_row, in_page_i, key_index, x_t, w_qkv, q_norm_w, k_norm_w, inv_freq,
            block_table, seqlens, q_dram, k_dram, v_dram):
    MM_BANKS = 4
    QUARTER = 4
    PAIRS = NSL // 2
    PS = 2 * NT

    with ExitStack() as ctx:
        def sb(name, shape, dt=F32):
            return ctx.enter_context(nc.sbuf_tensor(name, shape, dt))

        x_raw = sb("x_raw", [P, 2, DC, QUARTER * P])
        x_hi = sb("x_hi", [P, DC, TOK], F32R)
        x_lo = sb("x_lo", [P, DC, TOK], F32R)
        w_raw = sb("w_raw", [P, 2, DC, SLICE])
        w_hi = sb("w_hi", [P, 2, DC, SLICE], F32R)
        w_lo = sb("w_lo", [P, 2, DC, SLICE], F32R)
        seq_i = sb("seq_i", [P, B], I32)
        in_page = sb("in_page", [P, 1])
        pos = sb("pos", [P, NT])
        freq = sb("freq", [P, HALF])
        norm_q = sb("norm_q", [P, HD])
        norm_k = sb("norm_k", [P, HD])
        eps = sb("eps", [P, 1])
        sin = sb("sin", [P, NT, HALF])
        straight = {"q": sb("straight_q", [P, NT, HD]), "k": sb("straight_k", [P, NT, HD])}
        crossed = {"q": sb("crossed_q", [P, NT, HD]), "k": sb("crossed_k", [P, NT, HD])}
        squares = sb("squares", [P, 2, HS, HD])
        sumsq = sb("sumsq", [P, 2, HS])
        rms = sb("rms", [P, 2, HS])
        rstd = sb("rstd", [P, 2, HS])
        normed = sb("normed", [P, 2, HS, HD])
        part_s = sb("part_s", [P, HS, HD])
        part_c = sb("part_c", [P, 2, HS, HD])
        roped = sb("roped", [P, 2, HS, HD])
        stage = sb("stage", [P, 2, QUARTER * SLICE])
        TRIG = NT * HALF

        def trig_view(ap):
            return ap.rearrange("p (t f) -> p t f", f=HALF)

        angle = trig_view(stage[:, 0, 0:TRIG])
        turns = trig_view(stage[:, 0, TRIG:2 * TRIG])
        reduced = trig_view(stage[:, 1, 0:TRIG])
        key_i = stage[:, 1, TRIG:TRIG + L].bitcast(I32)
        cos = trig_view(roped[:, :, :, :].rearrange("p a h d -> p (a h d)"))
        nsin = trig_view(part_c[:, :, :, :].rearrange("p a h d -> p (a h d)"))
        acc = [ctx.enter_context(nc.psum_tensor(f"acc{i}", [P, SLICE], F32)) for i in range(MM_BANKS)]
        flip = [ctx.enter_context(nc.psum_tensor(f"flip{i}", [P, SLICE], F32)) for i in range(2)]

        consts_in = sem("consts_in")
        x_in = [sem("x_in0"), sem("x_in1")]
        w_in = [sem("w_in0"), sem("w_in1")]
        iota_done = sem("iota_done")
        ident_done = sem("ident_done")
        table_step = sem("table_step")
        angles_done = sem("angles_done")
        trig_done = sem("trig_done")
        tables_q = sem("tables_q")
        tables_k = sem("tables_k")
        x_hi_done = sem("x_hi_done")
        x_split = sem("x_split")
        w_hi_done = sem("w_hi_done")
        w_split = sem("w_split")
        mm_done = sem("mm_done")
        squared = sem("squared")
        summed = sem("summed")
        rooted = sem("rooted")
        rstd_done = sem("rstd_done")
        drained = sem("drained")
        straight_done = sem("straight_done")
        crossed_done = sem("crossed_done")
        roped_done = sem("roped_done")
        flipped = sem("flipped")
        staged_qk = sem("staged_qk")
        staged_v = sem("staged_v")
        stored = [sem("stored0"), sem("stored1")]

        KIND = ["q"] * (NQ // 2) + ["k"] * (NK // 2) + ["v"] * (NV // 2)
        QKS = (NQ + NK) * NT

        def over_pairs(engine, emit):
            emit(0, "q", None)
            with engine.Fori(1, NQ // 2) as p:
                emit(p, "q", "q")
            for p in range(NQ // 2, PAIRS):
                emit(p, KIND[p], KIND[p - 1])

        with nc.Block() as block:

            @block.sync
            def _(sp):
                sp.dma_start(w_raw[:, 0], w_qkv[0]).then_inc(w_in[0], 16)
                sp.dma_start(x_raw[:, 0], x_t[0]).then_inc(x_in[0], 16)
                sp.dma_start(seq_i[:, :], seqlens.partition_broadcast(P)).then_inc(consts_in, 16)
                sp.dma_start(freq[:, :], inv_freq.partition_broadcast(P)).then_inc(consts_in, 16)
                sp.dma_start(norm_q[:, :], q_norm_w.partition_broadcast(P)).then_inc(consts_in, 16)
                sp.dma_start(norm_k[:, :], k_norm_w.partition_broadcast(P)).then_inc(consts_in, 16)
                sp.dma_start(pages[:, :], block_table.partition_broadcast(P)).then_inc(consts_in, 16)
                sp.dma_start(x_raw[:, 1], x_t[1]).then_inc(x_in[1], 16)
                sp.dma_start(w_raw[:, 1], w_qkv[1]).then_inc(w_in[1], 16)
                for q in range(2, NT // QUARTER):
                    sp.wait_ge(x_split, q - 1)
                    sp.dma_start(x_raw[:, q % 2], x_t[q]).then_inc(x_in[q % 2], 16)

                def emit(p, kind, before):
                    for par in range(2):
                        s = p * 2 + par
                        if kind != "v":
                            sp.wait_ge(w_split, DC * s + DC)
                            sp.dma_start(w_raw[:, par], w_qkv[bass.ds(s + 2, 1)].rearrange("a p c n -> (a p) c n")
                                         if not isinstance(s, int) else w_qkv[s + 2]).then_inc(w_in[par], 16)
                        for g in range(NT // QUARTER):
                            buf = stage[:, g % 2]
                            if kind == "v":
                                sp.wait_ge(staged_v, NT * s - QKS + QUARTER * (g + 1))
                                n = s - NQ - NK
                                dst = v_dram[g * QUARTER * P:(g + 1) * QUARTER * P, n * SLICE:(n + 1) * SLICE]
                                sp.dma_start(dst.rearrange("(t p) n -> p t n", p=P),
                                             buf.rearrange("p (t n) -> p t n", n=SLICE)).then_inc(stored[g % 2], 16)
                            else:
                                sp.wait_ge(staged_qk, NT * s + QUARTER * (g + 1))
                                to, n = (q_dram, s) if kind == "q" else (k_dram, s - NQ)
                                b0 = g * QUARTER * TB
                                dst = to[b0:b0 + QUARTER * TB, :, bass.ds(n * HS * S, HS * S)]
                                sp.dma_start(dst.rearrange("b d n -> d b n"),
                                             buf.rearrange("p (b n) -> p b n", n=HS * S)).then_inc(stored[g % 2], 16)

                over_pairs(sp, emit)
                for i in range(2):
                    sp.wait_ge(stored[i], 16 * NSL * (NT // QUARTER) // 2)

            @block.gpsimd
            def _(pool):
                nc.gpsimd.memset(ident[:, :], 0.0).then_inc(ident_done, 1)
                pool.wait_ge(ident_done, 1)
                nc.gpsimd.affine_select(out=ident[:, :], in_=ident[:, :], compare_op=ALU.not_equal, fill=1.0,
                                        base=0, pattern=[[-1, P]], channel_multiplier=1).then_inc(ident_done, 1)
                pool.wait_ge(ident_done, 2)
                for i in range(TB):
                    nc.gpsimd.iota(in_page_i[PSIZE * i:PSIZE * (i + 1), :], [[0, 1]], base=0, channel_multiplier=1)\
                        .then_inc(iota_done, 1)
                pool.wait_ge(iota_done, TB)
                nc.gpsimd.iota(key_i[:, :], [[1, L]], base=0, channel_multiplier=0).then_inc(iota_done, 1)

                def split(s, par, c):
                    nc.gpsimd.tensor_copy(w_hi[:, par, c], w_raw[:, par, c]).then_inc(w_hi_done, 1)
                    pool.wait_ge(w_hi_done, DC * s + c + 1)
                    nc.gpsimd.tensor_sub(w_lo[:, par, c], w_raw[:, par, c], w_hi[:, par, c].bitcast(F32))\
                        .then_inc(w_split, 1)

                pool.wait_ge(w_in[0], 16)
                for c in range(DC):
                    split(0, 0, c)
                pool.wait_ge(trig_done, 3)
                pool.wait_ge(consts_in, 16 * 5)

                def table(to, trig, w):
                    nc.gpsimd.tensor_mul(to, trig[:, :, :], w.unsqueeze(1).broadcast_to([P, NT, HALF]))\
                        .then_inc(tables_k, 1)

                table(straight["k"][:, :, 0:HALF], cos, norm_k[:, 0:HALF])
                table(straight["k"][:, :, HALF:HD], cos, norm_k[:, HALF:HD])
                table(crossed["k"][:, :, 0:HALF], nsin, norm_k[:, HALF:HD])
                table(crossed["k"][:, :, HALF:HD], sin, norm_k[:, 0:HALF])
                pool.wait_ge(tables_k, 4)
                pool.wait_ge(tables_q, 4)

                def emit(p, kind, before):
                    for j in range(PS):
                        n = p * PS + j
                        par, t = j // NT, j % NT
                        s = p * 2 + par + 1
                        splits = t in (3, 6, 9, 12) and not (kind == "v" and par == 1)
                        if splits and t == 3:
                            pool.wait_ge(w_in[1 - par], 16 * p + 16 if par == 0 else 16 * p + 32)
                            at_least(pool, mm_done, NT * (s - 1))
                        lag = kind if j >= 2 else before
                        if lag in ("q", "k"):
                            m, i = n - 2, j % 2
                            pool.wait_ge(drained, m + 1)
                            at_least(pool, roped_done, m - 1)
                            cr = crossed[lag]
                            for lo, hi in ((0, HALF), (HALF, 0)):
                                last = nc.gpsimd.tensor_mul(
                                    part_c[:, i, :, lo:lo + HALF], normed[:, i, :, hi:hi + HALF],
                                    cr[:, (j - 2) % NT, lo:lo + HALF].unsqueeze(1).broadcast_to([P, HS, HALF]))
                            last.then_inc(crossed_done, 1)
                        if splits:
                            split(s, 1 - par, t // 3 - 1)

                over_pairs(pool, emit)

            @block.scalar
            def _(act):
                for q in range(NT // QUARTER):
                    act.wait_ge(x_in[q % 2], 16 * (q // 2 + 1))
                    cols = slice(q * QUARTER * P, (q + 1) * QUARTER * P)
                    nc.scalar.activation(x_hi[:, :, cols], x_raw[:, q % 2], ACT.Copy).then_inc(x_hi_done, 1)
                    if q == 0:
                        act.wait_ge(angles_done, 1)
                        nc.scalar.activation(sin[:, :, :], reduced[:, :, :], ACT.Sin).then_inc(trig_done, 1)
                        nc.scalar.activation(nsin[:, :, :], reduced[:, :, :], ACT.Sin, scale=-1.0).then_inc(trig_done, 1)
                        act.wait_ge(angles_done, 2)
                        nc.scalar.activation(cos[:, :, :], angle[:, :, :], ACT.Sin).then_inc(trig_done, 1)

                def emit(p, kind, before):
                    for j in range(PS):
                        n = p * PS + j
                        lag, i = (kind if j >= 1 else before), (j - 1) % 2
                        if lag in ("q", "k"):
                            act.wait_ge(summed, n)
                            nc.scalar.activation(rms[:, i], sumsq[:, i], ACT.Sqrt, bias=eps[:, 0:1], scale=1.0 / HD)\
                                .then_inc(rooted, 1)
                        if kind != "v":
                            act.wait_ge(mm_done, n + 1)
                            nc.scalar.activation(squares[:, j % 2], acc[j % MM_BANKS][:, :].rearrange(
                                "p (h d) -> p h d", d=HD), ACT.Square).then_inc(squared, 1)
                        if lag in ("q", "k"):
                            act.wait_ge(rstd_done, n)
                            at_least(act, roped_done, n - 2)
                            for h in range(HS):
                                last = nc.scalar.activation(normed[:, i, h],
                                                            acc[(j - 1) % MM_BANKS][:, h * HD:(h + 1) * HD],
                                                            ACT.Copy, scale=rstd[:, i, h:h + 1])
                            last.then_inc(drained, 1)
                        if kind == "v":
                            act.wait_ge(mm_done, n + 1)
                            t = j % NT
                            if t % QUARTER == 0:
                                g = t // QUARTER
                                s = p * 2 + j // NT
                                act.wait_ge(stored[g % 2], 16 * (s * 2 + g // 2))
                            nc.scalar.activation(stage[:, (t // QUARTER) % 2, (t % QUARTER) * SLICE:(t % QUARTER + 1) * SLICE],
                                                 acc[j % MM_BANKS][:, :], ACT.Copy).then_inc(staged_v, 1)

                over_pairs(act, emit)

            @block.vector
            def _(dve):
                steps = [0]

                def link(ins):
                    steps[0] += 1
                    ins.then_inc(table_step, 1)
                    dve.wait_ge(table_step, steps[0])

                nc.vector.memset(eps[:, :], RMS_EPS)
                dve.wait_ge(iota_done, TB + 1)
                dve.wait_ge(consts_in, 16 * 5)
                link(nc.vector.tensor_copy(in_page[:, :], in_page_i[:, :]))
                link(nc.vector.tensor_copy(seq_f[:, :], seq_i[:, :]))
                for i in range(TB):
                    q = slice(PSIZE * i, PSIZE * (i + 1))
                    nc.vector.tensor_scalar(pos[q, :], seq_f[q, i::TB], in_page[q, 0:1], None, ALU.add)
                nc.vector.tensor_copy(key_index[:, 0:L], key_i[:, :])
                link(nc.vector.memset(key_index[:, L:KEYS], OWN_KEY))
                link(nc.vector.tensor_tensor(angle[:, :, :], pos[:, :].unsqueeze(2).broadcast_to([P, NT, HALF]),
                                             freq[:, :].unsqueeze(1).broadcast_to([P, NT, HALF]), ALU.mult))

                def reduce(to, quarter, last):
                    link(nc.vector.tensor_scalar(turns[:, :, :], angle[:, :, :], 1.0 / 6.283185307179586, quarter,
                                                 ALU.mult, ALU.add))
                    link(nc.vector.tensor_scalar(turns[:, :, :], turns[:, :, :], ROUND, ROUND, ALU.add, ALU.subtract))
                    src = angle
                    for part in (TWO_PI_HI, TWO_PI_MID, TWO_PI_LO):
                        link(nc.vector.scalar_tensor_tensor(out=to[:, :, :], in0=turns[:, :, :], scalar=-part,
                                                            in1=src[:, :, :], op0=ALU.mult, op1=ALU.add))
                        src = to
                    if quarter:
                        link(nc.vector.tensor_scalar(to[:, :, :], to[:, :, :], 1.5707963267948966, None, ALU.add))
                    nc.vector.tensor_scalar(to[:, :, :], to[:, :, :], PI_IN, -PI_IN, ALU.min, ALU.max)\
                        .then_inc(angles_done, 1)

                reduce(reduced, 0.0, False)
                reduce(angle, 0.25, True)
                for i in range(TB):
                    q = slice(PSIZE * i, PSIZE * (i + 1))
                    nc.vector.tensor_scalar(page_row[q, :].rearrange("p (b c) -> p b c", c=KC),
                                            pages[q, :].rearrange("p (b c i) -> p b c i", c=KC, i=TB)[:, :, :, i],
                                            float(PSIZE), None, ALU.mult)

                def lower(q):
                    dve.wait_ge(x_hi_done, q + 1)
                    cols = slice(q * QUARTER * P, (q + 1) * QUARTER * P)
                    nc.vector.tensor_tensor(x_lo[:, :, cols], x_raw[:, q % 2], x_hi[:, :, cols].bitcast(F32),
                                            ALU.subtract).then_inc(x_split, 1)

                lower(0)
                dve.wait_ge(trig_done, 3)
                for to, trig, w in ((straight["q"][:, :, 0:HALF], cos, norm_q[:, 0:HALF]),
                                    (straight["q"][:, :, HALF:HD], cos, norm_q[:, HALF:HD]),
                                    (crossed["q"][:, :, 0:HALF], nsin, norm_q[:, HALF:HD]),
                                    (crossed["q"][:, :, HALF:HD], sin, norm_q[:, 0:HALF])):
                    nc.vector.tensor_tensor(to, trig[:, :, :], w.unsqueeze(1).broadcast_to([P, NT, HALF]), ALU.mult)\
                        .then_inc(tables_q, 1)
                for q in range(1, NT // QUARTER):
                    lower(q)
                dve.wait_ge(tables_q, 4)

                def emit(p, kind, before):
                    if kind == "k":
                        dve.wait_ge(tables_k, 4)
                    for j in range(PS):
                        n = p * PS + j
                        if (kind if j >= 1 else before) in ("q", "k"):
                            i = (j - 1) % 2
                            dve.wait_ge(rooted, n)
                            nc.vector.reciprocal(rstd[:, i], rms[:, i]).then_inc(rstd_done, 1)
                        if kind != "v":
                            dve.wait_ge(squared, n + 1)
                            nc.vector.tensor_reduce(sumsq[:, j % 2], squares[:, j % 2], AX.X, ALU.add).then_inc(summed, 1)
                        lag = kind if j >= 2 else before
                        if lag in ("q", "k"):
                            m, i, t = n - 2, j % 2, (j - 2) % NT
                            at_least(dve, roped_done, m)
                            dve.wait_ge(drained, m + 1)
                            nc.vector.tensor_tensor(part_s[:, :, :], normed[:, i],
                                                    straight[lag][:, t].unsqueeze(1).broadcast_to([P, HS, HD]),
                                                    ALU.mult).then_inc(straight_done, 1)
                            dve.wait_ge(straight_done, m + 1)
                            dve.wait_ge(crossed_done, m + 1)
                            at_least(dve, flipped, m - 1)
                            nc.vector.tensor_tensor(roped[:, i], part_s[:, :, :], part_c[:, i], ALU.add)\
                                .then_inc(roped_done, 1)
                        lag = kind if j >= 4 else before
                        if lag in ("q", "k"):
                            m, t = n - 4, (j - 4) % NT
                            dve.wait_ge(flipped, m + 1)
                            g, s2 = t // QUARTER, (p * 2 + (j - 4) // NT) * 2
                            if t % QUARTER == 0:
                                at_least(dve, stored[g % 2], 16 * (s2 + g // 2))
                            to = stage[:, g % 2, (t % QUARTER) * SLICE:(t % QUARTER + 1) * SLICE]
                            nc.vector.tensor_copy(to.rearrange("p (b h s) -> p b h s", h=HS, s=S),
                                                  flip[j % 2][:, :].rearrange("p (h b s) -> p b h s", h=HS, s=S))\
                                .then_inc(staged_qk, 1)

                over_pairs(dve, emit)

            @block.tensor
            def _(pe):
                pe.wait_ge(ident_done, 2)

                def emit(p, kind, before):
                    for j in range(PS):
                        n = p * PS + j
                        par, t = j // NT, j % NT
                        if t == 0:
                            pe.wait_ge(w_split, DC * (p * 2 + par) + DC)
                        if isinstance(p, int) and p == 0 and par == 0 and t % QUARTER == 0:
                            pe.wait_ge(x_split, t // QUARTER + 1)
                        if kind == "v":
                            if j < MM_BANKS:
                                pe.wait_ge(drained, n - MM_BANKS + 1)
                            else:
                                pe.wait_ge(staged_v, j - MM_BANKS + 1)
                        else:
                            at_least(pe, drained, n - MM_BANKS + 1)
                        bank = acc[j % MM_BANKS][:, :]
                        for c in range(DC):
                            toks = slice(t * P, (t + 1) * P)
                            pe.matmul(bank, x_hi[:, c, toks], w_hi[:, par, c], start=c == 0, stop=False)
                            pe.matmul(bank, x_hi[:, c, toks], w_lo[:, par, c], start=False, stop=False)
                            last = pe.matmul(bank, x_lo[:, c, toks], w_hi[:, par, c], start=False, stop=c == DC - 1)
                        last.then_inc(mm_done, 1)
                        lag = kind if j >= 3 else before
                        if lag in ("q", "k"):
                            m, i = n - 3, (j - 3) % 2
                            pe.wait_ge(roped_done, m + 1)
                            at_least(pe, staged_qk, m - 1)
                            for h in range(HS):
                                last = pe.transpose(flip[i][:, h * P:(h + 1) * P], roped[:, i, h], ident[:, :])
                            last.then_inc(flipped, 1)

                over_pairs(pe, emit)


def attend(nc, sem, ident, seq_f, pages, page_row, in_page_i, key_index, k_pages, v_rows, q_dram, k_dram, v_dram, o_dram):
    UNITS = 2 * HK
    PAIRS = B // 2
    SLOTS = NPP + 1
    CUT = 9 * PSIZE
    BANK = 512

    with ExitStack() as ctx:
        def sb(name, shape, dt=F32):
            return ctx.enter_context(nc.sbuf_tensor(name, shape, dt))

        def ps(name, shape):
            return ctx.enter_context(nc.psum_tensor(name, shape, F32))

        q_t = sb("q_t", [P, 2, HK, ROWS])
        k_t = sb("k_t", [P, 2, SLOTS, HK, PSIZE])
        v_c = sb("v_c", [P, 2, KC, HK * HD])
        v_own = sb("v_own", [S, 2, HK * HD])
        v_row = sb("v_row", [P, 2, KC], I32)
        past = sb("past", [P, KEYS])
        mask = sb("mask", [P, 2, KEYS])
        scores = sb("scores", [P, 2, KEYS])
        probs = sb("probs", [P, 2, KEYS])
        neg_max = sb("neg_max", [P, 2])
        row_sum = sb("row_sum", [P, 2])
        inv_sum = sb("inv_sum", [P, 2])
        p_t = sb("p_t", [P, 2, KC, ROWS])
        p_t_own = sb("p_t_own", [S, 2, ROWS])
        o_t = sb("o_t", [P, 2, HK, ROWS])
        s_banks = [ps(f"s_bank{i}", [P, 2 * BANK]) for i in range(2)]
        s_run = [x[:, BANK - CUT:BANK - CUT + KEYS] for x in s_banks]
        pt_a = ps("pt_a", [P, BANK])
        pt_b = ps("pt_b", [P, BANK])
        o_banks = [ps(f"o_bank{i}", [P, BANK]) for i in range(2)]

        qk_in = [sem("qk_in0"), sem("qk_in1")]
        v_in = [sem("v_in0"), sem("v_in1")]
        v_own_in = [sem("v_own_in0"), sem("v_own_in1")]
        v_named = sem("v_named")
        past_done = sem("past_done")
        scored = sem("scored")
        masked_in = sem("mask_built")
        masked = sem("masked")
        weighed = sem("weighed")
        inverted = sem("inverted")
        normed = sem("weights_normed")
        turned = sem("weights_turned")
        pt_a_out = sem("pt_a_out")
        pt_b_out = sem("pt_b_out")
        summed = sem("values_summed")
        o_out = sem("o_out")
        o_stored = [sem("o_stored0"), sem("o_stored1")]
        QK_DMAS = 2 + NPP

        def over_pairs(engine, emit, tail=None):
            emit(0, True)
            with engine.Fori(1, PAIRS) as p:
                emit(p, False)
            if tail:
                tail(PAIRS)

        with nc.Block() as block:

            @block.sync
            def _(sp):
                def store(p, par, b):
                    sp.wait_ge(o_out, b * HK + HK)
                    sp.dma_start(o_dram[bass.ds(b, 1)].rearrange("b d n -> (b d) n"),
                                 o_t[:, par].rearrange("p g n -> p (g n)")).then_inc(o_stored[par], 16)

                def emit(p, first):
                    for par in range(2):
                        b = p * 2 + par
                        at_least(sp, scored, (b - 1) * HK)
                        sp.dma_start(q_t[:, par].rearrange("p g n -> p (g n)"),
                                     q_dram[bass.ds(b, 1)].rearrange("b d n -> (b d) n")).then_inc(qk_in[par], 16)
                        sp.dma_start(k_t[:, par, NPP].rearrange("p g n -> p (g n)"),
                                     k_dram[bass.ds(b, 1)].rearrange("b d n -> (b d) n")).then_inc(qk_in[par], 16)
                        _, page = nc.values_load_multi_w_load_instructions(
                            pages[0:1, bass.ds(b * NPP, NPP)], engines=[mybir.EngineType.SP], min_val=0,
                            max_val=PAGES - 1, skip_runtime_bounds_check_because="the table names pages of the cache")
                        for i in range(NPP):
                            sp.dma_start(k_t[:, par, i].rearrange("p g n -> p (g n)"),
                                         k_pages[bass.ds(page[i], 1)].rearrange("b d n -> (b d) n"))\
                                .then_inc(qk_in[par], 16)
                        at_least(sp, summed, (b - 1) * HK)
                        sp.dma_start(v_own[:, par], v_dram[bass.ds(b * S, S), :]).then_inc(v_own_in[par], 16)
                        if not first:
                            store(p, par, b - 2)

                def tail(p):
                    for par in range(2):
                        store(p, par, p * 2 + par - 2)
                    for par in range(2):
                        sp.wait_ge(o_stored[par], 16 * PAIRS)

                over_pairs(sp, emit, tail)

            @block.gpsimd
            def _(pool):
                def emit(p, first):
                    for par in range(2):
                        b = p * 2 + par
                        at_least(pool, summed, (b - 1) * HK)
                        nc.gpsimd.tensor_add(v_row[:, par], page_row[:, bass.ds(b * KC, KC)],
                                             in_page_i[:, :].broadcast_to([P, KC])).then_inc(v_named, 1)
                        at_least(pool, masked_in, b)
                        pool.wait_ge(v_named, b + 1)
                        nc.gpsimd.tensor_sub(past[:, :], key_index[:, :],
                                             seq_f[:, bass.ds(b, 1)].broadcast_to([P, KEYS])).then_inc(past_done, 1)
                        for c in range(KC):
                            pool.indirect_dma_start(
                                out=v_c[:, par, c], out_offset=None, in_=v_rows[:, :],
                                in_offset=bass.IndirectOffsetOnAxis(ap=v_row[:, par, c:c + 1], axis=0))\
                                .then_inc(v_in[par], 16)

                over_pairs(pool, emit)

            @block.scalar
            def _(act):
                def pt_evacuate(n, i):
                    act.wait_ge(turned, n + 1)
                    at_least(act, summed, n - 1)
                    nc.scalar.activation(p_t[:, i, 2:4].rearrange("p c n -> p (c n)"), pt_b[:, 0:2 * ROWS], ACT.Copy)
                    nc.scalar.activation(p_t_own[:, i], pt_b[0:S, 2 * ROWS:3 * ROWS], ACT.Copy).then_inc(pt_b_out, 1)

                def o_evacuate(n, p, j):
                    par, g = (j // HK) % 2, j % HK
                    act.wait_ge(summed, n + 1)
                    if g == 0:
                        at_least(act, o_stored[par], p * 16)
                    nc.scalar.activation(o_t[:, par, g], o_banks[j % 2][:, 0:ROWS], ACT.Copy).then_inc(o_out, 1)

                def emit(p, first):
                    for j in range(UNITS):
                        n = p * UNITS + j
                        if not (first and j < 2):
                            pt_evacuate(n - 2, j % 2)
                        if not (first and j < 3):
                            o_evacuate(n - 3, p if j >= 3 else p - 1, (j - 3) % UNITS)
                        act.wait_ge(masked, n + 1)
                        at_least(act, turned, n - 1)
                        nc.scalar.activation(probs[:, j % 2], scores[:, j % 2], ACT.Exp, scale=-1.0,
                                             bias=neg_max[:, j % 2:j % 2 + 1],
                                             accum_out=row_sum[:, j % 2:j % 2 + 1]).then_inc(weighed, 1)

                def tail(p):
                    n = p * UNITS
                    for j in range(3):
                        if j < 2:
                            pt_evacuate(n + j - 2, j % 2)
                        o_evacuate(n + j - 3, p - 1, (j - 3) % UNITS)

                over_pairs(act, emit, tail)

            @block.vector
            def _(dve):
                def pt_evacuate(n, i):
                    dve.wait_ge(turned, n + 1)
                    at_least(dve, summed, n - 1)
                    nc.vector.tensor_copy(p_t[:, i, 0:2].rearrange("p c n -> p (c n)"), pt_a[:, 0:2 * ROWS])\
                        .then_inc(pt_a_out, 1)

                def invert(n, i):
                    dve.wait_ge(weighed, n + 1)
                    nc.vector.reciprocal(inv_sum[:, i:i + 1], row_sum[:, i:i + 1]).then_inc(inverted, 1)

                def normalise(n, i):
                    nc.vector.tensor_scalar(probs[:, i], probs[:, i], inv_sum[:, i:i + 1], None, ALU.mult)\
                        .then_inc(normed, 1)

                def emit(p, first):
                    for j in range(UNITS):
                        n = p * UNITS + j
                        par, g, i = j // HK, j % HK, j % 2
                        if not (first and j < 2):
                            pt_evacuate(n - 2, i)
                        if g == 0:
                            b = p * 2 + par
                            dve.wait_ge(past_done, b + 1)
                            nc.vector.tensor_scalar(mask[:, par], past[:, :], 0.0, NEG, ALU.is_ge, ALU.mult)\
                                .then_inc(masked_in, 1)
                            dve.wait_ge(masked_in, b + 1)
                        if not (first and j < 1):
                            invert(n - 1, 1 - i)
                            dve.wait_ge(inverted, n)
                            dve.wait_ge(scored, n + 1)
                            normalise(n - 1, 1 - i)
                        else:
                            dve.wait_ge(scored, n + 1)
                        nc.vector.tensor_tensor_reduce(out=scores[:, i], in0=s_run[i], in1=mask[:, par],
                                                       scale=-SCALE, scalar=3.0e38, op0=ALU.add, op1=ALU.min,
                                                       accum_out=neg_max[:, i:i + 1]).then_inc(masked, 1)

                def tail(p):
                    n = p * UNITS
                    pt_evacuate(n - 2, 0)
                    invert(n - 1, 1)
                    dve.wait_ge(inverted, n)
                    normalise(n - 1, 1)
                    pt_evacuate(n - 1, 1)

                over_pairs(dve, emit, tail)

            @block.tensor
            def _(pe):
                def score(n, p, j):
                    par, g, i = j // HK, j % HK, j % 2
                    if g == 0:
                        pe.wait_ge(qk_in[par], 16 * QK_DMAS * (p + 1))
                    at_least(pe, masked, n - 1)
                    pe.matmul(s_banks[i][:, BANK - CUT:BANK], q_t[:, par, g], k_t[:, par, 0:CUT // PSIZE, g],
                              start=True, stop=True)
                    pe.matmul(s_banks[i][:, BANK:BANK - CUT + KEYS], q_t[:, par, g], k_t[:, par, CUT // PSIZE:, g],
                              start=True, stop=True).then_inc(scored, 1)

                def weigh_values(n, p, j):
                    par, g, i = (j // HK) % 2, j % HK, j % 2
                    if g == 0:
                        pe.wait_ge(v_in[par], 16 * KC * (p + 1))
                        pe.wait_ge(v_own_in[par], 16 * (p + 1))
                    at_least(pe, o_out, n - 1)
                    pe.wait_ge(pt_a_out, n + 1)
                    o_bank = o_banks[i][:, 0:ROWS]
                    for c in range(KC):
                        if c == 2:
                            pe.wait_ge(pt_b_out, n + 1)
                        pe.matmul(o_bank, v_c[:, par, c, g * HD:(g + 1) * HD], p_t[:, i, c], start=c == 0, stop=False)
                    pe.matmul(o_bank, v_own[:, par, g * HD:(g + 1) * HD], p_t_own[:, i], start=False, stop=True)\
                        .then_inc(summed, 1)

                def turn(n, i):
                    pe.wait_ge(normed, n + 1)
                    at_least(pe, pt_a_out, n)
                    at_least(pe, pt_b_out, n)
                    for c in range(KC):
                        pe.transpose((pt_a, pt_b)[c // 2][:, (c % 2) * ROWS:(c % 2 + 1) * ROWS],
                                     probs[:, i, c * P:(c + 1) * P], ident[:, :])
                    pe.transpose(pt_b[0:S, 2 * ROWS:3 * ROWS], probs[:, i, L:KEYS], ident[:, :]).then_inc(turned, 1)

                def emit(p, first):
                    for j in range(UNITS):
                        n = p * UNITS + j
                        score(n, p, j)
                        if not (first and j < 2):
                            weigh_values(n - 2, p if j >= 2 else p - 1, (j - 2) % UNITS)
                        if not (first and j < 1):
                            turn(n - 1, (j - 1) % 2)

                def tail(p):
                    n = p * UNITS
                    weigh_values(n - 2, p - 1, UNITS - 2)
                    turn(n - 1, 1)
                    weigh_values(n - 1, p - 1, UNITS - 1)

                over_pairs(pe, emit, tail)


def finish(nc, sem, ident, o_dram, x_rows, wo_t, lang, slot2, slot3, w1_t, wr_a_t, b1_rows, w2_t, bias2,
           a2_rows, b2_rows, b3_rows, a3_rows, out):
    CH = 8
    NCH = HQ // CH
    ER = E * R1
    LOWS = TB * R2
    GATE_STEPS = 10
    assert R2 == R3

    with ExitStack() as ctx:
        def sb(name, shape, dt=F32):
            return ctx.enter_context(nc.sbuf_tensor(name, shape, dt))

        def ps(name, shape):
            return ctx.enter_context(nc.psum_tensor(name, shape, F32))

        wo_hi = sb("wo_hi", [P, HQ, D], F32R)
        wo_lo = sb("wo_lo", [P, HQ, D], F32R)
        raw = sb("raw", [P, NCH, TB * CH * S])
        o_hi = sb("o_hi", [P, 2, CH, P], F32R)
        o_lo = sb("o_lo", [P, 2, CH, P], F32R)
        w1 = sb("w1", [P, DC, D])
        wr_a = sb("wr_a", [P, DC, E + ER])
        b1 = sb("b1", [ER, D])
        w2 = sb("w2", [P, DC, D])
        bias = sb("bias", [P, D])
        x_in = sb("x_in", [P, D])
        x1 = sb("x1", [P, D])
        x2 = sb("x2", [P, D])
        x2_bias = sb("x2_bias", [P, D])
        x3 = sb("x3", [P, D])
        x4 = sb("x4", [P, D])
        x_t = sb("x_t", [P, DC, P])
        low = sb("low", [P, ER])
        low_t = sb("low_t", [ER, P])
        down2 = sb("down2", [P, TB, DC, R2])
        up2 = sb("up2", [LOWS, D])
        down3 = sb("down3", [P, TB, DC, R3])
        up3 = sb("up3", [LOWS, D])
        own2 = sb("own2", [P, TB, R2])
        own3 = sb("own3", [P, TB, R3])
        lang_i = sb("lang_i", [P, NT], I32)
        lang_f = sb("lang_f", [P, NT])
        expert_i = sb("expert_i", [P, E], I32)
        expert = sb("expert", [P, E])
        slots = sb("slots", [1, NT, 2, TB], I32)
        logits = sb("logits", [P, E])
        lang_bias = sb("lang_bias", [P, E])
        highest = sb("highest", [P, 1])
        top = sb("top", [P, E])
        top_i = sb("top_i", [P, E], U32)
        top_f = sb("top_f", [P, E])
        gap = sb("gap", [P, 1])
        ratio = sb("ratio", [P, 1])
        denom = sb("denom", [P, 1])
        gate = sb("gate", [P, 2])
        gates1 = sb("gates1", [P, E])
        gates = sb("gates", [P, E])

        proj = ps("proj", [P, D])
        turn = ps("turn", [P, D])
        wide = ps("wide", [P, D])
        slim = ps("slim", [P, D])

        slots_in, lang_in, w_small_in = sem("slots_in"), sem("lang_in"), sem("w_small_in")
        raw_in = [sem(f"raw_in{i}") for i in range(NCH)]
        x_rows_in = sem("x_rows_in")
        own_set, expert_set, lang_set = sem("own_set"), sem("expert_set"), sem("lang_set")
        wo_hi_done, wo_split = sem("wo_hi_done"), sem("wo_split")
        o_hi_done, o_split = sem("o_hi_done"), sem("o_split")
        chunk_done = sem("chunk_done")
        x1_done, x2_done, x2b_done, x3_done, x4_done = (sem(f"x{i}_done") for i in ("1", "2", "2b", "3", "4"))
        x_turned, xt_out = sem("x_turned"), sem("xt_out")
        slim_done, low_done, low_turned, low_out = sem("slim_done"), sem("low_done"), sem("low_turned"), sem("low_out")
        wide_done = sem("wide_done")
        gate_step, gap_done, ratio_done, gates_done = sem("gate_step"), sem("gap_done"), sem("ratio_done"), sem("gates_done")
        down_in, up_in = [sem("down2_in"), sem("down3_in")], [sem("up2_in"), sem("up3_in")]
        out_stored = sem("out_stored")
        LAYERS = 3
        WO_PIECE = TB * CH * S // D
        WO_PIECES = HQ // WO_PIECE

        with nc.Block() as block:

            @block.sync
            def _(sp):
                for k in range(WO_PIECES):
                    at_least(sp, wo_split, k - NCH + 1)
                    sp.dma_start(raw[:, k % NCH].rearrange("p (h n) -> p h n", n=D),
                                 wo_t[:, k * WO_PIECE:(k + 1) * WO_PIECE, :]).then_inc(raw_in[k % NCH], 16)
                    if k == NCH - 1:
                        for i, ids in enumerate((slot2, slot3)):
                            sp.dma_start(slots[0:1, :, i], ids.rearrange("(o t a) -> o t a", o=1, a=TB)).then_inc(slots_in, 16)
                        for a in range(TB):
                            sp.dma_start(lang_i[S * a:S * (a + 1), :], lang[a::TB].partition_broadcast(S),
                                         allow_slow_non_contiguous=True).then_inc(lang_in, 16)
                    if k == NCH:
                        sp.dma_start(w1[:, :, :], w1_t).then_inc(w_small_in, 16)
                        sp.dma_start(wr_a[:, :, :], wr_a_t).then_inc(w_small_in, 16)
                        sp.dma_start(b1[:, :], b1_rows).then_inc(w_small_in, 16)
                        sp.dma_start(w2[:, :, :], w2_t).then_inc(w_small_in, 16)
                        sp.dma_start(bias[:, :], bias2.partition_broadcast(P)).then_inc(w_small_in, 16)

                def load_chunk(t, c):
                    if isinstance(t, int) and t == 0:
                        sp.wait_ge(wo_split, WO_PIECES - NCH + c + 1)
                    else:
                        sp.wait_ge(o_split, (t - 1) * NCH + c + 1)
                    src = o_dram[bass.ds(t * TB, TB), :, c * CH * S:(c + 1) * CH * S]
                    sp.dma_start(raw[:, c].rearrange("p (b n) -> p b n", b=TB), src.rearrange("b d n -> d b n"))\
                        .then_inc(raw_in[c], 16)

                def load_x(t):
                    sp.dma_start(x_in[:, :], x_rows[bass.ds(t * P, P), :]).then_inc(x_rows_in, 16)

                def gather(t, i, wait):
                    rows_d, rows_u = (a2_rows, b3_rows)[i], (b2_rows, a3_rows)[i]
                    down, up = (down2, down3)[i], (up2, up3)[i]
                    _, slot = nc.values_load_multi_w_load_instructions(
                        slots[0:1, bass.ds(t, 1), i].rearrange("o t a -> o (t a)"), engines=[mybir.EngineType.SP],
                        min_val=0, max_val=rows_d.shape[0] - 1, skip_runtime_bounds_check_because="slots name adapters")
                    if wait:
                        sp.wait_ge(wide_done, (t - 1) * LAYERS + 2 + i)
                    for a in range(TB):
                        sp.dma_start(down[:, a].rearrange("p c r -> p (c r)"),
                                     rows_d[bass.ds(slot[a], 1)].rearrange("s p n -> (s p) n")).then_inc(down_in[i], 16)
                        sp.dma_start(up[R2 * a:R2 * (a + 1), :],
                                     rows_u[bass.ds(slot[a], 1)].rearrange("s r n -> (s r) n")).then_inc(up_in[i], 16)

                def store(t):
                    sp.wait_ge(x4_done, t + 1)
                    sp.dma_start(out[bass.ds(t * P, P), :], x4[:, :]).then_inc(out_stored, 16)

                for c in range(NCH):
                    load_chunk(0, c)
                load_x(0)
                sp.wait_ge(slots_in, 16 * 2)
                gather(0, 0, False)
                gather(0, 1, False)
                for c in range(NCH):
                    load_chunk(1, c)

                def follow(t, ahead):
                    sp.wait_ge(x1_done, t + 1)
                    load_x(t + 1)
                    if ahead:
                        load_chunk(t + 2, 0)
                        load_chunk(t + 2, 1)
                    gather(t + 1, 0, True)
                    if ahead:
                        load_chunk(t + 2, 2)
                        load_chunk(t + 2, 3)
                    gather(t + 1, 1, True)
                    store(t)

                with sp.Fori(0, NT - 2) as t:
                    follow(t, True)
                follow(NT - 2, False)
                store(NT - 1)
                sp.wait_ge(out_stored, 16 * NT)

            @block.gpsimd
            def _(pool):
                nc.gpsimd.iota(expert_i[:, :], [[1, E]], base=0, channel_multiplier=0).then_inc(expert_set, 1)
                for own in (own2, own3):
                    nc.gpsimd.memset(own[:, :, :], 0.0).then_inc(own_set, 1)
                pool.wait_ge(own_set, 2)
                for own, scale in ((own2, LORA_SCALING), (own3, 1.0)):
                    for a in range(TB):
                        nc.gpsimd.memset(own[S * a:S * (a + 1), a, :], scale).then_inc(own_set, 1)

                def add_bias(t):
                    pool.wait_ge(x2_done, t + 1)
                    nc.gpsimd.tensor_add(x2_bias[:, :], x2[:, :], bias[:, :]).then_inc(x2b_done, 1)

                pool.wait_ge(w_small_in, 16 * 5)
                with pool.Fori(0, NT) as t:
                    add_bias(t)

            @block.scalar
            def _(act):
                for k in range(WO_PIECES):
                    act.wait_ge(raw_in[k % NCH], 16 * (k // NCH + 1))
                    nc.scalar.activation(wo_hi[:, k * WO_PIECE:(k + 1) * WO_PIECE, :],
                                         raw[:, k % NCH].rearrange("p (h n) -> p h n", n=D), ACT.Copy).then_inc(wo_hi_done, 1)

                def upper(t, c):
                    k = t * NCH + c
                    act.wait_ge(raw_in[c], 16 * (WO_PIECES // NCH) + 16 * t + 16)
                    at_least(act, chunk_done, k - 1)
                    nc.scalar.activation(o_hi[:, c % 2].rearrange("p h (b s) -> p b h s", s=S),
                                         raw[:, c].rearrange("p (b h s) -> p b h s", b=TB, s=S), ACT.Copy)\
                        .then_inc(o_hi_done, 1)

                def x_turn_out(t, layer):
                    act.wait_ge(x_turned, t * LAYERS + layer + 1)
                    nc.scalar.activation(x_t[:, :, :].rearrange("p c n -> p (c n)"), turn[:, :], ACT.Copy).then_inc(xt_out, 1)

                def low_turn_out(t, layer):
                    rows = ER if layer == 0 else LOWS
                    act.wait_ge(low_turned, t * LAYERS + layer + 1)
                    nc.scalar.activation(low_t[0:rows, :], turn[0:rows, 0:P], ACT.Copy).then_inc(low_out, 1)

                def chain(t, ahead, beyond):
                    if ahead:
                        upper(t + 1, 1)
                    x_turn_out(t, 0)
                    act.wait_ge(gap_done, t + 1)
                    nc.scalar.activation(ratio[:, :], gap[:, :], ACT.Exp).then_inc(ratio_done, 1)
                    low_turn_out(t, 0)
                    if ahead:
                        upper(t + 1, 2)
                    x_turn_out(t, 1)
                    low_turn_out(t, 1)
                    if ahead:
                        upper(t + 1, 3)
                    x_turn_out(t, 2)
                    low_turn_out(t, 2)
                    if beyond:
                        upper(t + 2, 0)

                for c in range(NCH):
                    upper(0, c)
                upper(1, 0)
                with act.Fori(0, NT - 2) as t:
                    chain(t, True, True)
                chain(NT - 2, True, False)
                chain(NT - 1, False, False)

            @block.vector
            def _(dve):
                for k in range(WO_PIECES):
                    dve.wait_ge(wo_hi_done, k + 1)
                    nc.vector.tensor_tensor(wo_lo[:, k * WO_PIECE:(k + 1) * WO_PIECE, :],
                                            raw[:, k % NCH].rearrange("p (h n) -> p h n", n=D),
                                            wo_hi[:, k * WO_PIECE:(k + 1) * WO_PIECE, :].bitcast(F32), ALU.subtract)\
                        .then_inc(wo_split, 1)
                dve.wait_ge(expert_set, 1)
                dve.wait_ge(lang_in, 16 * TB)
                nc.vector.tensor_copy(expert[:, :], expert_i[:, :]).then_inc(lang_set, 1)
                nc.vector.tensor_copy(lang_f[:, :], lang_i[:, :]).then_inc(lang_set, 1)
                dve.wait_ge(lang_set, 2)

                def lower(t, c):
                    k = t * NCH + c
                    dve.wait_ge(o_hi_done, k + 1)
                    nc.vector.tensor_tensor(o_lo[:, c % 2].rearrange("p h (b s) -> p b h s", s=S),
                                            raw[:, c].rearrange("p (b h s) -> p b h s", b=TB, s=S),
                                            o_hi[:, c % 2].bitcast(F32).rearrange("p h (b s) -> p b h s", s=S),
                                            ALU.subtract).then_inc(o_split, 1)

                def chain(t, ahead, beyond):
                    links = [0]

                    def link(ins):
                        links[0] += 1
                        ins.then_inc(gate_step, 1)
                        dve.wait_ge(gate_step, t * GATE_STEPS + links[0])

                    dve.wait_ge(chunk_done, t * NCH + NCH)
                    dve.wait_ge(x_rows_in, t * 16 + 16)
                    nc.vector.tensor_tensor(x1[:, :], proj[:, :], x_in[:, :], ALU.add).then_inc(x1_done, 1)
                    if ahead:
                        lower(t + 1, 1)
                    link(nc.vector.tensor_scalar(lang_bias[:, :], expert[:, :], lang_f[:, bass.ds(t, 1)], LANG_BIAS,
                                                 ALU.is_equal, ALU.mult))
                    dve.wait_ge(slim_done, t * LAYERS + 1)
                    link(nc.vector.tensor_tensor(logits[:, :], slim[:, 0:E], lang_bias[:, :], ALU.add))
                    nc.vector.tensor_reduce(highest[:, :], logits[:, :], AX.X, ALU.max)
                    link(nc.vector.max(top[:, :], logits[:, :]))
                    nc.vector.tensor_tensor(gap[:, :], top[:, 1:2], highest[:, :], ALU.subtract).then_inc(gap_done, 1)
                    link(nc.vector.max_index(top_i[:, :], top[:, :], logits[:, :]))
                    link(nc.vector.tensor_copy(top_f[:, :], top_i[:, :]))
                    dve.wait_ge(ratio_done, t + 1)
                    link(nc.vector.tensor_scalar(denom[:, :], ratio[:, :], 1.0, 1.0 / MOE_SCALING, ALU.add, ALU.mult))
                    link(nc.vector.reciprocal(gate[:, 0:1], denom[:, :]))
                    link(nc.vector.tensor_tensor(gate[:, 1:2], gate[:, 0:1], ratio[:, :], ALU.mult))
                    link(nc.vector.tensor_scalar(gates1[:, :], expert[:, :], top_f[:, 0:1], gate[:, 0:1], ALU.is_equal, ALU.mult))
                    link(nc.vector.tensor_scalar(gates[:, :], expert[:, :], top_f[:, 1:2], gate[:, 1:2], ALU.is_equal, ALU.mult))
                    assert links[0] == GATE_STEPS
                    nc.vector.tensor_tensor(gates[:, :], gates[:, :], gates1[:, :], ALU.add).then_inc(gates_done, 1)
                    dve.wait_ge(gates_done, t + 1)
                    nc.vector.tensor_tensor(low[:, :].rearrange("p (e r) -> p e r", r=R1),
                                            slim[:, E:E + ER].rearrange("p (e r) -> p e r", r=R1),
                                            gates[:, :].unsqueeze(2).broadcast_to([P, E, R1]), ALU.mult).then_inc(low_done, 1)
                    if ahead:
                        lower(t + 1, 2)
                    dve.wait_ge(wide_done, t * LAYERS + 1)
                    nc.vector.tensor_tensor(x2[:, :], wide[:, :], x1[:, :], ALU.add).then_inc(x2_done, 1)
                    dve.wait_ge(slim_done, t * LAYERS + 2)
                    nc.vector.tensor_tensor(low[:, 0:LOWS], slim[:, 0:LOWS], own2[:, :, :].rearrange("p a r -> p (a r)"),
                                            ALU.mult).then_inc(low_done, 1)
                    if ahead:
                        lower(t + 1, 3)
                    dve.wait_ge(wide_done, t * LAYERS + 2)
                    dve.wait_ge(x2b_done, t + 1)
                    nc.vector.tensor_tensor(x3[:, :], wide[:, :], x2_bias[:, :], ALU.add).then_inc(x3_done, 1)
                    dve.wait_ge(slim_done, t * LAYERS + 3)
                    nc.vector.tensor_tensor(low[:, 0:LOWS], slim[:, 0:LOWS], own3[:, :, :].rearrange("p a r -> p (a r)"),
                                            ALU.mult).then_inc(low_done, 1)
                    if beyond:
                        lower(t + 2, 0)
                    dve.wait_ge(wide_done, t * LAYERS + 3)
                    at_least(dve, out_stored, t * 16)
                    nc.vector.tensor_tensor(x4[:, :], wide[:, :], x3[:, :], ALU.add).then_inc(x4_done, 1)

                dve.wait_ge(own_set, 2 + 2 * TB)
                for c in range(NCH):
                    lower(0, c)
                lower(1, 0)
                chain(0, True, True)
                with dve.Fori(1, NT - 2) as t:
                    chain(t, True, True)
                chain(NT - 2, True, False)
                chain(NT - 1, False, False)

            @block.tensor
            def _(pe):
                def heads(t, h0, h1):
                    for h in range(h0, h1):
                        c, k = h // CH, t * NCH + h // CH
                        if h % CH == 0:
                            pe.wait_ge(o_split, k + 1)
                        i = h % CH
                        pe.matmul(proj[:, :], o_hi[:, c % 2, i], wo_hi[:, h], start=h == 0, stop=False)
                        pe.matmul(proj[:, :], o_hi[:, c % 2, i], wo_lo[:, h], start=False, stop=False)
                        last = pe.matmul(proj[:, :], o_lo[:, c % 2, i], wo_hi[:, h], start=False, stop=h == HQ - 1)
                        if i == CH - 1:
                            last.then_inc(chunk_done, 1)

                def chain(t, ahead):
                    at = [0]

                    def fill(n):
                        if ahead:
                            heads(t + 1, at[0], at[0] + n)
                            at[0] += n

                    for layer, (x, done) in enumerate(((x1, x1_done), (x2, x2_done), (x3, x3_done))):
                        pe.wait_ge(done, t + 1)
                        for c in range(DC):
                            last = pe.transpose(turn[:, c * P:(c + 1) * P], x[:, c * P:(c + 1) * P], ident[:, :])
                        last.then_inc(x_turned, 1)
                        fill((3, 2, 2)[layer])
                        pe.wait_ge(xt_out, t * LAYERS + layer + 1)
                        if layer:
                            pe.wait_ge(down_in[layer - 1], (t + 1) * 16 * TB)
                        for c in range(DC):
                            if layer == 0:
                                last = pe.matmul(slim[:, 0:E + ER], x_t[:, c], wr_a[:, c], start=c == 0, stop=c == DC - 1)
                            else:
                                last = pe.matmul(slim[:, 0:LOWS], x_t[:, c], (down2, down3)[layer - 1][:, :, c, :],
                                                 start=c == 0, stop=c == DC - 1)
                        last.then_inc(slim_done, 1)
                        if layer < 2:
                            for c in range(DC):
                                pe.matmul(wide[:, :], x_t[:, c], (w1, w2)[layer][:, c], start=c == 0, stop=False)
                        fill((4, 3, 4)[layer])
                        rows = ER if layer == 0 else LOWS
                        pe.wait_ge(low_done, t * LAYERS + layer + 1)
                        pe.transpose(turn[:, 0:P], low[:, :], ident[:, :]).then_inc(low_turned, 1)
                        fill((3, 3, 3)[layer])
                        pe.wait_ge(low_out, t * LAYERS + layer + 1)
                        if layer:
                            pe.wait_ge(up_in[layer - 1], (t + 1) * 16 * TB)
                        pe.matmul(wide[:, :], low_t[0:rows, :], (b1, up2, up3)[layer][:, :], start=layer == 2, stop=True)\
                            .then_inc(wide_done, 1)
                        fill((2, 2, 1)[layer])
                    assert not ahead or at[0] == HQ

                pe.wait_ge(wo_split, WO_PIECES)
                heads(0, 0, HQ)
                pe.wait_ge(w_small_in, 16 * 5)
                with pe.Fori(0, NT - 1) as t:
                    chain(t, True)
                chain(NT - 1, False)


def kernel(**inputs):
    import numpy as np
    import concourse.bacc as bacc
    from concourse.bass_utils import run_bass_kernel_spmd as run

    a = {k: np.asarray(v) for k, v in inputs.items()}

    def chunked(w):
        return w.T.reshape(DC, P, -1).transpose(1, 0, 2)

    x = a["x"].reshape(TOK, D)
    w = np.concatenate([a["L0_cond_Wq"], a["L0_cond_Wk"], a["L0_cond_Wv"]])
    exponent = np.arange(0, HD, 2, dtype=np.float32) / np.float32(HD)
    arrays = {
        "x_t": chunked(x).reshape(P, DC, 4, TOK // 4).transpose(2, 0, 1, 3),
        "x_rows": x,
        "w_qkv": chunked(w).reshape(P, DC, NSL, SLICE).transpose(2, 0, 1, 3),
        "wo_t": a["L0_cond_Wo"].T.reshape(HQ, HD, D).transpose(1, 0, 2),
        "q_norm_w": a["L0_cond_q_norm_w"],
        "k_norm_w": a["L0_cond_k_norm_w"],
        "inv_freq": (np.float32(1.0) / np.float32(10000.0) ** exponent).astype(np.float32),
        "k_pages": a["L0_cond_k_cache"].transpose(0, 3, 2, 1).reshape(PAGES, HD, HK * PSIZE),
        "v_rows": a["L0_cond_v_cache"].reshape(PAGES * PSIZE, HK * HD),
        "block_table": a["itok_Bx16_0_63"].reshape(B * NPP),
        "seqlens": a["itok_B_207_1644"],
        "lang": a["itok_B_0_7"],
        "slot2": a["itok_B_0_23"],
        "slot3": a["itok_B_4_50"],
        "w1_t": chunked(a["L1_cond_W"]),
        "wr_a_t": chunked(np.concatenate([a["L1_cond_Wr"], a["L1_cond_A"].reshape(E * R1, D)])),
        "b1_rows": a["L1_cond_B"].transpose(0, 2, 1).reshape(E * R1, D),
        "w2_t": chunked(a["L2_cond_W"]),
        "bias2": a["L2_cond_b"],
        "a2_rows": a["L2_cond_lora_As"].reshape(-1, DC, P, R2).transpose(0, 2, 1, 3).reshape(-1, P, DC * R2),
        "b2_rows": a["L2_cond_lora_Bs"],
        "b3_rows": a["L3_cond_B"].reshape(-1, R3, DC, P).transpose(0, 3, 2, 1).reshape(-1, P, DC * R3),
        "a3_rows": a["L3_cond_A"].transpose(0, 2, 1),
    }
    arrays = {k: np.ascontiguousarray(v) for k, v in arrays.items()}
    nc = bacc.Bacc("TRN2", target_bir_lowering=False, num_devices=1)
    args = [nc.dram_tensor(f"in_{k}", v.shape, mybir.dt.from_np(v.dtype), kind="ExternalInput").ap()
            for k, v in arrays.items()]
    out = nc.dram_tensor("out_x", (TOK, D), F32, kind="ExternalOutput").ap()
    decoder(nc, *args, out)
    r = run(nc, [{f"in_{k}": v for k, v in arrays.items()}], core_ids=[0])
    return r.results[0]["out_x"].reshape(B, S, D)
```

```python
from contextlib import ExitStack

import numpy as np

import concourse.bass as bass
from concourse import mybir
from concourse.alu_op_type import AluOpType as ALU

ACT = mybir.ActivationFunctionType
AX = mybir.AxisListType
F32 = mybir.dt.float32
F32R = mybir.dt.float32r
I32 = mybir.dt.int32
U32 = mybir.dt.uint32

P = 128
B, S, D = 64, 32, 512
DC = D // P
TOK = B * S
TB = P // S
NT = TOK // P
HQ, HK, HD = 32, 8, 128
REP = HQ // HK
NPP, PSIZE, PAGES = 16, 32, 64
L = NPP * PSIZE
KEYS = L + S
KC = L // P
ROWS = REP * S
QUARTER = 4
SLICE = 512
NQ, NK, NV = HQ * HD // SLICE, HK * HD // SLICE, HK * HD // SLICE
NSL = NQ + NK + NV
HS = SLICE // HD
SLOTS = NPP + 2
O_BYTES = 2 * HK * ROWS * 4
WO_EARLY = 24
HALF = HD // 2
SCALE = float(HD) ** -0.5
RMS_EPS = 1e-6
NEG = -1e30
E, R1 = 8, 16
LANG_BIAS = 5.0
MOE_SCALING = 2.0
R2, LORA_SCALING = 16, 2.0
R3 = 16
TWO_PI = 6.283185307179586
TWO_PI_HI, TWO_PI_LO = 6.28125, 0.0019353071795864769
ROUND = 12582912.0
PI_IN = 3.1415925


def at_least(engine, sem, value):
    if not (isinstance(value, int) and value <= 0):
        engine.wait_ge(sem, value)


def o_start(nc):
    return (nc.sbuf_usable_end - O_BYTES) // 32 * 32


def decoder(nc, x_t, x_rows, w_qkv, wo_t, q_norm_w, k_norm_w, inv_freq, k_pages, v_rows, block_table, seqlens,
            lang, slot2, slot3, w1_t, wr_a_t, b1_rows, w2_t, bias2, a2_rows, b2_rows, b3_rows, a3_rows, out):
    with ExitStack() as whole:
        def sem(name):
            return whole.enter_context(nc.semaphore(name))

        ident = whole.enter_context(nc.sbuf_tensor("ident", [P, P], F32))
        wo_start = nc.sbuf_base
        wo_early = whole.enter_context(nc.sbuf_tensor("wo_early", [P, WO_EARLY, D], F32))
        wo_in = sem("wo_in")
        o_stored = [sem("o_stored0"), sem("o_stored1")]
        q_dram = nc.dram_tensor("q_spill", (B, HD, HQ * S), F32, kind="Internal").ap()
        k_dram = nc.dram_tensor("k_spill", (B, HD, HK * S), F32, kind="Internal").ap()
        v_dram = nc.dram_tensor("v_spill", (TOK, HK * HD), F32, kind="Internal").ap()
        o_dram = nc.dram_tensor("o_spill", (B, HD, HQ * S), F32, kind="Internal").ap()

        with ExitStack() as ctx:
            def sb(name, shape, dt=F32):
                return ctx.enter_context(nc.sbuf_tensor(name, shape, dt))

            seq_f = sb("seq_f", [P, B])
            pages = sb("pages", [P, B * NPP], I32)
            page_row = sb("page_row", [P, B * KC], I32)
            in_page_i = sb("in_page_i", [P, 1], I32)
            key_index = sb("key_index", [P, L])
            tables = (seq_f, pages, page_row, in_page_i, key_index)
            q_t = sb("q_t", [P, 2, HK, ROWS])
            k_t = sb("k_t", [P, 2, SLOTS, HK, PSIZE])
            v_c = sb("v_c", [P, 2, KC, HK * HD])
            v_row = sb("v_row", [P, 2, KC], I32)
            qk_in = [sem("qk_in0"), sem("qk_in1")]
            v_in = [sem("v_in0"), sem("v_in1")]
            v_named = sem("v_named")

            def load_keys(sp, b, par):
                for i in (0, SLOTS - 1):
                    sp.dma_start(k_t[:, par, i].rearrange("p g n -> p (g n)"),
                                 k_dram[bass.ds(b, 1)].rearrange("b d n -> (b d) n")).then_inc(qk_in[par], 16)
                _, page = nc.values_load_multi_w_load_instructions(
                    pages[0:1, bass.ds(b * NPP, NPP)], engines=[mybir.EngineType.SP], min_val=0,
                    max_val=PAGES - 1, skip_runtime_bounds_check_because="the table names pages of the cache")
                for i in range(NPP):
                    sp.dma_start(k_t[:, par, i + 1].rearrange("p g n -> p (g n)"),
                                 k_pages[bass.ds(page[i], 1)].rearrange("b d n -> (b d) n")).then_inc(qk_in[par], 16)

            def load_queries(sp, b, par):
                sp.dma_start(q_t[:, par].rearrange("p g n -> p (g n)"),
                             q_dram[bass.ds(b, 1)].rearrange("b d n -> (b d) n")).then_inc(qk_in[par], 16)

            def name_values(b, par):
                nc.gpsimd.tensor_add(v_row[:, par], page_row[:, bass.ds(b * KC, KC)],
                                     in_page_i[:, :].broadcast_to([P, KC])).then_inc(v_named, 1)

            def gather_values(pool, par):
                for c in range(KC):
                    pool.indirect_dma_start(
                        out=v_c[:, par, c], out_offset=None, in_=v_rows[:, :],
                        in_offset=bass.IndirectOffsetOnAxis(ap=v_row[:, par, c:c + 1], axis=0)).then_inc(v_in[par], 16)

            stored = [sem("stored0"), sem("stored1")]
            loads = (load_keys, load_queries, name_values, gather_values)
            project(nc, sem, ident, *tables, q_t, k_t, v_c, v_named, wo_early, wo_start, stored, loads, x_t, w_qkv, q_norm_w, k_norm_w,
                    inv_freq, block_table, seqlens, q_dram, k_dram, v_dram)
            attend(nc, sem, ident, *tables, q_t, k_t, v_c, qk_in, v_in, v_named, wo_early, wo_in, stored, o_stored, loads, wo_t,
                   v_dram, o_dram)
        finish(nc, sem, ident, wo_early, wo_start, wo_in, o_stored, o_dram, x_rows, wo_t, lang, slot2, slot3, w1_t, wr_a_t, b1_rows, w2_t, bias2,
               a2_rows, b2_rows, b3_rows, a3_rows, out)


def project(nc, sem, ident, seq_f, pages, page_row, in_page_i, key_index, q_t, k_t, v_c, v_named, wo_early, wo_start, stored, loads,
            x_t, w_qkv, q_norm_w, k_norm_w, inv_freq, block_table, seqlens, q_dram, k_dram, v_dram):
    MM_BANKS = 4
    PAIRS = NSL // 2
    PS = 2 * NT

    with ExitStack() as ctx:
        def sb(name, shape, dt=F32):
            return ctx.enter_context(nc.sbuf_tensor(name, shape, dt))

        def part(buffer, start, shape, dt=F32):
            names = " ".join(f"d{i}" for i in range(len(shape) - 1))
            sizes = {f"d{i}": n for i, n in enumerate(shape[1:])}
            n = int(np.prod(shape[1:]))
            ap = buffer[:, start:start + n]
            ap = ap if dt == F32 else ap.bitcast(dt)
            return ap.rearrange(f"p ({names}) -> p {names}", **sizes)

        TRIG = NT * HALF
        k_halves = [k_t[:, i].rearrange("p s g n -> p (s g n)") for i in range(2)]
        v_flat = v_c[:, :, :, :].rearrange("p i c n -> p (i c n)")
        wo_flat = wo_early[:, :, :].rearrange("p h n -> p (h n)")
        X_RAW = 2 * DC * QUARTER * P
        x_raw = part(k_halves[0], 0, [P, 2, DC, QUARTER * P])
        freq = part(k_halves[0], X_RAW, [P, HALF])
        seq_i = part(k_halves[0], X_RAW + HALF, [P, B], I32)
        pos = part(k_halves[0], X_RAW + HALF + B, [P, NT])
        in_page = part(k_halves[0], X_RAW + HALF + B + NT, [P, 1])
        smalls = X_RAW + HALF + B + NT + 1
        eps = part(k_halves[0], smalls, [P, 1])
        sumsq, rms, rstd = (part(k_halves[0], smalls + 1 + i * 2 * HS, [P, 2, HS]) for i in range(3))
        w_raw = part(k_halves[1], 0, [P, 2, DC, SLICE])
        part_s = part(k_halves[1], 2 * DC * SLICE, [P, HS, HD])
        norm_q = part(k_halves[0], smalls + 1 + 6 * HS, [P, HD])
        norm_k = part(k_halves[0], smalls + 1 + 6 * HS + HD, [P, HD])
        tabs = [part(v_flat, i * NT * HD, [P, NT, HD]) for i in range(4)]
        straight, crossed = {"q": tabs[0], "k": tabs[1]}, {"q": tabs[2], "k": tabs[3]}
        part_c = part(q_t[:, 0].rearrange("p g n -> p (g n)"), 0, [P, 2, HS, HD])
        roped = part(q_t[:, 1].rearrange("p g n -> p (g n)"), 0, [P, 2, HS, HD])
        x_hi = nc.alloc_sbuf_tensor_at("x_hi", [P, DC, TOK], F32R, offset=wo_start)
        stage = part(wo_flat, DC * TOK, [P, 2, QUARTER * SLICE])

        x_lo = sb("x_lo", [P, DC, TOK], F32R)
        w_hi = sb("w_hi", [P, 2, DC, SLICE], F32R)
        w_lo = sb("w_lo", [P, 2, DC, SLICE], F32R)
        sin = sb("sin", [P, NT, HALF])
        squares = sb("squares", [P, 2, HS, HD])
        normed = sb("normed", [P, 2, HS, HD])
        stage_flat = stage.rearrange("p i n -> p (i n)")
        angle, turns, reduced = (part(stage_flat, i * TRIG, [P, NT, HALF]) for i in range(3))
        key_i = part(stage_flat, 3 * TRIG, [P, L], I32)
        cos = part(roped.rearrange("p i h d -> p (i h d)"), 0, [P, NT, HALF])
        nsin = part(part_c.rearrange("p i h d -> p (i h d)"), 0, [P, NT, HALF])
        acc = [ctx.enter_context(nc.psum_tensor(f"acc{i}", [P, SLICE], F32)) for i in range(MM_BANKS)]
        flip = [ctx.enter_context(nc.psum_tensor(f"flip{i}", [P, SLICE], F32)) for i in range(2)]

        load_keys, load_queries, name_values, gather_values = loads
        PIECES = [(0, 1), (1, 2), (2, 4), (4, 8), (8, 12), (12, 16)]
        X_DONE = [sum(hi <= QUARTER * (q + 1) for _, hi in PIECES) for q in range(NT // QUARTER)]

        LATE = {3: 4, 6: 5}

        def piece(k):
            lo, hi = PIECES[k]
            q = lo // QUARTER
            return slice(lo * P, hi * P), q, slice((lo - q * QUARTER) * P, (hi - q * QUARTER) * P)

        angles_in, consts_in = sem("angles_in"), sem("consts_in")
        x_in = [sem("x_in0"), sem("x_in1")]
        w_in = [sem("w_in0"), sem("w_in1")]
        iota_done = sem("iota_done")
        ident_done = sem("ident_done")
        table_step = sem("table_step")
        angles_done = sem("angles_done")
        trig_done = sem("trig_done")
        tables_q = sem("tables_q")
        tables_k = sem("tables_k")
        x_hi_done = sem("x_hi_done")
        x_split = sem("x_split")
        w_hi_done = sem("w_hi_done")
        w_split = sem("w_split")
        mm_done = sem("mm_done")
        squared = sem("squared")
        summed = sem("summed")
        rooted = sem("rooted")
        rstd_done = sem("rstd_done")
        drained = sem("drained")
        straight_done = sem("straight_done")
        crossed_done = sem("crossed_done")
        roped_done = sem("roped_done")
        flipped = sem("flipped")
        staged_qk = sem("staged_qk")
        staged_v = sem("staged_v")

        KIND = ["q"] * (NQ // 2) + ["k"] * (NK // 2) + ["v"] * (NV // 2)
        QKS = (NQ + NK) * NT

        def over_pairs(engine, emit):
            emit(0, "q", None)
            with engine.Fori(1, NQ // 2) as p:
                emit(p, "q", "q")
            for p in range(NQ // 2, PAIRS):
                emit(p, KIND[p], KIND[p - 1])

        with nc.Block() as block:

            @block.sync
            def _(sp):
                sp.dma_start(seq_i, seqlens.partition_broadcast(P)).then_inc(angles_in, 16)
                sp.dma_start(freq, inv_freq.partition_broadcast(P)).then_inc(angles_in, 16)
                sp.dma_start(w_raw[:, 0], w_qkv[0]).then_inc(w_in[0], 16)
                sp.dma_start(x_raw[:, 0], x_t[0]).then_inc(x_in[0], 16)
                sp.dma_start(norm_q, q_norm_w.partition_broadcast(P)).then_inc(consts_in, 16)
                sp.dma_start(norm_k, k_norm_w.partition_broadcast(P)).then_inc(consts_in, 16)
                sp.dma_start(pages[:, :], block_table.partition_broadcast(P)).then_inc(consts_in, 16)
                sp.dma_start(x_raw[:, 1], x_t[1]).then_inc(x_in[1], 16)
                sp.dma_start(w_raw[:, 1], w_qkv[1]).then_inc(w_in[1], 16)
                for q in range(2, NT // QUARTER):
                    sp.wait_ge(x_split, X_DONE[q - 2])
                    sp.dma_start(x_raw[:, q % 2], x_t[q]).then_inc(x_in[q % 2], 16)

                def first_batch(par):
                    if par == 0:
                        for i in range(2):
                            sp.wait_ge(stored[i], 16 * (NQ + NK) * (NT // QUARTER) // 2)
                        sp.wait_ge(x_split, len(PIECES))
                        sp.wait_ge(flipped, QKS)
                        sp.wait_ge(tables_k, 4)
                    else:
                        sp.wait_ge(w_split, DC * NSL)
                    load_keys(sp, par, par)
                    load_queries(sp, par, par)

                def emit(p, kind, before):
                    for par in range(2):
                        s = p * 2 + par
                        if kind != "v":
                            sp.wait_ge(w_split, DC * s + DC)
                            sp.dma_start(w_raw[:, par], w_qkv[bass.ds(s + 2, 1)].rearrange("a p c n -> (a p) c n")
                                         if not isinstance(s, int) else w_qkv[s + 2]).then_inc(w_in[par], 16)
                        for g in range(NT // QUARTER):
                            buf = stage[:, g % 2]
                            if kind == "v":
                                sp.wait_ge(staged_v, NT * s - QKS + QUARTER * (g + 1))
                                n = s - NQ - NK
                                dst = v_dram[g * QUARTER * P:(g + 1) * QUARTER * P, n * SLICE:(n + 1) * SLICE]
                                sp.dma_start(dst.rearrange("(t p) n -> p t n", p=P),
                                             buf.rearrange("p (t n) -> p t n", n=SLICE)).then_inc(stored[g % 2], 16)
                            else:
                                sp.wait_ge(staged_qk, NT * s + QUARTER * (g + 1))
                                to, n = (q_dram, s) if kind == "q" else (k_dram, s - NQ)
                                b0 = g * QUARTER * TB
                                dst = to[b0:b0 + QUARTER * TB, :, bass.ds(n * HS * S, HS * S)]
                                sp.dma_start(dst.rearrange("b d n -> d b n"),
                                             buf.rearrange("p (b n) -> p b n", n=HS * S)).then_inc(stored[g % 2], 16)
                            if kind == "v" and g == 1:
                                first_batch(par)

                over_pairs(sp, emit)
            @block.gpsimd
            def _(pool):
                nc.gpsimd.memset(ident[:, :], 0.0).then_inc(ident_done, 1)
                pool.wait_ge(ident_done, 1)
                nc.gpsimd.affine_select(out=ident[:, :], in_=ident[:, :], compare_op=ALU.not_equal, fill=1.0,
                                        base=0, pattern=[[-1, P]], channel_multiplier=1).then_inc(ident_done, 1)
                pool.wait_ge(ident_done, 2)
                for i in range(TB):
                    nc.gpsimd.iota(in_page_i[PSIZE * i:PSIZE * (i + 1), :], [[0, 1]], base=0, channel_multiplier=1)\
                        .then_inc(iota_done, 1)
                pool.wait_ge(iota_done, TB)
                nc.gpsimd.iota(key_i[:, :], [[1, L]], base=0, channel_multiplier=0).then_inc(iota_done, 1)

                def split(s, par, c):
                    nc.gpsimd.tensor_copy(w_hi[:, par, c], w_raw[:, par, c]).then_inc(w_hi_done, 1)
                    pool.wait_ge(w_hi_done, DC * s + c + 1)
                    nc.gpsimd.tensor_sub(w_lo[:, par, c], w_raw[:, par, c], w_hi[:, par, c].bitcast(F32))\
                        .then_inc(w_split, 1)

                pool.wait_ge(trig_done, 3)
                pool.wait_ge(consts_in, 16 * 3)

                def table(to, trig, w):
                    nc.gpsimd.tensor_mul(to, trig[:, :, :], w.unsqueeze(1).broadcast_to([P, NT, HALF]))\
                        .then_inc(tables_k, 1)

                table(straight["k"][:, :, 0:HALF], cos, norm_k[:, 0:HALF])
                table(straight["k"][:, :, HALF:HD], cos, norm_k[:, HALF:HD])
                table(crossed["k"][:, :, 0:HALF], nsin, norm_k[:, HALF:HD])
                table(crossed["k"][:, :, HALF:HD], sin, norm_k[:, 0:HALF])
                pool.wait_ge(tables_k, 4)
                pool.wait_ge(tables_q, 4)

                def emit(p, kind, before):
                    for j in range(PS):
                        n = p * PS + j
                        par, t = j // NT, j % NT
                        s = p * 2 + par + 1
                        splits = t in (3, 6, 9, 12) and not (kind == "v" and par == 1)
                        if splits and t == 3:
                            pool.wait_ge(w_in[1 - par], 16 * p + 16 if par == 0 else 16 * p + 32)
                            at_least(pool, mm_done, NT * (s - 1))
                        lag = kind if j >= 2 else before
                        if lag in ("q", "k"):
                            m, i = n - 2, j % 2
                            pool.wait_ge(drained, m + 1)
                            at_least(pool, roped_done, m - 1)
                            cr = crossed[lag]
                            for lo, hi in ((0, HALF), (HALF, 0)):
                                last = nc.gpsimd.tensor_mul(
                                    part_c[:, i, :, lo:lo + HALF], normed[:, i, :, hi:hi + HALF],
                                    cr[:, (j - 2) % NT, lo:lo + HALF].unsqueeze(1).broadcast_to([P, HS, HALF]))
                            last.then_inc(crossed_done, 1)
                        if splits:
                            split(s, 1 - par, t // 3 - 1)

                over_pairs(pool, emit)
                pool.wait_ge(roped_done, QKS)
                for par in range(2):
                    name_values(par, par)
                pool.wait_ge(v_named, 2)
                for par in range(2):
                    gather_values(pool, par)

            @block.scalar
            def _(act):
                def upper(k):
                    cols, q, raw = piece(k)
                    act.wait_ge(x_in[q % 2], 16 * (q // 2 + 1))
                    nc.scalar.activation(x_hi[:, :, cols], x_raw[:, q % 2, :, raw], ACT.Copy).then_inc(x_hi_done, 1)

                act.wait_ge(w_in[0], 16)
                for c in range(DC):
                    nc.scalar.activation(w_hi[:, 0, c], w_raw[:, 0, c], ACT.Copy).then_inc(w_hi_done, 1)
                for k in range(4):
                    upper(k)
                act.wait_ge(angles_done, 1)
                nc.scalar.activation(sin[:, :, :], reduced, ACT.Sin).then_inc(trig_done, 1)
                nc.scalar.activation(nsin, reduced, ACT.Sin, scale=-1.0).then_inc(trig_done, 1)
                act.wait_ge(angles_done, 2)
                nc.scalar.activation(cos, angle, ACT.Sin).then_inc(trig_done, 1)
                def emit(p, kind, before):
                    for j in range(PS):
                        n = p * PS + j
                        lag, i = (kind if j >= 1 else before), (j - 1) % 2
                        if lag in ("q", "k"):
                            act.wait_ge(summed, n)
                            nc.scalar.activation(rms[:, i], sumsq[:, i], ACT.Sqrt, bias=eps[:, 0:1], scale=1.0 / HD)\
                                .then_inc(rooted, 1)
                        if kind != "v":
                            act.wait_ge(mm_done, n + 1)
                            nc.scalar.activation(squares[:, j % 2], acc[j % MM_BANKS][:, :].rearrange(
                                "p (h d) -> p h d", d=HD), ACT.Square).then_inc(squared, 1)
                        if lag in ("q", "k"):
                            act.wait_ge(rstd_done, n)
                            at_least(act, roped_done, n - 2)
                            for h in range(HS):
                                last = nc.scalar.activation(normed[:, i, h],
                                                            acc[(j - 1) % MM_BANKS][:, h * HD:(h + 1) * HD],
                                                            ACT.Copy, scale=rstd[:, i, h:h + 1])
                            last.then_inc(drained, 1)
                        if kind == "v":
                            act.wait_ge(mm_done, n + 1)
                            t = j % NT
                            if t % QUARTER == 0:
                                g = t // QUARTER
                                s = p * 2 + j // NT
                                act.wait_ge(stored[g % 2], 16 * (s * 2 + g // 2))
                            nc.scalar.activation(stage[:, (t // QUARTER) % 2, (t % QUARTER) * SLICE:(t % QUARTER + 1) * SLICE],
                                                 acc[j % MM_BANKS][:, :], ACT.Copy).then_inc(staged_v, 1)

                        if before is None and j in LATE:
                            upper(LATE[j])

                over_pairs(act, emit)

            @block.vector
            def _(dve):
                steps = [0]

                def link(ins):
                    steps[0] += 1
                    ins.then_inc(table_step, 1)
                    dve.wait_ge(table_step, steps[0])

                nc.vector.memset(eps[:, :], RMS_EPS)
                dve.wait_ge(iota_done, TB + 1)
                dve.wait_ge(angles_in, 16 * 2)
                link(nc.vector.tensor_copy(in_page, in_page_i[:, :]))
                link(nc.vector.tensor_copy(seq_f[:, :], seq_i))
                for i in range(TB):
                    q = slice(PSIZE * i, PSIZE * (i + 1))
                    last = nc.vector.tensor_scalar(pos[q, :], seq_f[q, i::TB], in_page[q, 0:1], None, ALU.add)
                link(last)
                link(nc.vector.tensor_tensor(angle, pos.unsqueeze(2).broadcast_to([P, NT, HALF]),
                                             freq.unsqueeze(1).broadcast_to([P, NT, HALF]), ALU.mult))

                for c in range(DC):
                    dve.wait_ge(w_hi_done, c + 1)
                    nc.vector.tensor_tensor(w_lo[:, 0, c], w_raw[:, 0, c], w_hi[:, 0, c].bitcast(F32), ALU.subtract)\
                        .then_inc(w_split, 1)

                def lower(k):
                    cols, q, raw = piece(k)
                    dve.wait_ge(x_hi_done, k + 1)
                    nc.vector.tensor_tensor(x_lo[:, :, cols], x_raw[:, q % 2, :, raw], x_hi[:, :, cols].bitcast(F32),
                                            ALU.subtract).then_inc(x_split, 1)

                lower(0)
                nc.vector.tensor_copy(key_index[:, :], key_i)
                link(nc.vector.tensor_scalar(turns, angle, 1.0 / TWO_PI, ROUND, ALU.mult, ALU.add))
                link(nc.vector.tensor_scalar(turns, turns, ROUND, None, ALU.subtract))
                link(nc.vector.scalar_tensor_tensor(out=reduced, in0=turns, scalar=-TWO_PI_HI, in1=angle,
                                                    op0=ALU.mult, op1=ALU.add))
                link(nc.vector.scalar_tensor_tensor(out=reduced, in0=turns, scalar=-TWO_PI_LO, in1=reduced,
                                                    op0=ALU.mult, op1=ALU.add))
                lower(1)
                nc.vector.tensor_scalar(reduced, reduced, PI_IN, -PI_IN, ALU.min, ALU.max).then_inc(angles_done, 1)
                lower(2)
                dve.wait_ge(angles_done, 1)
                link(nc.vector.tensor_scalar(turns, reduced, TWO_PI / 4, -TWO_PI, ALU.is_gt, ALU.mult))
                link(nc.vector.scalar_tensor_tensor(out=angle, in0=reduced, scalar=TWO_PI / 4, in1=turns,
                                                    op0=ALU.add, op1=ALU.add))
                nc.vector.tensor_scalar(angle, angle, PI_IN, -PI_IN, ALU.min, ALU.max).then_inc(angles_done, 1)
                lower(3)
                def page_rows():
                    for i in range(TB):
                        q = slice(PSIZE * i, PSIZE * (i + 1))
                        nc.vector.tensor_scalar(page_row[q, :].rearrange("p (b c) -> p b c", c=KC),
                                                pages[q, :].rearrange("p (b c i) -> p b c i", c=KC, i=TB)[:, :, :, i],
                                                float(PSIZE), None, ALU.mult)

                def query_tables():
                    for k, (to, trig, w) in enumerate(((crossed["q"][:, :, 0:HALF], nsin, norm_q[:, HALF:HD]),
                                                       (crossed["q"][:, :, HALF:HD], sin, norm_q[:, 0:HALF]),
                                                       (straight["q"][:, :, 0:HALF], cos, norm_q[:, 0:HALF]),
                                                       (straight["q"][:, :, HALF:HD], cos, norm_q[:, HALF:HD]))):
                        if k == 0:
                            dve.wait_ge(trig_done, 2)
                            dve.wait_ge(consts_in, 16 * 3)
                        if k == 2:
                            dve.wait_ge(trig_done, 3)
                        nc.vector.tensor_tensor(to, trig[:, :, :], w.unsqueeze(1).broadcast_to([P, NT, HALF]), ALU.mult)\
                            .then_inc(tables_q, 1)
                    dve.wait_ge(tables_q, 4)

                def emit(p, kind, before):
                    if kind == "k":
                        dve.wait_ge(tables_k, 4)
                    for j in range(PS):
                        n = p * PS + j
                        if (kind if j >= 1 else before) in ("q", "k"):
                            i = (j - 1) % 2
                            dve.wait_ge(rooted, n)
                            nc.vector.reciprocal(rstd[:, i], rms[:, i]).then_inc(rstd_done, 1)
                        lag = kind if j >= 4 else before
                        if lag in ("q", "k"):
                            m, t = n - 4, (j - 4) % NT
                            dve.wait_ge(flipped, m + 1)
                            g, s2 = t // QUARTER, (p * 2 + (j - 4) // NT) * 2
                            if t % QUARTER == 0:
                                at_least(dve, stored[g % 2], 16 * (s2 + g // 2))
                            to = stage[:, g % 2, (t % QUARTER) * SLICE:(t % QUARTER + 1) * SLICE]
                            nc.vector.tensor_copy(to.rearrange("p (b h s) -> p b h s", h=HS, s=S),
                                                  flip[j % 2][:, :].rearrange("p (h b s) -> p b h s", h=HS, s=S))\
                                .then_inc(staged_qk, 1)
                        if kind != "v":
                            dve.wait_ge(squared, n + 1)
                            nc.vector.tensor_reduce(sumsq[:, j % 2], squares[:, j % 2], AX.X, ALU.add).then_inc(summed, 1)
                        if before is None and j == 2:
                            query_tables()
                        if before is None and j in LATE:
                            lower(LATE[j])
                        if before is None and j == NT - 1:
                            page_rows()
                        lag = kind if j >= 2 else before
                        if lag in ("q", "k"):
                            m, i, t = n - 2, j % 2, (j - 2) % NT
                            at_least(dve, roped_done, m)
                            dve.wait_ge(drained, m + 1)
                            nc.vector.tensor_tensor(part_s[:, :, :], normed[:, i],
                                                    straight[lag][:, t].unsqueeze(1).broadcast_to([P, HS, HD]),
                                                    ALU.mult).then_inc(straight_done, 1)
                            dve.wait_ge(straight_done, m + 1)
                            dve.wait_ge(crossed_done, m + 1)
                            at_least(dve, flipped, m - 1)
                            nc.vector.tensor_tensor(roped[:, i], part_s[:, :, :], part_c[:, i], ALU.add)\
                                .then_inc(roped_done, 1)

                over_pairs(dve, emit)

            @block.tensor
            def _(pe):
                pe.wait_ge(ident_done, 2)

                def emit(p, kind, before):
                    for j in range(PS):
                        n = p * PS + j
                        par, t = j // NT, j % NT
                        if t == 0:
                            pe.wait_ge(w_split, DC * (p * 2 + par) + DC)
                        if isinstance(p, int) and p == 0 and par == 0 and t in dict(PIECES):
                            k = [lo for lo, _ in PIECES].index(t)
                            pe.wait_ge(x_split, k + 1)
                        if kind == "v":
                            if j < MM_BANKS:
                                pe.wait_ge(drained, n - MM_BANKS + 1)
                            else:
                                pe.wait_ge(staged_v, j - MM_BANKS + 1)
                        else:
                            at_least(pe, drained, n - MM_BANKS + 1)
                        bank = acc[j % MM_BANKS][:, :]
                        for c in range(DC):
                            toks = slice(t * P, (t + 1) * P)
                            pe.matmul(bank, x_hi[:, c, toks], w_hi[:, par, c], start=c == 0, stop=False)
                            pe.matmul(bank, x_hi[:, c, toks], w_lo[:, par, c], start=False, stop=False)
                            last = pe.matmul(bank, x_lo[:, c, toks], w_hi[:, par, c], start=False, stop=c == DC - 1)
                        last.then_inc(mm_done, 1)
                        lag = kind if j >= 3 else before
                        if lag in ("q", "k"):
                            m, i = n - 3, (j - 3) % 2
                            pe.wait_ge(roped_done, m + 1)
                            at_least(pe, staged_qk, m - 1)
                            for h in range(HS):
                                last = pe.transpose(flip[i][:, h * P:(h + 1) * P], roped[:, i, h], ident[:, :])
                            last.then_inc(flipped, 1)

                over_pairs(pe, emit)


def attend(nc, sem, ident, seq_f, pages, page_row, in_page_i, key_index, q_t, k_t, v_c, qk_in, v_in, v_named, wo_early,
           wo_in, stored, o_stored, loads, wo_t, v_dram, o_dram):
    UNITS = 2 * HK
    PAIRS = B // 2
    CUT = 9 * PSIZE
    BANK = 512

    with ExitStack() as ctx:
        def sb(name, shape, dt=F32):
            return ctx.enter_context(nc.sbuf_tensor(name, shape, dt))

        def ps(name, shape):
            return ctx.enter_context(nc.psum_tensor(name, shape, F32))

        q_hi = sb("q_hi", [P, HK, ROWS], F32R)
        q_lo = sb("q_lo", [P, HK, ROWS], F32R)
        k_hi = sb("k_hi", [P, HK, KEYS], F32R)
        k_lo = sb("k_lo", [P, HK, KEYS], F32R)
        v_own = sb("v_own", [2 * S, 2, HK // 2 * HD])
        past = sb("past", [P, L])
        mask = sb("mask", [P, 2, S + KEYS])
        probs = sb("probs", [P, 2, 2 * KEYS])
        neg_max = sb("neg_max", [P, 2])
        row_sum = sb("row_sum", [P, 2])
        inv_sum = sb("inv_sum", [P, 2])
        p_t = sb("p_t", [P, 2, KC, ROWS])
        p_t_own = sb("p_t_own", [2 * S, 2, ROWS])
        o_t = nc.alloc_sbuf_tensor_at("o_t", [P, 2, HK, ROWS], F32, offset=o_start(nc))
        s_bank = ps("s_bank", [P, 2 * BANK])
        s_run = s_bank[:, BANK - CUT:BANK - CUT + KEYS]
        pt_a = [ps(f"pt_a{i}", [P, BANK]) for i in range(2)]
        pt_b = [ps(f"pt_b{i}", [P, BANK]) for i in range(2)]
        o_banks = [ps(f"o_bank{i}", [P, BANK]) for i in range(2)]

        def run(j):
            return probs[:, j // 2 % 2, j % 2 * KEYS:(j % 2 + 1) * KEYS]

        def of_head(g):
            return slice(1, SLOTS) if g % 2 == 0 else slice(0, SLOTS - 1)

        assert nc.sbuf_base <= o_start(nc)
        load_keys, load_queries, name_values, gather_values = loads
        v_own_in = [sem("v_own_in0"), sem("v_own_in1")]
        q_hi_done, q_split = sem("q_hi_done"), sem("q_split")
        k_hi_done, k_split = sem("k_hi_done"), sem("k_split")
        past_done = sem("past_done")
        own_unmasked = sem("own_unmasked")
        scored = sem("scored")
        masked_in = sem("mask_built")
        masked = sem("masked")
        weighed = sem("weighed")
        inverted = sem("inverted")
        normed = sem("weights_normed")
        turned = sem("weights_turned")
        pt_a_out = sem("pt_a_out")
        pt_b_out = sem("pt_b_out")
        summed = sem("values_summed")
        o_out = sem("o_out")
        QK_DMAS = 3 + NPP
        PT_B = 3 * UNITS // 2
        QH = 2
        QP = HK // QH
        WO_WITH = [range(0, 0), range(0, 2 * HS, HS), range(2 * HS, 4 * HS, HS), range(4 * HS, WO_EARLY, HS)]
        GATHER_AT = 2

        def over_pairs(engine, emit, tail):
            emit(0, True, False)
            with engine.Fori(1, PAIRS - 1) as p:
                emit(p, False, False)
            emit(PAIRS - 1, False, True)
            tail(PAIRS)

        with nc.Block() as block:

            @block.sync
            def _(sp):
                def load_v_own(b, par):
                    at_least(sp, summed, (b - 1) * HK)
                    src = v_dram[bass.ds(b * S, S), :].rearrange("s (g e d) -> s e g d", e=2, d=HD)
                    for e in range(2):
                        sp.dma_start(v_own[e * S:(e + 1) * S, par].rearrange("s (g d) -> s g d", d=HD), src[:, e])\
                            .then_inc(v_own_in[par], 16)

                def store(b, par):
                    sp.wait_ge(o_out, b * HK + HK)
                    sp.dma_start(o_dram[bass.ds(b, 1)].rearrange("b d n -> (b d) n"),
                                 o_t[:, par].rearrange("p g n -> p (g n)")).then_inc(o_stored[par], 16)

                def emit(p):
                    for par in range(2):
                        b = p * 2 + par
                        early = isinstance(b, int)
                        if not (early and b < 2):
                            sp.wait_ge(k_split, (b - 1) * HK)
                            load_keys(sp, b, par)
                            sp.wait_ge(q_split, (b - 1) * QP)
                            load_queries(sp, b, par)
                        if not (early and b < 1):
                            load_v_own(b - 1, 1 - par)
                        if early:
                            for h in WO_WITH[b]:
                                sp.dma_start(wo_early[:, h:h + HS], wo_t[:, h:h + HS, :]).then_inc(wo_in, 16)
                        if not (early and b < 3):
                            store(b - 3, 1 - par)

                for i in range(2):
                    sp.wait_ge(stored[i], 16 * NSL * (NT // QUARTER) // 2)
                emit(0)
                emit(1)
                with sp.Fori(2, PAIRS) as p:
                    emit(p)
                load_v_own(B - 1, 1)
                for b in range(B - 3, B):
                    store(b, b % 2)
            @block.gpsimd
            def _(pool):
                def emit(p):
                    for j in range(UNITS):
                        par, g = j // HK, j % HK
                        b = p * 2 + par
                        early = isinstance(b, int)
                        if g == GATHER_AT:
                            if not (early and b < 2):
                                pool.wait_ge(summed, (b - 1) * HK)
                                name_values(b, par)
                            at_least(pool, masked_in, b)
                            if not (early and b < 2):
                                pool.wait_ge(v_named, b + 1)
                            nc.gpsimd.tensor_sub(past[:, :], key_index[:, :],
                                                 seq_f[:, bass.ds(b, 1)].broadcast_to([P, L])).then_inc(past_done, 1)
                            if not (early and b < 2):
                                gather_values(pool, par)
                        pool.wait_ge(k_hi_done, p * UNITS + j + 1)
                        nc.gpsimd.tensor_sub(k_lo[:, g].rearrange("p (s t) -> p s t", t=PSIZE), k_t[:, par, of_head(g), g],
                                             k_hi[:, g].bitcast(F32).rearrange("p (s t) -> p s t", t=PSIZE))\
                            .then_inc(k_split, 1)

                emit(0)
                with pool.Fori(1, PAIRS) as p:
                    emit(p)

            @block.scalar
            def _(act):
                def pt_evacuate(n, i, pair):
                    act.wait_ge(turned, n + 1)
                    at_least(act, summed, n - 1)
                    nc.scalar.activation(p_t[:, i, 2:4].rearrange("p c n -> p (c n)"), pt_b[i][:, 0:2 * ROWS], ACT.Copy)\
                        .then_inc(pt_b_out, 1)
                    if i:
                        nc.scalar.activation(p_t_own[:, pair], pt_b[i][0:2 * S, 2 * ROWS:3 * ROWS], ACT.Copy).then_inc(pt_b_out, 1)

                def o_evacuate(n, p, j):
                    par, g = (j // HK) % 2, j % HK
                    act.wait_ge(summed, n + 1)
                    if g == 0:
                        at_least(act, o_stored[par], p * 16)
                    nc.scalar.activation(o_t[:, par, g], o_banks[j % 2][:, 0:ROWS], ACT.Copy).then_inc(o_out, 1)

                def split_keys(b, k, par, g):
                    if g == 0:
                        act.wait_ge(qk_in[par], 16 * QK_DMAS * (k + 1))
                    nc.scalar.activation(k_hi[:, g].rearrange("p (s t) -> p s t", t=PSIZE), k_t[:, par, of_head(g), g], ACT.Copy)\
                        .then_inc(k_hi_done, 1)

                def split_queries(par, h):
                    heads = slice(h * QH, h * QH + QH)
                    nc.scalar.activation(q_hi[:, heads], q_t[:, par, heads], ACT.Copy).then_inc(q_hi_done, 1)

                def emit(p, first, last):
                    if first:
                        for g in range(HK):
                            split_keys(0, 0, 0, g)
                            if g == 0:
                                for h in range(QP):
                                    split_queries(0, h)
                    for j in range(UNITS):
                        n = p * UNITS + j
                        if not (first and j < 2):
                            pt_evacuate(n - 2, j % 2, (j - 2) // 2 % 2)
                        if not (first and j < 4):
                            o_evacuate(n - 4, p if j >= 4 else p - 1, (j - 4) % UNITS)
                        par, g = (j - 1) // HK % 2, (j - 1) % HK
                        if not (first and j == 0) and not (last and j > HK):
                            split_keys(p * 2 + (j - 1) // HK + 1, p + (j - 1) // HK, 1 - par, g)
                            if g % QH == QH - 1:
                                split_queries(1 - par, g // QH)
                        act.wait_ge(masked, n + 1)
                        nc.scalar.activation(run(j), run(j), ACT.Exp, scale=-1.0,
                                             bias=neg_max[:, j % 2:j % 2 + 1],
                                             accum_out=row_sum[:, j % 2:j % 2 + 1]).then_inc(weighed, 1)
                def tail(p):
                    n = p * UNITS
                    for j in range(4):
                        if j < 2:
                            pt_evacuate(n + j - 2, j % 2, 1)
                        o_evacuate(n + j - 4, p - 1, (j - 4) % UNITS)

                over_pairs(act, emit, tail)

            @block.vector
            def _(dve):
                def pt_evacuate(n, i):
                    dve.wait_ge(turned, n + 1)
                    at_least(dve, summed, n - 1)
                    nc.vector.tensor_copy(p_t[:, i, 0:2].rearrange("p c n -> p (c n)"), pt_a[i][:, 0:2 * ROWS])\
                        .then_inc(pt_a_out, 1)

                def invert(n, i):
                    dve.wait_ge(weighed, n + 1)
                    nc.vector.reciprocal(inv_sum[:, i:i + 1], row_sum[:, i:i + 1]).then_inc(inverted, 1)

                def normalise(j):
                    nc.vector.tensor_scalar(run(j), run(j), inv_sum[:, j % 2:j % 2 + 1], None, ALU.mult)\
                        .then_inc(normed, 1)

                def split_queries(b, par, h):
                    heads = slice(h * QH, h * QH + QH)
                    dve.wait_ge(q_hi_done, b * QP + h + 1)
                    nc.vector.tensor_tensor(q_lo[:, heads], q_t[:, par, heads], q_hi[:, heads].bitcast(F32), ALU.subtract)\
                        .then_inc(q_split, 1)

                def emit(p, first, last):
                    if first:
                        for own in (slice(0, S), slice(S + L, S + KEYS)):
                            nc.vector.memset(mask[:, :, own], 0.0).then_inc(own_unmasked, 1)
                        dve.wait_ge(own_unmasked, 2)
                        for h in range(QP):
                            split_queries(0, 0, h)
                    for j in range(UNITS):
                        n = p * UNITS + j
                        par, g, i = j // HK, j % HK, j % 2
                        if not (first and j < 2):
                            pt_evacuate(n - 2, i)
                        if g == 0:
                            b = p * 2 + par
                            dve.wait_ge(past_done, b + 1)
                            nc.vector.tensor_scalar(mask[:, par, S:S + L], past[:, :], 0.0, NEG, ALU.is_ge, ALU.mult)\
                                .then_inc(masked_in, 1)
                            dve.wait_ge(masked_in, b + 1)
                        if not (first and j < 1):
                            invert(n - 1, 1 - i)
                            dve.wait_ge(inverted, n)
                            dve.wait_ge(scored, n + 1)
                            normalise((j - 1) % UNITS)
                        else:
                            dve.wait_ge(scored, n + 1)
                        unmasked = S if g % 2 == 0 else 0
                        nc.vector.tensor_tensor_reduce(out=run(j), in0=s_run, in1=mask[:, par, unmasked:unmasked + KEYS],
                                                       scale=-SCALE, scalar=3.0e38, op0=ALU.add, op1=ALU.min,
                                                       accum_out=neg_max[:, i:i + 1]).then_inc(masked, 1)
                        if j % QH == 1 and not (first and j == 1) and not (last and j > HK + 1):
                            k, h = (j - QH) // HK + 1, (j - QH) % HK // QH
                            split_queries(p * 2 + k, k % 2, h)

                def tail(p):
                    n = p * UNITS
                    pt_evacuate(n - 2, 0)
                    invert(n - 1, 1)
                    dve.wait_ge(inverted, n)
                    normalise(UNITS - 1)
                    pt_evacuate(n - 1, 1)

                over_pairs(dve, emit, tail)

            @block.tensor
            def _(pe):
                def score(n, p, j):
                    par, g, i = j // HK, j % HK, j % 2
                    if g % QH == 0:
                        pe.wait_ge(q_split, (p * 2 + par) * QP + g // QH + 1)
                    pe.wait_ge(k_split, n + 1)
                    at_least(pe, masked, n)
                    for bank, keys in ((slice(BANK - CUT, BANK), slice(0, CUT)),
                                       (slice(BANK, BANK - CUT + KEYS), slice(CUT, KEYS))):
                        for k, (q, kk) in enumerate(((q_hi, k_hi), (q_hi, k_lo), (q_lo, k_hi))):
                            last = pe.matmul(s_bank[:, bank], q[:, g], kk[:, g, keys], start=k == 0, stop=k == 2)
                    last.then_inc(scored, 1)

                def weigh_values(n, p, j, before):
                    par, g, i = (j // HK) % 2, j % HK, j % 2
                    if g == 0:
                        pe.wait_ge(v_in[par], 16 * KC * (p + 1))
                        pe.wait_ge(v_own_in[par], 32 * (p + 1))
                    at_least(pe, o_out, n - 1)
                    pe.wait_ge(pt_a_out, n + 1)
                    pairs = before + 3 * (j // 2)
                    o_bank = o_banks[i][:, 0:ROWS]
                    for c in range(KC):
                        if c == 2:
                            pe.wait_ge(pt_b_out, pairs + 1 + j % 2)
                        pe.matmul(o_bank, v_c[:, par, c, g * HD:(g + 1) * HD], p_t[:, i, c], start=c == 0, stop=False)
                    pe.wait_ge(pt_b_out, pairs + 3)
                    own = slice(j % 2 * S, (j % 2 + 1) * S)
                    pe.matmul(o_bank, v_own[own, par, g // 2 * HD:(g // 2 + 1) * HD], p_t_own[own, j // 2 % 2],
                              start=False, stop=True).then_inc(summed, 1)

                def turn(n, j, before):
                    i, pair = j % 2, j // 2 % 2
                    at_least(pe, pt_a_out, n - 1)
                    at_least(pe, pt_b_out, before + 3 * (j // 2 - 1) + 1 + 2 * i)
                    pe.wait_ge(normed, n + 1)
                    for c in range(KC):
                        start = i * (KEYS + S) + c * P
                        last = pe.transpose((pt_a, pt_b)[c // 2][i][:, (c % 2) * ROWS:(c % 2 + 1) * ROWS],
                                            probs[:, pair, start:start + P], ident[:, :])
                    if i:
                        last = pe.transpose(pt_b[i][0:2 * S, 2 * ROWS:3 * ROWS], probs[:, pair, L:L + 2 * S], ident[:, :])
                    last.then_inc(turned, 1)

                def emit(p, first, last):
                    for j in range(UNITS):
                        n = p * UNITS + j
                        score(n, p, j)
                        if not (first and j < 3):
                            weigh_values(n - 3, p if j >= 3 else p - 1, (j - 3) % UNITS,
                                         p * PT_B if j >= 3 else (p - 1) * PT_B)
                        if not (first and j < 1):
                            turn(n - 1, (j - 1) % UNITS, p * PT_B if j >= 1 else (p - 1) * PT_B)

                def tail(p):
                    n, before = p * UNITS, (p - 1) * PT_B
                    weigh_values(n - 3, p - 1, UNITS - 3, before)
                    turn(n - 1, UNITS - 1, before)
                    weigh_values(n - 2, p - 1, UNITS - 2, before)
                    weigh_values(n - 1, p - 1, UNITS - 1, before)

                over_pairs(pe, emit, tail)


def finish(nc, sem, ident, wo_early, wo_start, wo_in, o_stored, o_dram, x_rows, wo_t, lang, slot2, slot3, w1_t, wr_a_t, b1_rows, w2_t, bias2,
           a2_rows, b2_rows, b3_rows, a3_rows, out):
    CH = 8
    NCH = HQ // CH
    ER = E * R1
    LOWS = TB * R2
    GATE_STEPS = 10
    assert R2 == R3

    with ExitStack() as ctx:
        def sb(name, shape, dt=F32):
            return ctx.enter_context(nc.sbuf_tensor(name, shape, dt))

        def ps(name, shape):
            return ctx.enter_context(nc.psum_tensor(name, shape, F32))

        wo_hi = sb("wo_hi", [P, HQ, D], F32R)
        late_start = nc.sbuf_base
        wo_late = sb("wo_late", [P, HQ - WO_EARLY, D])
        lo_early = nc.alloc_sbuf_tensor_at("lo_early", [P, WO_EARLY, D], F32R, offset=wo_start)
        lo_late = nc.alloc_sbuf_tensor_at("lo_late", [P, HQ - WO_EARLY, D], F32R, offset=late_start)
        raw = sb("raw", [P, NCH, TB * CH * S])
        o_hi = sb("o_hi", [P, 2, CH, P], F32R)
        o_lo = sb("o_lo", [P, 2, CH, P], F32R)
        w1 = nc.alloc_sbuf_tensor_at("w1", [P, DC, D], F32, offset=o_start(nc))
        wr_a = sb("wr_a", [P, DC, E + ER])
        b1 = sb("b1", [ER, D])
        w2 = sb("w2", [P, DC, D])
        bias = sb("bias", [P, D])
        x_in = sb("x_in", [P, D])
        x1 = sb("x1", [P, D])
        x2 = sb("x2", [P, D])
        x2_bias = sb("x2_bias", [P, D])
        x3 = sb("x3", [P, D])
        x4 = sb("x4", [P, D])
        x_t = sb("x_t", [P, DC, P])
        low = sb("low", [P, ER])
        low_t = sb("low_t", [ER, P])
        down2 = sb("down2", [P, TB, DC, R2])
        up2 = sb("up2", [LOWS, D])
        down3 = sb("down3", [P, TB, DC, R3])
        up3 = sb("up3", [LOWS, D])
        own2 = sb("own2", [P, TB, R2])
        own3 = sb("own3", [P, TB, R3])
        lang_i = sb("lang_i", [P, NT], I32)
        lang_f = sb("lang_f", [P, NT])
        expert_i = sb("expert_i", [P, E], I32)
        expert = sb("expert", [P, E])
        slots = sb("slots", [1, NT, 2, TB], I32)
        logits = sb("logits", [P, E])
        lang_bias = sb("lang_bias", [P, E])
        highest = sb("highest", [P, 1])
        top = sb("top", [P, E])
        top_i = sb("top_i", [P, E], U32)
        top_f = sb("top_f", [P, E])
        gap = sb("gap", [P, 1])
        ratio = sb("ratio", [P, 1])
        denom = sb("denom", [P, 1])
        gate = sb("gate", [P, 2])
        gates1 = sb("gates1", [P, E])
        gates = sb("gates", [P, E])

        assert nc.sbuf_base <= o_start(nc)
        proj = ps("proj", [P, D])
        turn = ps("turn", [P, D])
        wide = ps("wide", [P, D])
        slim = ps("slim", [P, D])

        slots_in, lang_in, w_small_in = sem("slots_in"), sem("lang_in"), sem("w_small_in")
        raw_in = [sem(f"raw_in{i}") for i in range(NCH)]
        x_rows_in = sem("x_rows_in")
        own_set, expert_set, lang_set = sem("own_set"), sem("expert_set"), sem("lang_set")
        wo_hi_done, wo_split, wo_split_pool = sem("wo_hi_done"), sem("wo_split"), sem("wo_split_pool")
        o_hi_done, o_split = sem("o_hi_done"), sem("o_split")
        chunk_done = sem("chunk_done")
        x1_done, x2_done, x2b_done, x3_done, x4_done = (sem(f"x{i}_done") for i in ("1", "2", "2b", "3", "4"))
        x_turned, xt_out = sem("x_turned"), sem("xt_out")
        slim_done, low_done, low_turned, low_out = sem("slim_done"), sem("low_done"), sem("low_turned"), sem("low_out")
        wide_done = sem("wide_done")
        gate_step, gap_done, ratio_done, gates_done = sem("gate_step"), sem("gap_done"), sem("ratio_done"), sem("gates_done")
        down_in, up_in = [sem("down2_in"), sem("down3_in")], [sem("up2_in"), sem("up3_in")]
        out_stored = sem("out_stored")
        LAYERS = 3
        WO_PIECE = 2
        WO_PIECES = HQ // WO_PIECE
        POOL_EVERY = 4

        def of_heads(early, late, h0, h1):
            return early[:, h0:h1] if h1 <= WO_EARLY else late[:, h0 - WO_EARLY:h1 - WO_EARLY]

        def wo_raw(k):
            return of_heads(wo_early, wo_late, k * WO_PIECE, (k + 1) * WO_PIECE)

        def wo_lower(k):
            h0, h1 = k * WO_PIECE, (k + 1) * WO_PIECE
            return of_heads(lo_early, lo_late, h0, h1), wo_raw(k), wo_hi[:, h0:h1].bitcast(F32)

        with nc.Block() as block:

            @block.sync
            def _(sp):
                def load_chunk(t, c):
                    if not (isinstance(t, int) and t == 0):
                        sp.wait_ge(o_split, (t - 1) * NCH + c + 1)
                    src = o_dram[bass.ds(t * TB, TB), :, c * CH * S:(c + 1) * CH * S]
                    sp.dma_start(raw[:, c].rearrange("p (b n) -> p b n", b=TB), src.rearrange("b d n -> d b n"))\
                        .then_inc(raw_in[c], 16)

                def load_x(t):
                    sp.dma_start(x_in[:, :], x_rows[bass.ds(t * P, P), :]).then_inc(x_rows_in, 16)

                def gather(t, i, wait):
                    rows_d, rows_u = (a2_rows, b3_rows)[i], (b2_rows, a3_rows)[i]
                    down, up = (down2, down3)[i], (up2, up3)[i]
                    _, slot = nc.values_load_multi_w_load_instructions(
                        slots[0:1, bass.ds(t, 1), i].rearrange("o t a -> o (t a)"), engines=[mybir.EngineType.SP],
                        min_val=0, max_val=rows_d.shape[0] - 1, skip_runtime_bounds_check_because="slots name adapters")
                    if wait:
                        sp.wait_ge(wide_done, (t - 1) * LAYERS + 2 + i)
                    for a in range(TB):
                        sp.dma_start(down[:, a].rearrange("p c r -> p (c r)"),
                                     rows_d[bass.ds(slot[a], 1)].rearrange("s p n -> (s p) n")).then_inc(down_in[i], 16)
                        sp.dma_start(up[R2 * a:R2 * (a + 1), :],
                                     rows_u[bass.ds(slot[a], 1)].rearrange("s r n -> (s r) n")).then_inc(up_in[i], 16)

                def store(t):
                    sp.wait_ge(x4_done, t + 1)
                    sp.dma_start(out[bass.ds(t * P, P), :], x4[:, :]).then_inc(out_stored, 16)

                for par in range(2):
                    sp.wait_ge(o_stored[par], 16 * (B // 2 - 2))
                for c in range(NCH):
                    load_chunk(0, c)
                sp.dma_start(wo_late[:, :, :], wo_t[:, WO_EARLY:HQ, :]).then_inc(wo_in, 16)
                for i, ids in enumerate((slot2, slot3)):
                    sp.dma_start(slots[0:1, :, i], ids.rearrange("(o t a) -> o t a", o=1, a=TB)).then_inc(slots_in, 16)
                for a in range(TB):
                    sp.dma_start(lang_i[S * a:S * (a + 1), :], lang[a::TB].partition_broadcast(S),
                                 allow_slow_non_contiguous=True).then_inc(lang_in, 16)
                load_x(0)
                load_chunk(1, 0)
                sp.dma_start(wr_a[:, :, :], wr_a_t).then_inc(w_small_in, 16)
                sp.dma_start(b1[:, :], b1_rows).then_inc(w_small_in, 16)
                sp.dma_start(w2[:, :, :], w2_t).then_inc(w_small_in, 16)
                sp.dma_start(bias[:, :], bias2.partition_broadcast(P)).then_inc(w_small_in, 16)
                sp.wait_ge(slots_in, 16 * 2)
                gather(0, 0, False)
                gather(0, 1, False)
                for c in range(1, NCH):
                    load_chunk(1, c)
                for par in range(2):
                    sp.wait_ge(o_stored[par], 16 * (B // 2))
                sp.dma_start(w1[:, :, :], w1_t).then_inc(w_small_in, 16)

                def follow(t, ahead):
                    sp.wait_ge(x1_done, t + 1)
                    load_x(t + 1)
                    if ahead:
                        load_chunk(t + 2, 0)
                        load_chunk(t + 2, 1)
                    gather(t + 1, 0, True)
                    if ahead:
                        load_chunk(t + 2, 2)
                        load_chunk(t + 2, 3)
                    gather(t + 1, 1, True)
                    store(t)

                with sp.Fori(0, NT - 2) as t:
                    follow(t, True)
                follow(NT - 2, False)
                store(NT - 1)
                sp.wait_ge(out_stored, 16 * NT)

            @block.gpsimd
            def _(pool):
                nc.gpsimd.iota(expert_i[:, :], [[1, E]], base=0, channel_multiplier=0).then_inc(expert_set, 1)
                for own in (own2, own3):
                    nc.gpsimd.memset(own[:, :, :], 0.0).then_inc(own_set, 1)
                pool.wait_ge(own_set, 2)
                for own, scale in ((own2, LORA_SCALING), (own3, 1.0)):
                    for a in range(TB):
                        nc.gpsimd.memset(own[S * a:S * (a + 1), a, :], scale).then_inc(own_set, 1)

                pool.wait_ge(own_set, 2 + 2 * TB)
                for k in range(POOL_EVERY - 1, WO_PIECES, POOL_EVERY):
                    pool.wait_ge(wo_hi_done, k + 1)
                    low_half, whole_piece, high_half = wo_lower(k)
                    nc.gpsimd.tensor_sub(low_half, whole_piece, high_half).then_inc(wo_split_pool, 1)

                def add_bias(t):
                    pool.wait_ge(x2_done, t + 1)
                    nc.gpsimd.tensor_add(x2_bias[:, :], x2[:, :], bias[:, :]).then_inc(x2b_done, 1)

                pool.wait_ge(w_small_in, 16 * 5)
                with pool.Fori(0, NT) as t:
                    add_bias(t)

            @block.scalar
            def _(act):
                def upper(t, c):
                    k = t * NCH + c
                    act.wait_ge(raw_in[c], 16 * t + 16)
                    at_least(act, chunk_done, k - 1)
                    nc.scalar.activation(o_hi[:, c % 2].rearrange("p h (b s) -> p b h s", s=S),
                                         raw[:, c].rearrange("p (b h s) -> p b h s", b=TB, s=S), ACT.Copy)\
                        .then_inc(o_hi_done, 1)

                def x_turn_out(t, layer):
                    act.wait_ge(x_turned, t * LAYERS + layer + 1)
                    nc.scalar.activation(x_t[:, :, :].rearrange("p c n -> p (c n)"), turn[:, :], ACT.Copy).then_inc(xt_out, 1)

                def low_turn_out(t, layer):
                    rows = ER if layer == 0 else LOWS
                    act.wait_ge(low_turned, t * LAYERS + layer + 1)
                    nc.scalar.activation(low_t[0:rows, :], turn[0:rows, 0:P], ACT.Copy).then_inc(low_out, 1)

                def chain(t, ahead, beyond):
                    if ahead:
                        upper(t + 1, 1)
                    x_turn_out(t, 0)
                    act.wait_ge(gap_done, t + 1)
                    nc.scalar.activation(ratio[:, :], gap[:, :], ACT.Exp).then_inc(ratio_done, 1)
                    low_turn_out(t, 0)
                    if ahead:
                        upper(t + 1, 2)
                    x_turn_out(t, 1)
                    low_turn_out(t, 1)
                    if ahead:
                        upper(t + 1, 3)
                    x_turn_out(t, 2)
                    low_turn_out(t, 2)
                    if beyond:
                        upper(t + 2, 0)

                act.wait_ge(wo_in, 16 * (WO_EARLY // HS))
                for k in range(WO_PIECES):
                    if k * WO_PIECE == WO_EARLY:
                        act.wait_ge(wo_in, 16 * (WO_EARLY // HS + 1))
                    nc.scalar.activation(wo_hi[:, k * WO_PIECE:(k + 1) * WO_PIECE], wo_raw(k), ACT.Copy)\
                        .then_inc(wo_hi_done, 1)
                    if k % NCH == 1:
                        upper(0, k // NCH)
                upper(1, 0)
                with act.Fori(0, NT - 2) as t:
                    chain(t, True, True)
                chain(NT - 2, True, False)
                chain(NT - 1, False, False)

            @block.vector
            def _(dve):
                def lower(t, c):
                    k = t * NCH + c
                    dve.wait_ge(o_hi_done, k + 1)
                    nc.vector.tensor_tensor(o_lo[:, c % 2].rearrange("p h (b s) -> p b h s", s=S),
                                            raw[:, c].rearrange("p (b h s) -> p b h s", b=TB, s=S),
                                            o_hi[:, c % 2].bitcast(F32).rearrange("p h (b s) -> p b h s", s=S),
                                            ALU.subtract).then_inc(o_split, 1)

                def chain(t, ahead, beyond):
                    links = [0]

                    def link(ins):
                        links[0] += 1
                        ins.then_inc(gate_step, 1)
                        dve.wait_ge(gate_step, t * GATE_STEPS + links[0])

                    dve.wait_ge(chunk_done, t * NCH + NCH)
                    dve.wait_ge(x_rows_in, t * 16 + 16)
                    nc.vector.tensor_tensor(x1[:, :], proj[:, :], x_in[:, :], ALU.add).then_inc(x1_done, 1)
                    if ahead:
                        lower(t + 1, 1)
                    link(nc.vector.tensor_scalar(lang_bias[:, :], expert[:, :], lang_f[:, bass.ds(t, 1)], LANG_BIAS,
                                                 ALU.is_equal, ALU.mult))
                    dve.wait_ge(slim_done, t * LAYERS + 1)
                    link(nc.vector.tensor_tensor(logits[:, :], slim[:, 0:E], lang_bias[:, :], ALU.add))
                    nc.vector.tensor_reduce(highest[:, :], logits[:, :], AX.X, ALU.max)
                    link(nc.vector.max(top[:, :], logits[:, :]))
                    nc.vector.tensor_tensor(gap[:, :], top[:, 1:2], highest[:, :], ALU.subtract).then_inc(gap_done, 1)
                    link(nc.vector.max_index(top_i[:, :], top[:, :], logits[:, :]))
                    link(nc.vector.tensor_copy(top_f[:, :], top_i[:, :]))
                    dve.wait_ge(ratio_done, t + 1)
                    link(nc.vector.tensor_scalar(denom[:, :], ratio[:, :], 1.0, 1.0 / MOE_SCALING, ALU.add, ALU.mult))
                    link(nc.vector.reciprocal(gate[:, 0:1], denom[:, :]))
                    link(nc.vector.tensor_tensor(gate[:, 1:2], gate[:, 0:1], ratio[:, :], ALU.mult))
                    link(nc.vector.tensor_scalar(gates1[:, :], expert[:, :], top_f[:, 0:1], gate[:, 0:1], ALU.is_equal, ALU.mult))
                    link(nc.vector.tensor_scalar(gates[:, :], expert[:, :], top_f[:, 1:2], gate[:, 1:2], ALU.is_equal, ALU.mult))
                    assert links[0] == GATE_STEPS
                    nc.vector.tensor_tensor(gates[:, :], gates[:, :], gates1[:, :], ALU.add).then_inc(gates_done, 1)
                    dve.wait_ge(gates_done, t + 1)
                    nc.vector.tensor_tensor(low[:, :].rearrange("p (e r) -> p e r", r=R1),
                                            slim[:, E:E + ER].rearrange("p (e r) -> p e r", r=R1),
                                            gates[:, :].unsqueeze(2).broadcast_to([P, E, R1]), ALU.mult).then_inc(low_done, 1)
                    if ahead:
                        lower(t + 1, 2)
                    dve.wait_ge(wide_done, t * LAYERS + 1)
                    nc.vector.tensor_tensor(x2[:, :], wide[:, :], x1[:, :], ALU.add).then_inc(x2_done, 1)
                    dve.wait_ge(slim_done, t * LAYERS + 2)
                    nc.vector.tensor_tensor(low[:, 0:LOWS], slim[:, 0:LOWS], own2[:, :, :].rearrange("p a r -> p (a r)"),
                                            ALU.mult).then_inc(low_done, 1)
                    if ahead:
                        lower(t + 1, 3)
                    dve.wait_ge(wide_done, t * LAYERS + 2)
                    dve.wait_ge(x2b_done, t + 1)
                    nc.vector.tensor_tensor(x3[:, :], wide[:, :], x2_bias[:, :], ALU.add).then_inc(x3_done, 1)
                    dve.wait_ge(slim_done, t * LAYERS + 3)
                    nc.vector.tensor_tensor(low[:, 0:LOWS], slim[:, 0:LOWS], own3[:, :, :].rearrange("p a r -> p (a r)"),
                                            ALU.mult).then_inc(low_done, 1)
                    if beyond:
                        lower(t + 2, 0)
                    dve.wait_ge(wide_done, t * LAYERS + 3)
                    at_least(dve, out_stored, t * 16)
                    nc.vector.tensor_tensor(x4[:, :], wide[:, :], x3[:, :], ALU.add).then_inc(x4_done, 1)

                for k in range(WO_PIECES):
                    if k % POOL_EVERY != POOL_EVERY - 1:
                        dve.wait_ge(wo_hi_done, k + 1)
                        low_half, whole_piece, high_half = wo_lower(k)
                        nc.vector.tensor_tensor(low_half, whole_piece, high_half, ALU.subtract).then_inc(wo_split, 1)
                    if k % NCH == 1:
                        lower(0, k // NCH)
                dve.wait_ge(expert_set, 1)
                dve.wait_ge(lang_in, 16 * TB)
                nc.vector.tensor_copy(expert[:, :], expert_i[:, :]).then_inc(lang_set, 1)
                nc.vector.tensor_copy(lang_f[:, :], lang_i[:, :]).then_inc(lang_set, 1)
                dve.wait_ge(lang_set, 2)
                dve.wait_ge(own_set, 2 + 2 * TB)
                lower(1, 0)
                chain(0, True, True)
                with dve.Fori(1, NT - 2) as t:
                    chain(t, True, True)
                chain(NT - 2, True, False)
                chain(NT - 1, False, False)

            @block.tensor
            def _(pe):
                def heads(t, h0, h1):
                    for h in range(h0, h1):
                        c, k = h // CH, t * NCH + h // CH
                        if h % CH == 0:
                            pe.wait_ge(o_split, k + 1)
                        if isinstance(t, int) and t == 0 and h % WO_PIECE == 0:
                            k = h // WO_PIECE
                            if k % POOL_EVERY == POOL_EVERY - 1:
                                pe.wait_ge(wo_split_pool, k // POOL_EVERY + 1)
                            else:
                                pe.wait_ge(wo_split, k - k // POOL_EVERY + 1)
                        i = h % CH
                        lower = of_heads(lo_early, lo_late, h, h + 1)[:, 0]
                        pe.matmul(proj[:, :], o_hi[:, c % 2, i], wo_hi[:, h], start=h == 0, stop=False)
                        pe.matmul(proj[:, :], o_hi[:, c % 2, i], lower, start=False, stop=False)
                        last = pe.matmul(proj[:, :], o_lo[:, c % 2, i], wo_hi[:, h], start=False, stop=h == HQ - 1)
                        if i == CH - 1:
                            last.then_inc(chunk_done, 1)

                def chain(t, ahead):
                    at = [0]

                    def fill(n):
                        if ahead:
                            heads(t + 1, at[0], at[0] + n)
                            at[0] += n

                    for layer, (x, done) in enumerate(((x1, x1_done), (x2, x2_done), (x3, x3_done))):
                        pe.wait_ge(done, t + 1)
                        for c in range(DC):
                            last = pe.transpose(turn[:, c * P:(c + 1) * P], x[:, c * P:(c + 1) * P], ident[:, :])
                        last.then_inc(x_turned, 1)
                        fill((3, 2, 2)[layer])
                        pe.wait_ge(xt_out, t * LAYERS + layer + 1)
                        if layer:
                            pe.wait_ge(down_in[layer - 1], (t + 1) * 16 * TB)
                        for c in range(DC):
                            if layer == 0:
                                last = pe.matmul(slim[:, 0:E + ER], x_t[:, c], wr_a[:, c], start=c == 0, stop=c == DC - 1)
                            else:
                                last = pe.matmul(slim[:, 0:LOWS], x_t[:, c], (down2, down3)[layer - 1][:, :, c, :],
                                                 start=c == 0, stop=c == DC - 1)
                        last.then_inc(slim_done, 1)
                        if layer < 2:
                            for c in range(DC):
                                pe.matmul(wide[:, :], x_t[:, c], (w1, w2)[layer][:, c], start=c == 0, stop=False)
                        fill((4, 3, 4)[layer])
                        rows = ER if layer == 0 else LOWS
                        pe.wait_ge(low_done, t * LAYERS + layer + 1)
                        pe.transpose(turn[:, 0:P], low[:, :], ident[:, :]).then_inc(low_turned, 1)
                        fill((3, 3, 3)[layer])
                        pe.wait_ge(low_out, t * LAYERS + layer + 1)
                        if layer:
                            pe.wait_ge(up_in[layer - 1], (t + 1) * 16 * TB)
                        pe.matmul(wide[:, :], low_t[0:rows, :], (b1, up2, up3)[layer][:, :], start=layer == 2, stop=True)\
                            .then_inc(wide_done, 1)
                        fill((2, 2, 1)[layer])
                    assert not ahead or at[0] == HQ

                heads(0, 0, HQ)
                pe.wait_ge(w_small_in, 16 * 5)
                with pe.Fori(0, NT - 1) as t:
                    chain(t, True)
                chain(NT - 1, False)


def kernel(**inputs):
    import numpy as np
    import concourse.bacc as bacc
    from concourse.bass_utils import run_bass_kernel_spmd as run

    a = {k: np.asarray(v) for k, v in inputs.items()}

    def chunked(w):
        return w.T.reshape(DC, P, -1).transpose(1, 0, 2)

    x = a["x"].reshape(TOK, D)
    w = np.concatenate([a["L0_cond_Wq"], a["L0_cond_Wk"], a["L0_cond_Wv"]])
    exponent = np.arange(0, HD, 2, dtype=np.float32) / np.float32(HD)
    arrays = {
        "x_t": chunked(x).reshape(P, DC, 4, TOK // 4).transpose(2, 0, 1, 3),
        "x_rows": x,
        "w_qkv": chunked(w).reshape(P, DC, NSL, SLICE).transpose(2, 0, 1, 3),
        "wo_t": a["L0_cond_Wo"].T.reshape(HQ, HD, D).transpose(1, 0, 2),
        "q_norm_w": a["L0_cond_q_norm_w"],
        "k_norm_w": a["L0_cond_k_norm_w"],
        "inv_freq": (np.float32(1.0) / np.float32(10000.0) ** exponent).astype(np.float32),
        "k_pages": a["L0_cond_k_cache"].transpose(0, 3, 2, 1).reshape(PAGES, HD, HK * PSIZE),
        "v_rows": a["L0_cond_v_cache"].reshape(PAGES * PSIZE, HK * HD),
        "block_table": a["itok_Bx16_0_63"].reshape(B * NPP),
        "seqlens": a["itok_B_207_1644"],
        "lang": a["itok_B_0_7"],
        "slot2": a["itok_B_0_23"],
        "slot3": a["itok_B_4_50"],
        "w1_t": chunked(a["L1_cond_W"]),
        "wr_a_t": chunked(np.concatenate([a["L1_cond_Wr"], a["L1_cond_A"].reshape(E * R1, D)])),
        "b1_rows": a["L1_cond_B"].transpose(0, 2, 1).reshape(E * R1, D),
        "w2_t": chunked(a["L2_cond_W"]),
        "bias2": a["L2_cond_b"],
        "a2_rows": a["L2_cond_lora_As"].reshape(-1, DC, P, R2).transpose(0, 2, 1, 3).reshape(-1, P, DC * R2),
        "b2_rows": a["L2_cond_lora_Bs"],
        "b3_rows": a["L3_cond_B"].reshape(-1, R3, DC, P).transpose(0, 3, 2, 1).reshape(-1, P, DC * R3),
        "a3_rows": a["L3_cond_A"].transpose(0, 2, 1),
    }
    arrays = {k: np.ascontiguousarray(v) for k, v in arrays.items()}
    nc = bacc.Bacc("TRN2", target_bir_lowering=False, num_devices=1)
    args = [nc.dram_tensor(f"in_{k}", v.shape, mybir.dt.from_np(v.dtype), kind="ExternalInput").ap()
            for k, v in arrays.items()]
    out = nc.dram_tensor("out_x", (TOK, D), F32, kind="ExternalOutput").ap()
    decoder(nc, *args, out)
    r = run(nc, [{f"in_{k}": v for k, v in arrays.items()}], core_ids=[0])
    return r.results[0]["out_x"].reshape(B, S, D)
```

```python
from contextlib import ExitStack

import numpy as np

import concourse.bass as bass
from concourse import mybir
from concourse.alu_op_type import AluOpType as ALU

ACT = mybir.ActivationFunctionType
AX = mybir.AxisListType
F32 = mybir.dt.float32
F32R = mybir.dt.float32r
I32 = mybir.dt.int32
U32 = mybir.dt.uint32

P = 128
B, S, D = 64, 32, 512
DC = D // P
TOK = B * S
TB = P // S
NT = TOK // P
HQ, HK, HD = 32, 8, 128
REP = HQ // HK
NPP, PSIZE, PAGES = 16, 32, 64
L = NPP * PSIZE
KEYS = L + S
KC = L // P
ROWS = REP * S
QUARTER = 4
SLICE = 512
NQ, NK, NV = HQ * HD // SLICE, HK * HD // SLICE, HK * HD // SLICE
NSL = NQ + NK + NV
HS = SLICE // HD
SLOTS = NPP + 2
O_BYTES = 2 * HK * ROWS * 4
WO_EARLY = 24
HALF = HD // 2
SCALE = float(HD) ** -0.5
RMS_EPS = 1e-6
NEG = -1e30
E, R1 = 8, 16
LANG_BIAS = 5.0
MOE_SCALING = 2.0
R2, LORA_SCALING = 16, 2.0
R3 = 16
ER = E * R1
LOWS = TB * R2
CH = 8
NCH = HQ // CH
TWO_PI = 6.283185307179586
TWO_PI_HI, TWO_PI_LO = 6.28125, 0.0019353071795864769
ROUND = 12582912.0
PI_IN = 3.1415925


def at_least(engine, sem, value):
    if not (isinstance(value, int) and value <= 0):
        engine.wait_ge(sem, value)


def o_start(nc):
    return (nc.sbuf_usable_end - O_BYTES) // 32 * 32


def decoder(nc, x_t, x_rows, w_qkv, wo_t, q_norm_w, k_norm_w, inv_freq, k_pages, v_rows, block_table, seqlens,
            lang, slot2, slot3, w1_t, wr_a_t, b1_rows, w2_t, bias2, a2_rows, b2_rows, b3_rows, a3_rows, out):
    with ExitStack() as whole:
        def sem(name):
            return whole.enter_context(nc.semaphore(name))

        ident = whole.enter_context(nc.sbuf_tensor("ident", [P, P], F32))
        wo_start = nc.sbuf_base
        wo_early = whole.enter_context(nc.sbuf_tensor("wo_early", [P, WO_EARLY, D], F32))
        wo_in = sem("wo_in")
        o_stored = [sem("o_stored0"), sem("o_stored1")]
        q_dram = nc.dram_tensor("q_spill", (B, HD, HQ * S), F32, kind="Internal").ap()
        k_dram = nc.dram_tensor("k_spill", (B, HD, HK * S), F32, kind="Internal").ap()
        v_dram = nc.dram_tensor("v_spill", (TOK, HK * HD), F32, kind="Internal").ap()
        o_dram = nc.dram_tensor("o_spill", (B, HD, HQ * S), F32, kind="Internal").ap()

        with ExitStack() as ctx:
            def sb(name, shape, dt=F32):
                return ctx.enter_context(nc.sbuf_tensor(name, shape, dt))

            q_start = nc.sbuf_base
            q_t = sb("q_t", [P, 2, HK, ROWS])
            k_start = nc.sbuf_base
            k_t = sb("k_t", [P, 2, SLOTS, HK, PSIZE])
            v_start = nc.sbuf_base
            v_c = sb("v_c", [P, 2, KC, HK * HD])
            v_row = sb("v_row", [P, 2, KC], I32)
            seq_f = sb("seq_f", [P, B])
            pages = sb("pages", [P, B * NPP], I32)
            page_row = sb("page_row", [P, B * KC], I32)
            in_page_i = sb("in_page_i", [P, 1], I32)
            key_index = sb("key_index", [P, L])
            tables = (seq_f, pages, page_row, in_page_i, key_index)
            qk_in = [sem("qk_in0"), sem("qk_in1")]
            v_in = [sem("v_in0"), sem("v_in1")]
            v_named = sem("v_named")

            def load_keys(sp, b, par):
                for i in (0, SLOTS - 1):
                    sp.dma_start(k_t[:, par, i].rearrange("p g n -> p (g n)"),
                                 k_dram[bass.ds(b, 1)].rearrange("b d n -> (b d) n")).then_inc(qk_in[par], 16)
                _, page = nc.values_load_multi_w_load_instructions(
                    pages[0:1, bass.ds(b * NPP, NPP)], engines=[mybir.EngineType.SP], min_val=0,
                    max_val=PAGES - 1, skip_runtime_bounds_check_because="the table names pages of the cache")
                for i in range(NPP):
                    sp.dma_start(k_t[:, par, i + 1].rearrange("p g n -> p (g n)"),
                                 k_pages[bass.ds(page[i], 1)].rearrange("b d n -> (b d) n")).then_inc(qk_in[par], 16)

            def load_queries(sp, b, par):
                sp.dma_start(q_t[:, par].rearrange("p g n -> p (g n)"),
                             q_dram[bass.ds(b, 1)].rearrange("b d n -> (b d) n")).then_inc(qk_in[par], 16)

            def name_values(b, par):
                nc.gpsimd.tensor_add(v_row[:, par], page_row[:, bass.ds(b * KC, KC)],
                                     in_page_i[:, :].broadcast_to([P, KC])).then_inc(v_named, 1)

            def gather_values(pool, par):
                for c in range(KC):
                    pool.indirect_dma_start(
                        out=v_c[:, par, c], out_offset=None, in_=v_rows[:, :],
                        in_offset=bass.IndirectOffsetOnAxis(ap=v_row[:, par, c:c + 1], axis=0)).then_inc(v_in[par], 16)

            raw = nc.alloc_sbuf_tensor_at("raw", [P, 2, TB * CH * S], F32, offset=q_start)
            place = [k_start]

            def after(name, shape, halves=""):
                at, n = place[0], int(np.prod(shape[1:])) * 4
                place[0] = at + n
                whole_one = nc.alloc_sbuf_tensor_at(name, shape, F32, offset=at)
                return (whole_one, nc.alloc_sbuf_tensor_at(halves, shape, F32R, offset=at)) if halves else whole_one

            wo_late, lo_late = after("wo_late", [P, HQ - WO_EARLY, D], "lo_late")
            w2, w2_lo = after("w2", [P, DC, D], "w2_lo")
            wr_a = after("wr_a", [P, DC, E + ER])
            b1 = after("b1", [ER, D])
            bias = after("bias", [P, D])
            x1 = after("x1", [P, D])
            up = after("up", [2 * LOWS, D])
            down2 = after("down2", [P, TB, DC, R2])
            low_t = after("low_t", [ER, P])
            assert place[0] <= v_start
            place = [v_start]
            w1, w1_lo = after("w1", [P, DC, D], "w1_lo")
            assert place[0] <= v_start + KC * HK * HD * 4
            early_bytes = place[0] - q_start
            raw_in = [sem(f"raw_in{i}") for i in range(NCH)]
            x_rows_in, w_small_in = sem("x_rows_in"), sem("w_small_in")

            def load_chunk(sp, t, c):
                src = o_dram[bass.ds(t * TB, TB), :, c * CH * S:(c + 1) * CH * S]
                sp.dma_start(raw[:, c % 2].rearrange("p (b n) -> p b n", b=TB), src.rearrange("b d n -> d b n"))\
                    .then_inc(raw_in[c], 16)

            def load_x(sp, t):
                sp.dma_start(x1[:, :], x_rows[bass.ds(t * P, P), :]).then_inc(x_rows_in, 16)

            def load_first(sp):
                for c in range(2):
                    load_chunk(sp, 0, c)
                sp.dma_start(wo_late[:, :, :], wo_t[:, WO_EARLY:HQ, :]).then_inc(wo_in, 16)
                load_x(sp, 0)
                sp.dma_start(wr_a[:, :, :], wr_a_t).then_inc(w_small_in, 16)
                sp.dma_start(b1[:, :], b1_rows).then_inc(w_small_in, 16)

            def load_weights(sp):
                sp.dma_start(w1[:, :, :], w1_t).then_inc(w_small_in, 16)
                sp.dma_start(w2[:, :, :], w2_t).then_inc(w_small_in, 16)
                sp.dma_start(bias[:, :], bias2.partition_broadcast(P)).then_inc(w_small_in, 16)

            stored = [sem("stored0"), sem("stored1")]
            loads = (load_keys, load_queries, name_values, gather_values)
            project(nc, sem, ident, *tables, q_t, k_t, v_c, v_named, wo_early, wo_start, stored, loads, x_t, w_qkv, q_norm_w, k_norm_w,
                    inv_freq, block_table, seqlens, q_dram, k_dram, v_dram)
            attend(nc, sem, ident, *tables, q_t, k_t, v_c, qk_in, v_in, v_named, wo_early, wo_in, stored, o_stored, loads, load_first,
                   load_weights, wo_t, v_dram, o_dram)
        buffers = (raw, wo_late, lo_late, w1, w1_lo, w2, w2_lo, wr_a, b1, bias, x1, up, down2, low_t)
        finish(nc, sem, ident, wo_early, wo_start, wo_in, o_stored, buffers, q_start, early_bytes, raw_in, x_rows_in,
               w_small_in, load_chunk, load_x, lang, slot2, slot3, a2_rows, b2_rows, b3_rows, a3_rows, out)


def project(nc, sem, ident, seq_f, pages, page_row, in_page_i, key_index, q_t, k_t, v_c, v_named, wo_early, wo_start, stored, loads,
            x_t, w_qkv, q_norm_w, k_norm_w, inv_freq, block_table, seqlens, q_dram, k_dram, v_dram):
    MM_BANKS = 4
    PAIRS = NSL // 2
    PS = 2 * NT

    with ExitStack() as ctx:
        def sb(name, shape, dt=F32):
            return ctx.enter_context(nc.sbuf_tensor(name, shape, dt))

        def part(buffer, start, shape, dt=F32):
            names = " ".join(f"d{i}" for i in range(len(shape) - 1))
            sizes = {f"d{i}": n for i, n in enumerate(shape[1:])}
            n = int(np.prod(shape[1:]))
            ap = buffer[:, start:start + n]
            ap = ap if dt == F32 else ap.bitcast(dt)
            return ap.rearrange(f"p ({names}) -> p {names}", **sizes)

        TRIG = NT * HALF
        k_halves = [k_t[:, i].rearrange("p s g n -> p (s g n)") for i in range(2)]
        v_flat = v_c[:, :, :, :].rearrange("p i c n -> p (i c n)")
        wo_flat = wo_early[:, :, :].rearrange("p h n -> p (h n)")
        X_RAW = 2 * DC * QUARTER * P
        x_raw = part(k_halves[0], 0, [P, 2, DC, QUARTER * P])
        freq = part(k_halves[0], X_RAW, [P, HALF])
        seq_i = part(k_halves[0], X_RAW + HALF, [P, B], I32)
        pos = part(k_halves[0], X_RAW + HALF + B, [P, NT])
        in_page = part(k_halves[0], X_RAW + HALF + B + NT, [P, 1])
        smalls = X_RAW + HALF + B + NT + 1
        eps = part(k_halves[0], smalls, [P, 1])
        sumsq, rms, rstd = (part(k_halves[0], smalls + 1 + i * 2 * HS, [P, 2, HS]) for i in range(3))
        w_raw = part(k_halves[1], 0, [P, 2, DC, SLICE])
        part_s = part(k_halves[1], 2 * DC * SLICE, [P, HS, HD])
        norm_q = part(k_halves[0], smalls + 1 + 6 * HS, [P, HD])
        norm_k = part(k_halves[0], smalls + 1 + 6 * HS + HD, [P, HD])
        tabs = [part(v_flat, i * NT * HD, [P, NT, HD]) for i in range(4)]
        straight, crossed = {"q": tabs[0], "k": tabs[1]}, {"q": tabs[2], "k": tabs[3]}
        part_c = part(q_t[:, 0].rearrange("p g n -> p (g n)"), 0, [P, 2, HS, HD])
        roped = part(q_t[:, 1].rearrange("p g n -> p (g n)"), 0, [P, 2, HS, HD])
        x_hi = nc.alloc_sbuf_tensor_at("x_hi", [P, DC, TOK], F32R, offset=wo_start)
        stage = part(wo_flat, DC * TOK, [P, 2, QUARTER * SLICE])

        x_lo = sb("x_lo", [P, DC, TOK], F32R)
        w_hi = sb("w_hi", [P, 2, DC, SLICE], F32R)
        w_lo = sb("w_lo", [P, 2, DC, SLICE], F32R)
        minus_norm = sb("minus_norm", [P, 2, HALF])
        squares = sb("squares", [P, 2, HS, HD])
        normed = sb("normed", [P, 2, HS, HD])
        stage_flat = stage.rearrange("p i n -> p (i n)")
        angle, turns, reduced = (part(stage_flat, i * TRIG, [P, NT, HALF]) for i in range(3))
        key_i = part(stage_flat, 3 * TRIG, [P, L], I32)
        cos, sin = straight["k"][:, :, HALF:HD], crossed["k"][:, :, HALF:HD]
        acc = [ctx.enter_context(nc.psum_tensor(f"acc{i}", [P, SLICE], F32)) for i in range(MM_BANKS)]
        flip = [ctx.enter_context(nc.psum_tensor(f"flip{i}", [P, SLICE], F32)) for i in range(2)]

        load_keys, load_queries, name_values, gather_values = loads
        PIECES = [(0, 1), (1, 2)] + [(t, t + 2) for t in range(2, NT, 2)]
        X_DONE = [sum(hi <= QUARTER * (q + 1) for _, hi in PIECES) for q in range(NT // QUARTER)]

        LATE = {2: 4, 4: 5, 5: 6, 7: 7, 8: 8}

        KEY_TABLES = [NT + 2, NT + 5, NT + 8, NT + 11]

        def piece(k):
            lo, hi = PIECES[k]
            q = lo // QUARTER
            return slice(lo * P, hi * P), q, slice((lo - q * QUARTER) * P, (hi - q * QUARTER) * P)

        angles_in, consts_in = sem("angles_in"), sem("consts_in")
        x_in = [sem("x_in0"), sem("x_in1")]
        w_in = [sem("w_in0"), sem("w_in1")]
        iota_done = sem("iota_done")
        ident_done = sem("ident_done")
        table_step = sem("table_step")
        angles_done = sem("angles_done")
        trig_done = sem("trig_done")
        minus_done = sem("minus_done")
        straight_q_done, crossed_q_done = sem("straight_q_done"), sem("crossed_q_done")
        tables_k = sem("tables_k")
        x_hi_done = sem("x_hi_done")
        x_split = sem("x_split")
        w_hi_done = sem("w_hi_done")
        w_split = sem("w_split")
        mm_done = sem("mm_done")
        squared = sem("squared")
        summed = sem("summed")
        rooted = sem("rooted")
        rstd_done = sem("rstd_done")
        drained = sem("drained")
        straight_done = sem("straight_done")
        crossed_done = sem("crossed_done")
        roped_done = sem("roped_done")
        flipped = sem("flipped")
        staged_qk = sem("staged_qk")
        staged_v = sem("staged_v")

        KIND = ["q"] * (NQ // 2) + ["k"] * (NK // 2) + ["v"] * (NV // 2)
        QKS = (NQ + NK) * NT

        def over_pairs(engine, emit):
            emit(0, "q", None)
            with engine.Fori(1, NQ // 2) as p:
                emit(p, "q", "q")
            for p in range(NQ // 2, PAIRS):
                emit(p, KIND[p], KIND[p - 1])

        with nc.Block() as block:

            @block.sync
            def _(sp):
                sp.dma_start(seq_i, seqlens.partition_broadcast(P)).then_inc(angles_in, 16)
                sp.dma_start(freq, inv_freq.partition_broadcast(P)).then_inc(angles_in, 16)
                sp.dma_start(w_raw[:, 0], w_qkv[0]).then_inc(w_in[0], 16)
                sp.dma_start(x_raw[:, 0], x_t[0]).then_inc(x_in[0], 16)
                sp.dma_start(norm_q, q_norm_w.partition_broadcast(P)).then_inc(consts_in, 16)
                sp.dma_start(norm_k, k_norm_w.partition_broadcast(P)).then_inc(consts_in, 16)
                sp.dma_start(pages[:, :], block_table.partition_broadcast(P)).then_inc(consts_in, 16)
                sp.dma_start(x_raw[:, 1], x_t[1]).then_inc(x_in[1], 16)
                sp.dma_start(w_raw[:, 1], w_qkv[1]).then_inc(w_in[1], 16)
                for q in range(2, NT // QUARTER):
                    sp.wait_ge(x_split, X_DONE[q - 2])
                    sp.dma_start(x_raw[:, q % 2], x_t[q]).then_inc(x_in[q % 2], 16)

                def first_batch(par):
                    if par == 0:
                        for i in range(2):
                            sp.wait_ge(stored[i], 16 * (NQ + NK) * (NT // QUARTER) // 2)
                        sp.wait_ge(x_split, len(PIECES))
                        sp.wait_ge(flipped, QKS)
                        sp.wait_ge(tables_k, 4)
                    else:
                        sp.wait_ge(w_split, DC * NSL)
                    load_keys(sp, par, par)
                    load_queries(sp, par, par)

                def emit(p, kind, before):
                    for par in range(2):
                        s = p * 2 + par
                        if kind != "v":
                            sp.wait_ge(w_split, DC * s + DC)
                            sp.dma_start(w_raw[:, par], w_qkv[bass.ds(s + 2, 1)].rearrange("a p c n -> (a p) c n")
                                         if not isinstance(s, int) else w_qkv[s + 2]).then_inc(w_in[par], 16)
                        for g in range(NT // QUARTER):
                            buf = stage[:, g % 2]
                            if kind == "v":
                                sp.wait_ge(staged_v, NT * s - QKS + QUARTER * (g + 1))
                                n = s - NQ - NK
                                dst = v_dram[g * QUARTER * P:(g + 1) * QUARTER * P, n * SLICE:(n + 1) * SLICE]
                                sp.dma_start(dst.rearrange("(t p) n -> p t n", p=P),
                                             buf.rearrange("p (t n) -> p t n", n=SLICE)).then_inc(stored[g % 2], 16)
                            else:
                                sp.wait_ge(staged_qk, NT * s + QUARTER * (g + 1))
                                to, n = (q_dram, s) if kind == "q" else (k_dram, s - NQ)
                                b0 = g * QUARTER * TB
                                dst = to[b0:b0 + QUARTER * TB, :, bass.ds(n * HS * S, HS * S)]
                                sp.dma_start(dst.rearrange("b d n -> d b n"),
                                             buf.rearrange("p (b n) -> p b n", n=HS * S)).then_inc(stored[g % 2], 16)
                            if kind == "v" and g == 1:
                                first_batch(par)

                over_pairs(sp, emit)
            @block.gpsimd
            def _(pool):
                nc.gpsimd.memset(ident[:, :], 0.0).then_inc(ident_done, 1)
                pool.wait_ge(ident_done, 1)
                nc.gpsimd.affine_select(out=ident[:, :], in_=ident[:, :], compare_op=ALU.not_equal, fill=1.0,
                                        base=0, pattern=[[-1, P]], channel_multiplier=1).then_inc(ident_done, 1)
                pool.wait_ge(ident_done, 2)
                for i in range(TB):
                    nc.gpsimd.iota(in_page_i[PSIZE * i:PSIZE * (i + 1), :], [[0, 1]], base=0, channel_multiplier=1)\
                        .then_inc(iota_done, 1)
                pool.wait_ge(iota_done, TB)
                nc.gpsimd.iota(key_i[:, :], [[1, L]], base=0, channel_multiplier=0).then_inc(iota_done, 1)
                pool.wait_ge(iota_done, TB + 1)
                nc.gpsimd.tensor_copy(key_index[:, :], key_i)
                for c in (1, 3):
                    pool.wait_ge(w_hi_done, c + 1)
                    nc.gpsimd.tensor_sub(w_lo[:, 0, c], w_raw[:, 0, c], w_hi[:, 0, c].bitcast(F32)).then_inc(w_split, 1)

                def split(s, par, c):
                    nc.gpsimd.tensor_copy(w_hi[:, par, c], w_raw[:, par, c]).then_inc(w_hi_done, 1)
                    pool.wait_ge(w_hi_done, DC * s + c + 1)
                    nc.gpsimd.tensor_sub(w_lo[:, par, c], w_raw[:, par, c], w_hi[:, par, c].bitcast(F32))\
                        .then_inc(w_split, 1)

                def table(to, trig, w, done):
                    nc.gpsimd.tensor_mul(to, trig[:, :, :], w.unsqueeze(1).broadcast_to([P, NT, HALF])).then_inc(done, 1)

                def key_table(k):
                    if k == 1:
                        pool.wait_ge(straight_q_done, 2)
                    if k % 2:
                        pool.wait_ge(tables_k, k)
                    to, trig, w = ((straight["k"][:, :, 0:HALF], cos, norm_k[:, 0:HALF]),
                                   (cos, cos, norm_k[:, HALF:HD]),
                                   (crossed["k"][:, :, 0:HALF], sin, minus_norm[:, 1]),
                                   (sin, sin, norm_k[:, 0:HALF]))[k]
                    table(to, trig, w, tables_k)

                pool.wait_ge(minus_done, 2)
                pool.wait_ge(trig_done, 1)
                pool.wait_ge(consts_in, 16 * 3)
                table(crossed["q"][:, :, 0:HALF], sin, minus_norm[:, 0], crossed_q_done)
                table(crossed["q"][:, :, HALF:HD], sin, norm_q[:, 0:HALF], crossed_q_done)
                pool.wait_ge(crossed_q_done, 2)
                pool.wait_ge(trig_done, 2)

                def emit(p, kind, before):
                    if kind == "k":
                        pool.wait_ge(tables_k, 4)
                    for j in range(PS):
                        n = p * PS + j
                        par, t = j // NT, j % NT
                        s = p * 2 + par + 1
                        splits = t in (3, 6, 9, 12) and not (kind == "v" and par == 1)
                        if splits and t == 3:
                            pool.wait_ge(w_in[1 - par], 16 * p + 16 if par == 0 else 16 * p + 32)
                            at_least(pool, mm_done, NT * (s - 1))
                        lag = kind if j >= 2 else before
                        if lag in ("q", "k"):
                            m, i = n - 2, j % 2
                            pool.wait_ge(drained, m + 1)
                            at_least(pool, roped_done, m - 1)
                            cr = crossed[lag]
                            for lo, hi in ((0, HALF), (HALF, 0)):
                                last = nc.gpsimd.tensor_mul(
                                    part_c[:, i, :, lo:lo + HALF], normed[:, i, :, hi:hi + HALF],
                                    cr[:, (j - 2) % NT, lo:lo + HALF].unsqueeze(1).broadcast_to([P, HS, HALF]))
                            last.then_inc(crossed_done, 1)
                        if splits:
                            split(s, 1 - par, t // 3 - 1)
                        if before is None and j in KEY_TABLES:
                            key_table(KEY_TABLES.index(j))

                over_pairs(pool, emit)
                pool.wait_ge(roped_done, QKS)
                for par in range(2):
                    name_values(par, par)
                pool.wait_ge(v_named, 2)
                for par in range(2):
                    gather_values(pool, par)

            @block.scalar
            def _(act):
                def upper(k):
                    cols, q, raw = piece(k)
                    act.wait_ge(x_in[q % 2], 16 * (q // 2 + 1))
                    nc.scalar.activation(x_hi[:, :, cols], x_raw[:, q % 2, :, raw], ACT.Copy).then_inc(x_hi_done, 1)

                act.wait_ge(w_in[0], 16)
                for c in range(DC):
                    nc.scalar.activation(w_hi[:, 0, c], w_raw[:, 0, c], ACT.Copy).then_inc(w_hi_done, 1)
                for k in range(4):
                    upper(k)
                act.wait_ge(angles_done, 1)
                nc.scalar.activation(sin, reduced, ACT.Sin).then_inc(trig_done, 1)
                act.wait_ge(angles_done, 2)
                nc.scalar.activation(cos, angle, ACT.Sin).then_inc(trig_done, 1)
                def emit(p, kind, before):
                    for j in range(PS):
                        n = p * PS + j
                        lag, i = (kind if j >= 1 else before), (j - 1) % 2
                        if lag in ("q", "k"):
                            act.wait_ge(summed, n)
                            nc.scalar.activation(rms[:, i], sumsq[:, i], ACT.Sqrt, bias=eps[:, 0:1], scale=1.0 / HD)\
                                .then_inc(rooted, 1)
                        if kind != "v":
                            act.wait_ge(mm_done, n + 1)
                            nc.scalar.activation(squares[:, j % 2], acc[j % MM_BANKS][:, :].rearrange(
                                "p (h d) -> p h d", d=HD), ACT.Square).then_inc(squared, 1)
                        if lag in ("q", "k"):
                            act.wait_ge(rstd_done, n)
                            at_least(act, roped_done, n - 2)
                            for h in range(HS):
                                last = nc.scalar.activation(normed[:, i, h],
                                                            acc[(j - 1) % MM_BANKS][:, h * HD:(h + 1) * HD],
                                                            ACT.Copy, scale=rstd[:, i, h:h + 1])
                            last.then_inc(drained, 1)
                        if kind == "v":
                            act.wait_ge(mm_done, n + 1)
                            t = j % NT
                            if t % QUARTER == 0:
                                g = t // QUARTER
                                s = p * 2 + j // NT
                                act.wait_ge(stored[g % 2], 16 * (s * 2 + g // 2))
                            nc.scalar.activation(stage[:, (t // QUARTER) % 2, (t % QUARTER) * SLICE:(t % QUARTER + 1) * SLICE],
                                                 acc[j % MM_BANKS][:, :], ACT.Copy).then_inc(staged_v, 1)

                        if before is None and j + 1 in LATE:
                            upper(LATE[j + 1])

                over_pairs(act, emit)

            @block.vector
            def _(dve):
                steps = [0]

                def link(ins):
                    steps[0] += 1
                    ins.then_inc(table_step, 1)
                    dve.wait_ge(table_step, steps[0])

                nc.vector.memset(eps[:, :], RMS_EPS)
                dve.wait_ge(iota_done, TB + 1)
                dve.wait_ge(angles_in, 16 * 2)
                link(nc.vector.tensor_copy(in_page, in_page_i[:, :]))
                link(nc.vector.tensor_copy(seq_f[:, :], seq_i))
                for i in range(TB):
                    q = slice(PSIZE * i, PSIZE * (i + 1))
                    last = nc.vector.tensor_scalar(pos[q, :], seq_f[q, i::TB], in_page[q, 0:1], None, ALU.add)
                link(last)
                link(nc.vector.tensor_tensor(angle, pos.unsqueeze(2).broadcast_to([P, NT, HALF]),
                                             freq.unsqueeze(1).broadcast_to([P, NT, HALF]), ALU.mult))

                for c in (0, 2):
                    dve.wait_ge(w_hi_done, c + 1)
                    nc.vector.tensor_tensor(w_lo[:, 0, c], w_raw[:, 0, c], w_hi[:, 0, c].bitcast(F32), ALU.subtract)\
                        .then_inc(w_split, 1)

                def lower(k):
                    cols, q, raw = piece(k)
                    dve.wait_ge(x_hi_done, k + 1)
                    nc.vector.tensor_tensor(x_lo[:, :, cols], x_raw[:, q % 2, :, raw], x_hi[:, :, cols].bitcast(F32),
                                            ALU.subtract).then_inc(x_split, 1)

                lower(0)
                link(nc.vector.tensor_scalar(turns, angle, 1.0 / TWO_PI, ROUND, ALU.mult, ALU.add))
                link(nc.vector.tensor_scalar(turns, turns, ROUND, None, ALU.subtract))
                link(nc.vector.scalar_tensor_tensor(out=reduced, in0=turns, scalar=-TWO_PI_HI, in1=angle,
                                                    op0=ALU.mult, op1=ALU.add))
                link(nc.vector.scalar_tensor_tensor(out=reduced, in0=turns, scalar=-TWO_PI_LO, in1=reduced,
                                                    op0=ALU.mult, op1=ALU.add))
                lower(1)
                nc.vector.tensor_scalar(reduced, reduced, PI_IN, -PI_IN, ALU.min, ALU.max).then_inc(angles_done, 1)
                lower(2)
                dve.wait_ge(angles_done, 1)
                link(nc.vector.tensor_scalar(turns, reduced, TWO_PI / 4, -TWO_PI, ALU.is_gt, ALU.mult))
                link(nc.vector.scalar_tensor_tensor(out=angle, in0=reduced, scalar=TWO_PI / 4, in1=turns,
                                                    op0=ALU.add, op1=ALU.add))
                nc.vector.tensor_scalar(angle, angle, PI_IN, -PI_IN, ALU.min, ALU.max).then_inc(angles_done, 1)
                dve.wait_ge(consts_in, 16 * 3)
                for i, norm in enumerate((norm_q, norm_k)):
                    nc.vector.tensor_scalar(minus_norm[:, i], norm[:, HALF:HD], -1.0, None, ALU.mult).then_inc(minus_done, 1)
                lower(3)

                def page_rows():
                    for i in range(TB):
                        q = slice(PSIZE * i, PSIZE * (i + 1))
                        nc.vector.tensor_scalar(page_row[q, :].rearrange("p (b c) -> p b c", c=KC),
                                                pages[q, :].rearrange("p (b c i) -> p b c i", c=KC, i=TB)[:, :, :, i],
                                                float(PSIZE), None, ALU.mult)

                def query_tables():
                    dve.wait_ge(trig_done, 2)
                    for half in (slice(0, HALF), slice(HALF, HD)):
                        nc.vector.tensor_tensor(straight["q"][:, :, half], cos, norm_q[:, half].unsqueeze(1).broadcast_to([P, NT, HALF]),
                                                ALU.mult).then_inc(straight_q_done, 1)
                    dve.wait_ge(straight_q_done, 2)

                def emit(p, kind, before):
                    if kind == "k":
                        dve.wait_ge(tables_k, 4)
                    for j in range(PS):
                        n = p * PS + j
                        if (kind if j >= 1 else before) in ("q", "k"):
                            i = (j - 1) % 2
                            dve.wait_ge(rooted, n)
                            nc.vector.reciprocal(rstd[:, i], rms[:, i]).then_inc(rstd_done, 1)
                        lag = kind if j >= 4 else before
                        if lag in ("q", "k"):
                            m, t = n - 4, (j - 4) % NT
                            dve.wait_ge(flipped, m + 1)
                            g, s2 = t // QUARTER, (p * 2 + (j - 4) // NT) * 2
                            if t % QUARTER == 0:
                                at_least(dve, stored[g % 2], 16 * (s2 + g // 2))
                            to = stage[:, g % 2, (t % QUARTER) * SLICE:(t % QUARTER + 1) * SLICE]
                            nc.vector.tensor_copy(to.rearrange("p (b h s) -> p b h s", h=HS, s=S),
                                                  flip[j % 2][:, :].rearrange("p (h b s) -> p b h s", h=HS, s=S))\
                                .then_inc(staged_qk, 1)
                        if kind != "v":
                            dve.wait_ge(squared, n + 1)
                            nc.vector.tensor_reduce(sumsq[:, j % 2], squares[:, j % 2], AX.X, ALU.add).then_inc(summed, 1)
                        if before is None and j == 0:
                            query_tables()
                        if before is None and j == NT - 1:
                            page_rows()
                        lag = kind if j >= 2 else before
                        if lag in ("q", "k"):
                            m, i, t = n - 2, j % 2, (j - 2) % NT
                            at_least(dve, roped_done, m)
                            dve.wait_ge(drained, m + 1)
                            nc.vector.tensor_tensor(part_s[:, :, :], normed[:, i],
                                                    straight[lag][:, t].unsqueeze(1).broadcast_to([P, HS, HD]),
                                                    ALU.mult).then_inc(straight_done, 1)
                            dve.wait_ge(straight_done, m + 1)
                            dve.wait_ge(crossed_done, m + 1)
                            at_least(dve, flipped, m - 1)
                            nc.vector.tensor_tensor(roped[:, i], part_s[:, :, :], part_c[:, i], ALU.add)\
                                .then_inc(roped_done, 1)
                        if before is None and j in LATE:
                            lower(LATE[j])

                over_pairs(dve, emit)

            @block.tensor
            def _(pe):
                pe.wait_ge(ident_done, 2)

                def emit(p, kind, before):
                    for j in range(PS):
                        n = p * PS + j
                        par, t = j // NT, j % NT
                        if t == 0:
                            pe.wait_ge(w_split, DC * (p * 2 + par) + DC)
                        if isinstance(p, int) and p == 0 and par == 0 and t in dict(PIECES):
                            k = [lo for lo, _ in PIECES].index(t)
                            pe.wait_ge(x_split, k + 1)
                        if kind == "v":
                            if j < MM_BANKS:
                                pe.wait_ge(drained, n - MM_BANKS + 1)
                            else:
                                pe.wait_ge(staged_v, j - MM_BANKS + 1)
                        else:
                            at_least(pe, drained, n - MM_BANKS + 1)
                        bank = acc[j % MM_BANKS][:, :]
                        for c in range(DC):
                            toks = slice(t * P, (t + 1) * P)
                            pe.matmul(bank, x_hi[:, c, toks], w_hi[:, par, c], start=c == 0, stop=False)
                            pe.matmul(bank, x_hi[:, c, toks], w_lo[:, par, c], start=False, stop=False)
                            last = pe.matmul(bank, x_lo[:, c, toks], w_hi[:, par, c], start=False, stop=c == DC - 1)
                        last.then_inc(mm_done, 1)
                        lag = kind if j >= 3 else before
                        if lag in ("q", "k"):
                            m, i = n - 3, (j - 3) % 2
                            pe.wait_ge(roped_done, m + 1)
                            at_least(pe, staged_qk, m - 1)
                            for h in range(HS):
                                last = pe.transpose(flip[i][:, h * P:(h + 1) * P], roped[:, i, h], ident[:, :])
                            last.then_inc(flipped, 1)

                over_pairs(pe, emit)


def attend(nc, sem, ident, seq_f, pages, page_row, in_page_i, key_index, q_t, k_t, v_c, qk_in, v_in, v_named, wo_early,
           wo_in, stored, o_stored, loads, load_first, load_weights, wo_t, v_dram, o_dram):
    UNITS = 2 * HK
    PAIRS = B // 2
    CUT = 9 * PSIZE
    BANK = 512

    with ExitStack() as ctx:
        def sb(name, shape, dt=F32):
            return ctx.enter_context(nc.sbuf_tensor(name, shape, dt))

        def ps(name, shape):
            return ctx.enter_context(nc.psum_tensor(name, shape, F32))

        q_hi = sb("q_hi", [P, HK, ROWS], F32R)
        q_lo = sb("q_lo", [P, HK, ROWS], F32R)
        k_hi = sb("k_hi", [P, HK, KEYS], F32R)
        k_lo = sb("k_lo", [P, HK, KEYS], F32R)
        v_own = sb("v_own", [2 * S, 2, HK // 2 * HD])
        mask = sb("mask", [P, 2, S + KEYS])
        probs = sb("probs", [P, 2, 2 * KEYS])
        neg_max = sb("neg_max", [P, 2])
        row_sum = sb("row_sum", [P, 2])
        inv_sum = sb("inv_sum", [P, 2])
        p_t = sb("p_t", [P, 2, KC, ROWS])
        p_t_own = sb("p_t_own", [2 * S, 2, ROWS])
        o_t = nc.alloc_sbuf_tensor_at("o_t", [P, 2, HK, ROWS], F32, offset=o_start(nc))
        s_bank = ps("s_bank", [P, 2 * BANK])
        s_run = s_bank[:, BANK - CUT:BANK - CUT + KEYS]
        pt_a = [ps(f"pt_a{i}", [P, BANK]) for i in range(2)]
        pt_b = [ps(f"pt_b{i}", [P, BANK]) for i in range(2)]
        o_banks = [ps(f"o_bank{i}", [P, BANK]) for i in range(2)]

        def run(j):
            return probs[:, j // 2 % 2, j % 2 * KEYS:(j % 2 + 1) * KEYS]

        def of_head(g):
            return slice(1, SLOTS) if g % 2 == 0 else slice(0, SLOTS - 1)

        assert nc.sbuf_base <= o_start(nc)
        load_keys, load_queries, name_values, gather_values = loads
        v_own_in = [sem("v_own_in0"), sem("v_own_in1")]
        q_hi_done, q_split = sem("q_hi_done"), sem("q_split")
        k_hi_done, k_split = sem("k_hi_done"), sem("k_split")
        own_unmasked = sem("own_unmasked")
        scored = sem("scored")
        masked_in = sem("mask_built")
        masked = sem("masked")
        weighed = sem("weighed")
        inverted = sem("inverted")
        normed = sem("weights_normed")
        turned = sem("weights_turned")
        pt_a_out = sem("pt_a_out")
        pt_b_out = sem("pt_b_out")
        summed = sem("values_summed")
        o_out = sem("o_out")
        QK_DMAS = 3 + NPP
        PT_B = 3 * UNITS // 2
        QH = 2
        QP = HK // QH
        WO_WITH = [range(0, 0), range(0, 2 * HS, HS), range(2 * HS, 4 * HS, HS), range(4 * HS, WO_EARLY, HS)]
        FIRST = 3
        GATHER_AT = 2

        def over_pairs(engine, emit, tail):
            emit(0, True, False)
            with engine.Fori(1, PAIRS - 1) as p:
                emit(p, False, False)
            emit(PAIRS - 1, False, True)
            tail(PAIRS)

        with nc.Block() as block:

            @block.sync
            def _(sp):
                def load_v_own(b, par):
                    at_least(sp, summed, (b - 1) * HK)
                    src = v_dram[bass.ds(b * S, S), :].rearrange("s (g e d) -> s e g d", e=2, d=HD)
                    for e in range(2):
                        sp.dma_start(v_own[e * S:(e + 1) * S, par].rearrange("s (g d) -> s g d", d=HD), src[:, e])\
                            .then_inc(v_own_in[par], 16)

                def store(b, par):
                    sp.wait_ge(o_out, b * HK + HK)
                    sp.dma_start(o_dram[bass.ds(b, 1)].rearrange("b d n -> (b d) n"),
                                 o_t[:, par].rearrange("p g n -> p (g n)")).then_inc(o_stored[par], 16)

                def emit(p):
                    for par in range(2):
                        b = p * 2 + par
                        early = isinstance(b, int)
                        if not (early and b < 2):
                            sp.wait_ge(k_split, (b - 1) * HK)
                            load_keys(sp, b, par)
                            sp.wait_ge(q_split, (b - 1) * QP)
                            load_queries(sp, b, par)
                        if not (early and b < 1):
                            load_v_own(b - 1, 1 - par)
                        if early:
                            for h in WO_WITH[b]:
                                sp.dma_start(wo_early[:, h:h + HS], wo_t[:, h:h + HS, :]).then_inc(wo_in, 16)
                        if not (early and b < 3):
                            store(b - 3, 1 - par)

                for i in range(2):
                    sp.wait_ge(stored[i], 16 * NSL * (NT // QUARTER) // 2)
                emit(0)
                emit(1)
                with sp.Fori(2, PAIRS) as p:
                    emit(p)
                load_v_own(B - 1, 1)
                store(B - 3, 1)
                sp.wait_ge(q_split, B * QP)
                sp.wait_ge(k_split, B * HK)
                for par in range(2):
                    sp.wait_ge(o_stored[par], 16 * TB // 2)
                load_first(sp)
                store(B - 2, 0)
                sp.wait_ge(summed, (B - 1) * HK)
                load_weights(sp)
                store(B - 1, 1)
            @block.gpsimd
            def _(pool):
                def emit(p):
                    for j in range(UNITS):
                        par, g = j // HK, j % HK
                        b = p * 2 + par
                        early = isinstance(b, int)
                        if g == GATHER_AT and not (early and b < 2):
                            pool.wait_ge(summed, (b - 1) * HK)
                            name_values(b, par)
                        if g == GATHER_AT and not (early and b < 2):
                            pool.wait_ge(v_named, b + 1)
                        pool.wait_ge(k_hi_done, p * UNITS + j + 1)
                        nc.gpsimd.tensor_sub(k_lo[:, g].rearrange("p (s t) -> p s t", t=PSIZE), k_t[:, par, of_head(g), g],
                                             k_hi[:, g].bitcast(F32).rearrange("p (s t) -> p s t", t=PSIZE))\
                            .then_inc(k_split, 1)
                        if g == GATHER_AT and not (early and b < 2):
                            gather_values(pool, par)

                emit(0)
                with pool.Fori(1, PAIRS) as p:
                    emit(p)

            @block.scalar
            def _(act):
                def pt_evacuate(n, i, pair):
                    act.wait_ge(turned, n + 1)
                    at_least(act, summed, n - 1)
                    nc.scalar.activation(p_t[:, i, 2:4].rearrange("p c n -> p (c n)"), pt_b[i][:, 0:2 * ROWS], ACT.Copy)\
                        .then_inc(pt_b_out, 1)
                    if i:
                        nc.scalar.activation(p_t_own[:, pair], pt_b[i][0:2 * S, 2 * ROWS:3 * ROWS], ACT.Copy).then_inc(pt_b_out, 1)

                def o_evacuate(n, p, j):
                    par, g = (j // HK) % 2, j % HK
                    act.wait_ge(summed, n + 1)
                    if g == 0:
                        at_least(act, o_stored[par], p * 16)
                    nc.scalar.activation(o_t[:, par, g], o_banks[j % 2][:, 0:ROWS], ACT.Copy).then_inc(o_out, 1)

                def split_keys(b, k, par, g):
                    if g == 0:
                        act.wait_ge(qk_in[par], 16 * QK_DMAS * (k + 1))
                    nc.scalar.activation(k_hi[:, g].rearrange("p (s t) -> p s t", t=PSIZE), k_t[:, par, of_head(g), g], ACT.Copy)\
                        .then_inc(k_hi_done, 1)

                def split_queries(par, h):
                    heads = slice(h * QH, h * QH + QH)
                    nc.scalar.activation(q_hi[:, heads], q_t[:, par, heads], ACT.Copy).then_inc(q_hi_done, 1)

                def emit(p, first, last):
                    if first:
                        for g in range(FIRST):
                            split_keys(0, 0, 0, g)
                            if g == 0:
                                for h in range(QP):
                                    split_queries(0, h)
                    for j in range(UNITS):
                        n = p * UNITS + j
                        if not (first and j < 2):
                            pt_evacuate(n - 2, j % 2, (j - 2) // 2 % 2)
                        if not (first and j < 4):
                            o_evacuate(n - 4, p if j >= 4 else p - 1, (j - 4) % UNITS)
                        par, g = (j - 1) // HK % 2, (j - 1) % HK
                        if not (first and j == 0) and not (last and j > HK):
                            split_keys(p * 2 + (j - 1) // HK + 1, p + (j - 1) // HK, 1 - par, g)
                            if g % QH == QH - 1:
                                split_queries(1 - par, g // QH)
                        act.wait_ge(masked, n + 1)
                        nc.scalar.activation(run(j), run(j), ACT.Exp, scale=-1.0,
                                             bias=neg_max[:, j % 2:j % 2 + 1],
                                             accum_out=row_sum[:, j % 2:j % 2 + 1]).then_inc(weighed, 1)
                        if first and j == 0:
                            for g in range(FIRST, HK):
                                split_keys(0, 0, 0, g)

                def tail(p):
                    n = p * UNITS
                    for j in range(4):
                        if j < 2:
                            pt_evacuate(n + j - 2, j % 2, 1)
                        o_evacuate(n + j - 4, p - 1, (j - 4) % UNITS)

                over_pairs(act, emit, tail)

            @block.vector
            def _(dve):
                def pt_evacuate(n, i):
                    dve.wait_ge(turned, n + 1)
                    at_least(dve, summed, n - 1)
                    nc.vector.tensor_copy(p_t[:, i, 0:2].rearrange("p c n -> p (c n)"), pt_a[i][:, 0:2 * ROWS])\
                        .then_inc(pt_a_out, 1)

                def invert(n, i):
                    dve.wait_ge(weighed, n + 1)
                    nc.vector.reciprocal(inv_sum[:, i:i + 1], row_sum[:, i:i + 1]).then_inc(inverted, 1)

                def normalise(j):
                    nc.vector.tensor_scalar(run(j), run(j), inv_sum[:, j % 2:j % 2 + 1], None, ALU.mult)\
                        .then_inc(normed, 1)

                def split_queries(b, par, h):
                    heads = slice(h * QH, h * QH + QH)
                    dve.wait_ge(q_hi_done, b * QP + h + 1)
                    nc.vector.tensor_tensor(q_lo[:, heads], q_t[:, par, heads], q_hi[:, heads].bitcast(F32), ALU.subtract)\
                        .then_inc(q_split, 1)

                def emit(p, first, last):
                    if first:
                        for own in (slice(0, S), slice(S + L, S + KEYS)):
                            nc.vector.memset(mask[:, :, own], 0.0).then_inc(own_unmasked, 1)
                        dve.wait_ge(own_unmasked, 2)
                        for h in range(QP):
                            split_queries(0, 0, h)
                    for j in range(UNITS):
                        n = p * UNITS + j
                        par, g, i = j // HK, j % HK, j % 2
                        if not (first and j < 2):
                            pt_evacuate(n - 2, i)
                        if g == 0:
                            b = p * 2 + par
                            nc.vector.tensor_scalar(mask[:, par, S:S + L], key_index[:, :], seq_f[:, bass.ds(b, 1)], NEG,
                                                    ALU.is_ge, ALU.mult).then_inc(masked_in, 1)
                            dve.wait_ge(masked_in, b + 1)
                        if not (first and j < 1):
                            invert(n - 1, 1 - i)
                            dve.wait_ge(inverted, n)
                            dve.wait_ge(scored, n + 1)
                            normalise((j - 1) % UNITS)
                        else:
                            dve.wait_ge(scored, n + 1)
                        unmasked = S if g % 2 == 0 else 0
                        nc.vector.tensor_tensor_reduce(out=run(j), in0=s_run, in1=mask[:, par, unmasked:unmasked + KEYS],
                                                       scale=-SCALE, scalar=3.0e38, op0=ALU.add, op1=ALU.min,
                                                       accum_out=neg_max[:, i:i + 1]).then_inc(masked, 1)
                        if j % QH == 1 and not (first and j == 1) and not (last and j > HK + 1):
                            k, h = (j - QH) // HK + 1, (j - QH) % HK // QH
                            split_queries(p * 2 + k, k % 2, h)

                def tail(p):
                    n = p * UNITS
                    pt_evacuate(n - 2, 0)
                    invert(n - 1, 1)
                    dve.wait_ge(inverted, n)
                    normalise(UNITS - 1)
                    pt_evacuate(n - 1, 1)

                over_pairs(dve, emit, tail)

            @block.tensor
            def _(pe):
                def score(n, p, j):
                    par, g, i = j // HK, j % HK, j % 2
                    if g % QH == 0:
                        pe.wait_ge(q_split, (p * 2 + par) * QP + g // QH + 1)
                    pe.wait_ge(k_split, n + 1)
                    at_least(pe, masked, n)
                    for bank, keys in ((slice(BANK - CUT, BANK), slice(0, CUT)),
                                       (slice(BANK, BANK - CUT + KEYS), slice(CUT, KEYS))):
                        for k, (q, kk) in enumerate(((q_hi, k_hi), (q_hi, k_lo), (q_lo, k_hi))):
                            last = pe.matmul(s_bank[:, bank], q[:, g], kk[:, g, keys], start=k == 0, stop=k == 2)
                    last.then_inc(scored, 1)

                def weigh_values(n, p, j, before):
                    par, g, i = (j // HK) % 2, j % HK, j % 2
                    if g == 0:
                        pe.wait_ge(v_in[par], 16 * KC * (p + 1))
                        pe.wait_ge(v_own_in[par], 32 * (p + 1))
                    at_least(pe, o_out, n - 1)
                    pe.wait_ge(pt_a_out, n + 1)
                    pairs = before + 3 * (j // 2)
                    o_bank = o_banks[i][:, 0:ROWS]
                    for c in range(KC):
                        if c == 2:
                            pe.wait_ge(pt_b_out, pairs + 1 + j % 2)
                        pe.matmul(o_bank, v_c[:, par, c, g * HD:(g + 1) * HD], p_t[:, i, c], start=c == 0, stop=False)
                    pe.wait_ge(pt_b_out, pairs + 3)
                    own = slice(j % 2 * S, (j % 2 + 1) * S)
                    pe.matmul(o_bank, v_own[own, par, g // 2 * HD:(g // 2 + 1) * HD], p_t_own[own, j // 2 % 2],
                              start=False, stop=True).then_inc(summed, 1)

                def turn(n, j, before):
                    i, pair = j % 2, j // 2 % 2
                    at_least(pe, pt_a_out, n - 1)
                    at_least(pe, pt_b_out, before + 3 * (j // 2 - 1) + 1 + 2 * i)
                    pe.wait_ge(normed, n + 1)
                    for c in range(KC):
                        start = i * (KEYS + S) + c * P
                        last = pe.transpose((pt_a, pt_b)[c // 2][i][:, (c % 2) * ROWS:(c % 2 + 1) * ROWS],
                                            probs[:, pair, start:start + P], ident[:, :])
                    if i:
                        last = pe.transpose(pt_b[i][0:2 * S, 2 * ROWS:3 * ROWS], probs[:, pair, L:L + 2 * S], ident[:, :])
                    last.then_inc(turned, 1)

                def emit(p, first, last):
                    for j in range(UNITS):
                        n = p * UNITS + j
                        score(n, p, j)
                        if not (first and j < 3):
                            weigh_values(n - 3, p if j >= 3 else p - 1, (j - 3) % UNITS,
                                         p * PT_B if j >= 3 else (p - 1) * PT_B)
                        if not (first and j < 1):
                            turn(n - 1, (j - 1) % UNITS, p * PT_B if j >= 1 else (p - 1) * PT_B)

                def tail(p):
                    n, before = p * UNITS, (p - 1) * PT_B
                    weigh_values(n - 3, p - 1, UNITS - 3, before)
                    turn(n - 1, UNITS - 1, before)
                    weigh_values(n - 2, p - 1, UNITS - 2, before)
                    weigh_values(n - 1, p - 1, UNITS - 1, before)

                over_pairs(pe, emit, tail)


def finish(nc, sem, ident, wo_early, wo_start, wo_in, o_stored, buffers, early_start, early_bytes, raw_in, x_rows_in,
           w_small_in, load_chunk, load_x, lang, slot2, slot3, a2_rows, b2_rows, b3_rows, a3_rows, out):
    GATE_STEPS = 10
    assert R2 == R3

    with ExitStack() as ctx:
        def sb(name, shape, dt=F32):
            return ctx.enter_context(nc.sbuf_tensor(name, shape, dt))

        def ps(name, shape):
            return ctx.enter_context(nc.psum_tensor(name, shape, F32))

        raw, wo_late, lo_late, w1, w1_lo, w2, w2_lo, wr_a, b1, bias, x1, up, down2, low_t = buffers
        assert nc.sbuf_base == early_start
        sb("early_buffers", [P, early_bytes // 4])
        wo_hi = sb("wo_hi", [P, HQ, D], F32R)
        lo_early = nc.alloc_sbuf_tensor_at("lo_early", [P, WO_EARLY, D], F32R, offset=wo_start)
        o_hi = sb("o_hi", [P, 2, CH, P], F32R)
        o_lo = sb("o_lo", [P, 2, CH, P], F32R)
        w1_hi = sb("w1_hi", [P, DC, D], F32R)
        w2_hi = sb("w2_hi", [P, DC, D], F32R)
        ends = [o_start(nc) + i * D * 4 for i in range(4)]
        x = nc.alloc_sbuf_tensor_at("x", [P, D], F32, offset=ends[0])
        x_t = nc.alloc_sbuf_tensor_at("x_t", [P, DC, P], F32, offset=ends[1])
        xt_hi = nc.alloc_sbuf_tensor_at("xt_hi", [P, DC, P], F32R, offset=ends[2])
        xt_lo = nc.alloc_sbuf_tensor_at("xt_lo", [P, DC, P], F32R, offset=ends[3])
        low = sb("low", [P, ER])
        down3 = sb("down3", [P, TB, DC, R3])
        own2 = sb("own2", [P, TB, R2])
        own3 = sb("own3", [P, TB, R3])
        lang_i = sb("lang_i", [P, NT], I32)
        lang_f = sb("lang_f", [P, NT])
        expert_i = sb("expert_i", [P, E], I32)
        expert = sb("expert", [P, E])
        slots = sb("slots", [1, NT, 2, TB], I32)
        logits = sb("logits", [P, E])
        lang_bias = sb("lang_bias", [P, E])
        highest = sb("highest", [P, 1])
        top = sb("top", [P, E])
        top_i = sb("top_i", [P, E], U32)
        top_f = sb("top_f", [P, E])
        gap = sb("gap", [P, 1])
        ratio = sb("ratio", [P, 1])
        denom = sb("denom", [P, 1])
        gate = sb("gate", [P, 2])
        gates1 = sb("gates1", [P, E])
        gates = sb("gates", [P, E])

        assert nc.sbuf_base <= o_start(nc)
        proj = ps("proj", [P, D])
        turn = ps("turn", [P, D])
        wide = ps("wide", [P, D])
        slim = ps("slim", [P, D])

        slots_in, lang_in = sem("slots_in"), sem("lang_in")
        own_set, expert_set, lang_set = sem("own_set"), sem("expert_set"), sem("lang_set")
        wo_hi_done, wo_split, wo_split_pool = sem("wo_hi_done"), sem("wo_split"), sem("wo_split_pool")
        o_hi_done, o_split = sem("o_hi_done"), sem("o_split")
        chunk_done = sem("chunk_done")
        x1_done, x2_done, x2b_done, x3_done, x4_done = (sem(f"x{i}_done") for i in ("1", "2", "2b", "3", "4"))
        x_turned, xt_out = sem("x_turned"), sem("xt_out")
        slim_done, low_done, low_turned, low_out = sem("slim_done"), sem("low_done"), sem("low_turned"), sem("low_out")
        wide_done = sem("wide_done")
        w12_hi_done, w12_lo_done = sem("w12_hi_done"), sem("w12_lo_done")
        xt_hi_done, xt_lo_done = sem("xt_hi_done"), sem("xt_lo_done")
        gate_step, gap_done, ratio_done, gates_done = sem("gate_step"), sem("gap_done"), sem("ratio_done"), sem("gates_done")
        down_in, up_in = [sem("down2_in"), sem("down3_in")], [sem("up2_in"), sem("up3_in")]
        out_stored = sem("out_stored")
        LAYERS = 3
        WO_PIECE = 2
        WO_PIECES = HQ // WO_PIECE
        POOL_EVERY = 4

        def of_heads(early, late, h0, h1):
            return early[:, h0:h1] if h1 <= WO_EARLY else late[:, h0 - WO_EARLY:h1 - WO_EARLY]

        def low_columns(layer):
            return (slice(0, ER), slice(0, LOWS), slice(LOWS, 2 * LOWS))[layer]

        def wo_raw(k):
            return of_heads(wo_early, wo_late, k * WO_PIECE, (k + 1) * WO_PIECE)

        def wo_lower(k):
            h0, h1 = k * WO_PIECE, (k + 1) * WO_PIECE
            return of_heads(lo_early, lo_late, h0, h1), wo_raw(k), wo_hi[:, h0:h1].bitcast(F32)

        with nc.Block() as block:

            @block.sync
            def _(sp):
                def follow_chunk(t, c):
                    at_least(sp, o_split, t * NCH + c - 1)
                    load_chunk(sp, t, c)

                def gather(t, i, wait):
                    rows_d, rows_u = (a2_rows, b3_rows)[i], (b2_rows, a3_rows)[i]
                    down, first = (down2, down3)[i], i * LOWS
                    _, slot = nc.values_load_multi_w_load_instructions(
                        slots[0:1, bass.ds(t, 1), i].rearrange("o t a -> o (t a)"), engines=[mybir.EngineType.SP],
                        min_val=0, max_val=rows_d.shape[0] - 1, skip_runtime_bounds_check_because="slots name adapters")
                    if wait:
                        sp.wait_ge(wide_done, (t - 1) * LAYERS + 2 + i)
                    for a in range(TB):
                        sp.dma_start(down[:, a].rearrange("p c r -> p (c r)"),
                                     rows_d[bass.ds(slot[a], 1)].rearrange("s p n -> (s p) n")).then_inc(down_in[i], 16)
                        sp.dma_start(up[first + R2 * a:first + R2 * (a + 1), :],
                                     rows_u[bass.ds(slot[a], 1)].rearrange("s r n -> (s r) n")).then_inc(up_in[i], 16)

                def store(t):
                    sp.wait_ge(x4_done, t + 1)
                    sp.dma_start(out[bass.ds(t * P, P), :], x[:, :]).then_inc(out_stored, 16)

                for i, ids in enumerate((slot2, slot3)):
                    sp.dma_start(slots[0:1, :, i], ids.rearrange("(o t a) -> o t a", o=1, a=TB)).then_inc(slots_in, 16)
                for a in range(TB):
                    sp.dma_start(lang_i[S * a:S * (a + 1), :], lang[a::TB].partition_broadcast(S),
                                 allow_slow_non_contiguous=True).then_inc(lang_in, 16)
                follow_chunk(0, 2)
                sp.wait_ge(slots_in, 16 * 2)
                gather(0, 0, False)
                gather(0, 1, False)
                follow_chunk(0, 3)
                for par in range(2):
                    sp.wait_ge(o_stored[par], 16 * (B // 2))
                for c in range(NCH - 1):
                    follow_chunk(1, c)

                def follow(t, ahead):
                    follow_chunk(t + 1, NCH - 1)
                    if ahead:
                        follow_chunk(t + 2, 0)
                    sp.wait_ge(x2_done, t + 1)
                    load_x(sp, t + 1)
                    if ahead:
                        follow_chunk(t + 2, 1)
                    gather(t + 1, 0, True)
                    if ahead:
                        follow_chunk(t + 2, 2)
                    store(t)
                    gather(t + 1, 1, True)

                with sp.Fori(0, NT - 2) as t:
                    follow(t, True)
                follow(NT - 2, False)
                store(NT - 1)
                sp.wait_ge(out_stored, 16 * NT)

            @block.gpsimd
            def _(pool):
                nc.gpsimd.iota(expert_i[:, :], [[1, E]], base=0, channel_multiplier=0).then_inc(expert_set, 1)
                for own in (own2, own3):
                    nc.gpsimd.memset(own[:, :, :], 0.0).then_inc(own_set, 1)
                pool.wait_ge(own_set, 2)
                for own, scale in ((own2, LORA_SCALING), (own3, 1.0)):
                    for a in range(TB):
                        nc.gpsimd.memset(own[S * a:S * (a + 1), a, :], scale).then_inc(own_set, 1)

                pool.wait_ge(own_set, 2 + 2 * TB)
                for k in range(POOL_EVERY - 1, WO_PIECES, POOL_EVERY):
                    pool.wait_ge(wo_hi_done, k + 1)
                    low_half, whole_piece, high_half = wo_lower(k)
                    nc.gpsimd.tensor_sub(low_half, whole_piece, high_half).then_inc(wo_split_pool, 1)

                def add_bias(t):
                    pool.wait_ge(x_turned, t * LAYERS + 2)
                    nc.gpsimd.tensor_add(x[:, :], x[:, :], bias[:, :]).then_inc(x2b_done, 1)

                for i, (low_half, weights, high_half) in enumerate(((w1_lo, w1, w1_hi), (w2_lo, w2, w2_hi))):
                    pool.wait_ge(w12_hi_done, i + 1)
                    nc.gpsimd.tensor_sub(low_half[:, :, :], weights[:, :, :], high_half[:, :, :].bitcast(F32)).then_inc(w12_lo_done, 1)
                pool.wait_ge(w_small_in, 16 * 5)
                with pool.Fori(0, NT) as t:
                    add_bias(t)

            @block.scalar
            def _(act):
                def upper(t, c):
                    k = t * NCH + c
                    act.wait_ge(raw_in[c], 16 * t + 16)
                    at_least(act, chunk_done, k - 1)
                    nc.scalar.activation(o_hi[:, c % 2].rearrange("p h (b s) -> p b h s", s=S),
                                         raw[:, c % 2].rearrange("p (b h s) -> p b h s", b=TB, s=S), ACT.Copy)\
                        .then_inc(o_hi_done, 1)

                def x_turn_out(t, layer):
                    act.wait_ge(x_turned, t * LAYERS + layer + 1)
                    nc.scalar.activation(x_t[:, :, :].rearrange("p c n -> p (c n)"), turn[:, :], ACT.Copy).then_inc(xt_out, 1)
                    if layer < 2:
                        nc.scalar.activation(xt_hi[:, :, :].rearrange("p c n -> p (c n)"), turn[:, :], ACT.Copy).then_inc(xt_hi_done, 1)

                def low_turn_out(t, layer):
                    rows = low_columns(layer)
                    act.wait_ge(low_turned, t * LAYERS + layer + 1)
                    nc.scalar.activation(low_t[rows, :], turn[rows, 0:P], ACT.Copy).then_inc(low_out, 1)

                def chain(t, ahead, beyond):
                    if ahead:
                        upper(t + 1, 1)
                    x_turn_out(t, 0)
                    act.wait_ge(gap_done, t + 1)
                    nc.scalar.activation(ratio[:, :], gap[:, :], ACT.Exp).then_inc(ratio_done, 1)
                    low_turn_out(t, 0)
                    if ahead:
                        upper(t + 1, 2)
                    x_turn_out(t, 1)
                    low_turn_out(t, 1)
                    if ahead:
                        upper(t + 1, 3)
                    x_turn_out(t, 2)
                    low_turn_out(t, 2)
                    if beyond:
                        upper(t + 2, 0)

                act.wait_ge(wo_in, 16 * (WO_EARLY // HS))
                for k in range(WO_PIECES):
                    if k * WO_PIECE == WO_EARLY:
                        act.wait_ge(wo_in, 16 * (WO_EARLY // HS + 1))
                    nc.scalar.activation(wo_hi[:, k * WO_PIECE:(k + 1) * WO_PIECE], wo_raw(k), ACT.Copy)\
                        .then_inc(wo_hi_done, 1)
                    if k % NCH == 1:
                        upper(0, k // NCH)
                act.wait_ge(w_small_in, 16 * 5)
                for par in range(2):
                    act.wait_ge(o_stored[par], 16 * (B // 2))
                for high_half, weights in ((w1_hi, w1), (w2_hi, w2)):
                    nc.scalar.activation(high_half[:, :, :], weights[:, :, :], ACT.Copy).then_inc(w12_hi_done, 1)
                upper(1, 0)
                with act.Fori(0, NT - 2) as t:
                    chain(t, True, True)
                chain(NT - 2, True, False)
                chain(NT - 1, False, False)

            @block.vector
            def _(dve):
                def lower(t, c):
                    k = t * NCH + c
                    dve.wait_ge(o_hi_done, k + 1)
                    nc.vector.tensor_tensor(o_lo[:, c % 2].rearrange("p h (b s) -> p b h s", s=S),
                                            raw[:, c % 2].rearrange("p (b h s) -> p b h s", b=TB, s=S),
                                            o_hi[:, c % 2].bitcast(F32).rearrange("p h (b s) -> p b h s", s=S),
                                            ALU.subtract).then_inc(o_split, 1)

                def lower_x(t, layer):
                    dve.wait_ge(xt_hi_done, t * 2 + layer + 1)
                    nc.vector.tensor_tensor(xt_lo[:, :, :], x_t[:, :, :], xt_hi[:, :, :].bitcast(F32), ALU.subtract)\
                        .then_inc(xt_lo_done, 1)

                def result(t):
                    dve.wait_ge(wide_done, t * LAYERS + 3)
                    nc.vector.tensor_tensor(x[:, :], wide[:, :], x[:, :], ALU.add).then_inc(x4_done, 1)

                def chain(t, before, ahead, beyond):
                    links = [0]

                    def link(ins):
                        links[0] += 1
                        ins.then_inc(gate_step, 1)
                        dve.wait_ge(gate_step, t * GATE_STEPS + links[0])

                    dve.wait_ge(chunk_done, t * NCH + NCH)
                    dve.wait_ge(x_rows_in, t * 16 + 16)
                    nc.vector.tensor_tensor(x1[:, :], proj[:, :], x1[:, :], ALU.add).then_inc(x1_done, 1)
                    if before:
                        result(t - 1)
                    if ahead:
                        lower(t + 1, 1)
                    link(nc.vector.tensor_scalar(lang_bias[:, :], expert[:, :], lang_f[:, bass.ds(t, 1)], LANG_BIAS,
                                                 ALU.is_equal, ALU.mult))
                    dve.wait_ge(slim_done, t * LAYERS + 1)
                    link(nc.vector.tensor_tensor(logits[:, :], slim[:, 0:E], lang_bias[:, :], ALU.add))
                    nc.vector.tensor_reduce(highest[:, :], logits[:, :], AX.X, ALU.max)
                    link(nc.vector.max(top[:, :], logits[:, :]))
                    nc.vector.tensor_tensor(gap[:, :], top[:, 1:2], highest[:, :], ALU.subtract).then_inc(gap_done, 1)
                    link(nc.vector.max_index(top_i[:, :], top[:, :], logits[:, :]))
                    link(nc.vector.tensor_copy(top_f[:, :], top_i[:, :]))
                    lower_x(t, 0)
                    dve.wait_ge(ratio_done, t + 1)
                    link(nc.vector.tensor_scalar(denom[:, :], ratio[:, :], 1.0, 1.0 / MOE_SCALING, ALU.add, ALU.mult))
                    link(nc.vector.reciprocal(gate[:, 0:1], denom[:, :]))
                    link(nc.vector.tensor_tensor(gate[:, 1:2], gate[:, 0:1], ratio[:, :], ALU.mult))
                    link(nc.vector.tensor_scalar(gates1[:, :], expert[:, :], top_f[:, 0:1], gate[:, 0:1], ALU.is_equal, ALU.mult))
                    link(nc.vector.tensor_scalar(gates[:, :], expert[:, :], top_f[:, 1:2], gate[:, 1:2], ALU.is_equal, ALU.mult))
                    assert links[0] == GATE_STEPS
                    nc.vector.tensor_tensor(gates[:, :], gates[:, :], gates1[:, :], ALU.add).then_inc(gates_done, 1)
                    dve.wait_ge(gates_done, t + 1)
                    nc.vector.tensor_tensor(low[:, :].rearrange("p (e r) -> p e r", r=R1),
                                            slim[:, E:E + ER].rearrange("p (e r) -> p e r", r=R1),
                                            gates[:, :].unsqueeze(2).broadcast_to([P, E, R1]), ALU.mult).then_inc(low_done, 1)
                    if ahead:
                        lower(t + 1, 2)
                    dve.wait_ge(wide_done, t * LAYERS + 1)
                    at_least(dve, out_stored, t * 16)
                    nc.vector.tensor_tensor(x[:, :], wide[:, :], x1[:, :], ALU.add).then_inc(x2_done, 1)
                    lower_x(t, 1)
                    dve.wait_ge(slim_done, t * LAYERS + 2)
                    nc.vector.tensor_tensor(low[:, 0:LOWS], slim[:, 0:LOWS], own2[:, :, :].rearrange("p a r -> p (a r)"),
                                            ALU.mult).then_inc(low_done, 1)
                    if ahead:
                        lower(t + 1, 3)
                    dve.wait_ge(wide_done, t * LAYERS + 2)
                    dve.wait_ge(x2b_done, t + 1)
                    nc.vector.tensor_tensor(x[:, :], wide[:, :], x[:, :], ALU.add).then_inc(x3_done, 1)
                    dve.wait_ge(slim_done, t * LAYERS + 3)
                    nc.vector.tensor_tensor(low[:, low_columns(2)], slim[:, 0:LOWS], own3[:, :, :].rearrange("p a r -> p (a r)"),
                                            ALU.mult).then_inc(low_done, 1)
                    if beyond:
                        lower(t + 2, 0)

                for k in range(WO_PIECES):
                    if k % POOL_EVERY != POOL_EVERY - 1:
                        dve.wait_ge(wo_hi_done, k + 1)
                        low_half, whole_piece, high_half = wo_lower(k)
                        nc.vector.tensor_tensor(low_half, whole_piece, high_half, ALU.subtract).then_inc(wo_split, 1)
                    if k % NCH == 1:
                        lower(0, k // NCH)
                dve.wait_ge(expert_set, 1)
                dve.wait_ge(lang_in, 16 * TB)
                nc.vector.tensor_copy(expert[:, :], expert_i[:, :]).then_inc(lang_set, 1)
                nc.vector.tensor_copy(lang_f[:, :], lang_i[:, :]).then_inc(lang_set, 1)
                dve.wait_ge(lang_set, 2)
                dve.wait_ge(own_set, 2 + 2 * TB)
                for par in range(2):
                    dve.wait_ge(o_stored[par], 16 * (B // 2))
                lower(1, 0)
                chain(0, False, True, True)
                with dve.Fori(1, NT - 2) as t:
                    chain(t, True, True, True)
                chain(NT - 2, True, True, False)
                chain(NT - 1, True, False, False)
                result(NT - 1)

            @block.tensor
            def _(pe):
                def heads(t, h0, h1):
                    for h in range(h0, h1):
                        c, k = h // CH, t * NCH + h // CH
                        if h % CH == 0:
                            pe.wait_ge(o_split, k + 1)
                        if isinstance(t, int) and t == 0 and h % WO_PIECE == 0:
                            k = h // WO_PIECE
                            if k % POOL_EVERY == POOL_EVERY - 1:
                                pe.wait_ge(wo_split_pool, k // POOL_EVERY + 1)
                            else:
                                pe.wait_ge(wo_split, k - k // POOL_EVERY + 1)
                        i = h % CH
                        lower = of_heads(lo_early, lo_late, h, h + 1)[:, 0]
                        pe.matmul(proj[:, :], o_hi[:, c % 2, i], wo_hi[:, h], start=h == 0, stop=False)
                        pe.matmul(proj[:, :], o_hi[:, c % 2, i], lower, start=False, stop=False)
                        last = pe.matmul(proj[:, :], o_lo[:, c % 2, i], wo_hi[:, h], start=False, stop=h == HQ - 1)
                        if i == CH - 1:
                            last.then_inc(chunk_done, 1)

                def chain(t, ahead):
                    at = [0]

                    def fill(n):
                        if ahead:
                            heads(t + 1, at[0], at[0] + n)
                            at[0] += n

                    for layer, (residual, done) in enumerate(((x1, x1_done), (x, x2_done), (x, x3_done))):
                        pe.wait_ge(done, t + 1)
                        for c in range(DC):
                            last = pe.transpose(turn[:, c * P:(c + 1) * P], residual[:, c * P:(c + 1) * P], ident[:, :])
                        last.then_inc(x_turned, 1)
                        fill((3, 2, 2)[layer])
                        pe.wait_ge(xt_out, t * LAYERS + layer + 1)
                        if layer:
                            pe.wait_ge(down_in[layer - 1], (t + 1) * 16 * TB)
                        for c in range(DC):
                            if layer == 0:
                                last = pe.matmul(slim[:, 0:E + ER], x_t[:, c], wr_a[:, c], start=c == 0, stop=c == DC - 1)
                            else:
                                last = pe.matmul(slim[:, 0:LOWS], x_t[:, c], (down2, down3)[layer - 1][:, :, c, :],
                                                 start=c == 0, stop=c == DC - 1)
                        last.then_inc(slim_done, 1)
                        if layer < 2:
                            w_hi, w_lo = ((w1_hi, w1_lo), (w2_hi, w2_lo))[layer]
                            if layer == 0:
                                at_least(pe, x4_done, t)
                            if isinstance(t, int) and t == 0:
                                pe.wait_ge(w12_lo_done, layer + 1)
                            pe.wait_ge(xt_hi_done, t * 2 + layer + 1)
                            for c in range(DC):
                                pe.matmul(wide[:, :], xt_hi[:, c], w_hi[:, c], start=c == 0, stop=False)
                                pe.matmul(wide[:, :], xt_hi[:, c], w_lo[:, c], start=False, stop=False)
                            fill((2, 1)[layer])
                            pe.wait_ge(xt_lo_done, t * 2 + layer + 1)
                            for c in range(DC):
                                pe.matmul(wide[:, :], xt_lo[:, c], w_hi[:, c], start=False, stop=False)
                        fill((2, 2, 4)[layer])
                        rows = low_columns(layer)
                        pe.wait_ge(low_done, t * LAYERS + layer + 1)
                        pe.transpose(turn[:, 0:P], low[:, :], ident[:, :]).then_inc(low_turned, 1)
                        fill((3, 3, 4)[layer])
                        pe.wait_ge(low_out, t * LAYERS + layer + 1)
                        if layer:
                            pe.wait_ge(up_in[layer - 1], (t + 1) * 16 * TB)
                        pe.matmul(wide[:, :], low_t[rows, :], (b1, up, up)[layer][rows, :], start=layer == 2, stop=True)\
                            .then_inc(wide_done, 1)
                        fill((2, 2, 0)[layer])
                    assert not ahead or at[0] == HQ

                heads(0, 0, HQ)
                pe.wait_ge(w_small_in, 16 * 5)
                chain(0, True)
                with pe.Fori(1, NT - 1) as t:
                    chain(t, True)
                chain(NT - 1, False)


def kernel(**inputs):
    import numpy as np
    import concourse.bacc as bacc
    from concourse.bass_utils import run_bass_kernel_spmd as run

    a = {k: np.asarray(v) for k, v in inputs.items()}

    def chunked(w):
        return w.T.reshape(DC, P, -1).transpose(1, 0, 2)

    x = a["x"].reshape(TOK, D)
    w = np.concatenate([a["L0_cond_Wq"], a["L0_cond_Wk"], a["L0_cond_Wv"]])
    exponent = np.arange(0, HD, 2, dtype=np.float32) / np.float32(HD)
    arrays = {
        "x_t": chunked(x).reshape(P, DC, 4, TOK // 4).transpose(2, 0, 1, 3),
        "x_rows": x,
        "w_qkv": chunked(w).reshape(P, DC, NSL, SLICE).transpose(2, 0, 1, 3),
        "wo_t": a["L0_cond_Wo"].T.reshape(HQ, HD, D).transpose(1, 0, 2),
        "q_norm_w": a["L0_cond_q_norm_w"],
        "k_norm_w": a["L0_cond_k_norm_w"],
        "inv_freq": (np.float32(1.0) / np.float32(10000.0) ** exponent).astype(np.float32),
        "k_pages": a["L0_cond_k_cache"].transpose(0, 3, 2, 1).reshape(PAGES, HD, HK * PSIZE),
        "v_rows": a["L0_cond_v_cache"].reshape(PAGES * PSIZE, HK * HD),
        "block_table": a["itok_Bx16_0_63"].reshape(B * NPP),
        "seqlens": a["itok_B_207_1644"],
        "lang": a["itok_B_0_7"],
        "slot2": a["itok_B_0_23"],
        "slot3": a["itok_B_4_50"],
        "w1_t": chunked(a["L1_cond_W"]),
        "wr_a_t": chunked(np.concatenate([a["L1_cond_Wr"], a["L1_cond_A"].reshape(E * R1, D)])),
        "b1_rows": a["L1_cond_B"].transpose(0, 2, 1).reshape(E * R1, D),
        "w2_t": chunked(a["L2_cond_W"]),
        "bias2": a["L2_cond_b"],
        "a2_rows": a["L2_cond_lora_As"].reshape(-1, DC, P, R2).transpose(0, 2, 1, 3).reshape(-1, P, DC * R2),
        "b2_rows": a["L2_cond_lora_Bs"],
        "b3_rows": a["L3_cond_B"].reshape(-1, R3, DC, P).transpose(0, 3, 2, 1).reshape(-1, P, DC * R3),
        "a3_rows": a["L3_cond_A"].transpose(0, 2, 1),
    }
    arrays = {k: np.ascontiguousarray(v) for k, v in arrays.items()}
    nc = bacc.Bacc("TRN2", target_bir_lowering=False, num_devices=1)
    args = [nc.dram_tensor(f"in_{k}", v.shape, mybir.dt.from_np(v.dtype), kind="ExternalInput").ap()
            for k, v in arrays.items()]
    out = nc.dram_tensor("out_x", (TOK, D), F32, kind="ExternalOutput").ap()
    decoder(nc, *args, out)
    r = run(nc, [{f"in_{k}": v for k, v in arrays.items()}], core_ids=[0])
    return r.results[0]["out_x"].reshape(B, S, D)
```
